# Optimizing a Trainium2 kernel written in Bass

```python
import numpy as np
import jax
import jax.numpy as jnp

def _softmax(x, axis=-1):
    return jax.nn.softmax(x, axis=axis)

def _gelu(x):
    return jax.nn.gelu(x, approximate=True)

def _silu(x):
    return jax.nn.silu(x)

def _sigmoid(x):
    return jax.nn.sigmoid(x)

def _layernorm(x, axis=-1, eps=1e-05):
    m = jnp.mean(x, axis=axis, keepdims=True)
    v = jnp.var(x, axis=axis, keepdims=True)
    return (x - m) / jnp.sqrt(v + eps)

def _scatter_add(tgt, idx, src, axis=0):
    return tgt.at[idx].add(src)

def _segment_sum(src, seg, n):
    return jax.ops.segment_sum(src, seg, n)
kernel_name = 'mk_macaron_d2_jaxref_r8_503637'

def setup_inputs(seed: int=0):
    np.random.seed(seed)
    _w = jnp.asarray

    def _L0_attn_setup():
        import jax, jax.numpy as jnp
        import numpy as np
        NUM_HEADS = 16
        D_MODEL = 128
        HEAD_DIM = D_MODEL // NUM_HEADS
        WINDOW = 64
        SCALE = 8.0 / HEAD_DIM
        LN_EPS = 1e-05

        def _layernorm(t, gamma, beta):
            mu = jnp.mean(t, axis=-1, keepdims=True)
            var = jnp.var(t, axis=-1, keepdims=True)
            return (t - mu) * jax.lax.rsqrt(var + LN_EPS) * gamma + beta
        key = jax.random.key(seed)
        ks = jax.random.split(key, 4)
        x = jax.random.normal(ks[0], (4, 1024, D_MODEL), dtype=jnp.float32)
        W_qkv = jax.random.normal(ks[1], (D_MODEL, 3 * D_MODEL), dtype=jnp.float32) * D_MODEL ** (-0.5)
        ln_gamma = jnp.ones((HEAD_DIM,), dtype=jnp.float32)
        ln_beta = jnp.zeros((HEAD_DIM,), dtype=jnp.float32)
        W_proj = jax.random.normal(ks[2], (D_MODEL, D_MODEL), dtype=jnp.float32) * D_MODEL ** (-0.5)
        b_proj = jax.random.normal(ks[3], (D_MODEL,), dtype=jnp.float32) * 0.02
        return {'x': x, 'W_qkv': W_qkv, 'ln_gamma': ln_gamma, 'ln_beta': ln_beta, 'W_proj': W_proj, 'b_proj': b_proj}
    _L0_attn_in = _L0_attn_setup()

    def _L0_ffn_setup():
        import jax, jax.numpy as jnp
        import numpy as np
        D_MODEL = 128
        M = 64
        INNER = 16
        key = jax.random.key(seed)
        ks = jax.random.split(key, 9)

        def init(k, shape, fan_in):
            bound = 1.0 / np.sqrt(fan_in)
            return jax.random.uniform(k, shape, jnp.float32, -bound, bound)
        x = jax.random.normal(ks[0], (16, 512, D_MODEL), dtype=jnp.float32)
        Win = init(ks[1], (D_MODEL, M), D_MODEL)
        bin_ = init(ks[2], (M,), D_MODEL)
        W1 = init(ks[3], (M, INNER), 1)
        b1 = init(ks[4], (M, INNER), 1)
        W2 = init(ks[5], (M, INNER), INNER)
        b2 = init(ks[6], (M,), INNER)
        Wout = init(ks[7], (M, D_MODEL), M)
        bout = init(ks[8], (D_MODEL,), M)
        return {'x': x, 'Win': Win, 'bin_': bin_, 'W1': W1, 'b1': b1, 'W2': W2, 'b2': b2, 'Wout': Wout, 'bout': bout}
    _L0_ffn_in = _L0_ffn_setup()

    def _L1_attn_setup():
        import jax, jax.numpy as jnp
        import numpy as np
        D_MODEL = 128
        N_HEADS = 16
        TOP_FACTOR = 5
        key = jax.random.key(seed)
        ks = jax.random.split(key, 9)
        B, L, D = (2, 512, D_MODEL)
        s = 0.02
        return {'x': jax.random.normal(ks[0], (B, L, D), dtype=jnp.float32), 'Wq': jax.random.normal(ks[1], (D, D), dtype=jnp.float32) * s, 'bq': jnp.zeros((D,), dtype=jnp.float32), 'Wk': jax.random.normal(ks[2], (D, D), dtype=jnp.float32) * s, 'bk': jnp.zeros((D,), dtype=jnp.float32), 'Wv': jax.random.normal(ks[3], (D, D), dtype=jnp.float32) * s, 'bv': jnp.zeros((D,), dtype=jnp.float32), 'Wo': jax.random.normal(ks[4], (D, D), dtype=jnp.float32) * s, 'bo': jnp.zeros((D,), dtype=jnp.float32)}
    _L1_attn_in = _L1_attn_setup()

    def _L1_ffn_setup():
        import jax, jax.numpy as jnp
        import numpy as np
        TOPK = 8
        BN_EPS = 1e-05
        key = jax.random.key(seed)
        ks = jax.random.split(key, 5)
        b, n, d = (2, 128, 128)
        h, nk, kd = (8, 32, 128)
        ne = nk * nk
        scale = 0.02
        return {'inputs': jax.random.normal(ks[0], (b, n, d), jnp.float32), 'gamma': jnp.ones((d,), jnp.float32), 'beta': jnp.zeros((d,), jnp.float32), 'w_q': jax.random.normal(ks[1], (2 * h * kd, d), jnp.float32) * scale, 'keys': jax.random.normal(ks[2], (h, nk, 2, kd), jnp.float32) * scale, 'key_in': jax.random.normal(ks[3], (ne, d), jnp.float32) * scale, 'key_out': jax.random.normal(ks[4], (ne, d), jnp.float32) * scale}
    _L1_ffn_in = _L1_ffn_setup()
    _d = {'L0_attn_x': _L0_attn_in['x'], 'L0_attn_W_qkv': _L0_attn_in['W_qkv'], 'L0_attn_ln_gamma': _L0_attn_in['ln_gamma'], 'L0_attn_ln_beta': _L0_attn_in['ln_beta'], 'L0_attn_W_proj': _L0_attn_in['W_proj'], 'L0_attn_b_proj': _L0_attn_in['b_proj'], 'L0_ffn_Win': _L0_ffn_in['Win'], 'L0_ffn_bin_': _L0_ffn_in['bin_'], 'L0_ffn_W1': _L0_ffn_in['W1'], 'L0_ffn_b1': _L0_ffn_in['b1'], 'L0_ffn_W2': _L0_ffn_in['W2'], 'L0_ffn_b2': _L0_ffn_in['b2'], 'L0_ffn_Wout': _L0_ffn_in['Wout'], 'L0_ffn_bout': _L0_ffn_in['bout'], 'L1_attn_Wq': _L1_attn_in['Wq'], 'L1_attn_bq': _L1_attn_in['bq'], 'L1_attn_Wk': _L1_attn_in['Wk'], 'L1_attn_bk': _L1_attn_in['bk'], 'L1_attn_Wv': _L1_attn_in['Wv'], 'L1_attn_bv': _L1_attn_in['bv'], 'L1_attn_Wo': _L1_attn_in['Wo'], 'L1_attn_bo': _L1_attn_in['bo'], 'L1_ffn_gamma': _L1_ffn_in['gamma'], 'L1_ffn_beta': _L1_ffn_in['beta'], 'L1_ffn_w_q': _L1_ffn_in['w_q'], 'L1_ffn_keys': _L1_ffn_in['keys'], 'L1_ffn_key_in': _L1_ffn_in['key_in'], 'L1_ffn_key_out': _L1_ffn_in['key_out']}
    _x0 = _d['L0_attn_x']
    _d['L0_attn_x'] = jax.random.normal(jax.random.fold_in(jax.random.key(seed), 1), (16, 256, 128), dtype=_x0.dtype)
    del _x0
    return _d

def reference(L0_attn_x, L0_attn_W_qkv, L0_attn_ln_gamma, L0_attn_ln_beta, L0_attn_W_proj, L0_attn_b_proj, L0_ffn_Win, L0_ffn_bin_, L0_ffn_W1, L0_ffn_b1, L0_ffn_W2, L0_ffn_b2, L0_ffn_Wout, L0_ffn_bout, L1_attn_Wq, L1_attn_bq, L1_attn_Wk, L1_attn_bk, L1_attn_Wv, L1_attn_bv, L1_attn_Wo, L1_attn_bo, L1_ffn_gamma, L1_ffn_beta, L1_ffn_w_q, L1_ffn_keys, L1_ffn_key_in, L1_ffn_key_out):

    def _L0_attn_ref(x, W_qkv, ln_gamma, ln_beta, W_proj, b_proj):
        import jax, jax.numpy as jnp
        import numpy as np
        NUM_HEADS = 16
        D_MODEL = 128
        HEAD_DIM = D_MODEL // NUM_HEADS
        WINDOW = 64
        SCALE = 8.0 / HEAD_DIM
        LN_EPS = 1e-05

        def _layernorm(t, gamma, beta):
            mu = jnp.mean(t, axis=-1, keepdims=True)
            var = jnp.var(t, axis=-1, keepdims=True)
            return (t - mu) * jax.lax.rsqrt(var + LN_EPS) * gamma + beta
        B, N, C = x.shape
        nw = N // WINDOW
        xw = x.reshape(B * nw, WINDOW, C)
        qkv = (xw @ W_qkv).reshape(B * nw, WINDOW, 3, NUM_HEADS, HEAD_DIM)
        q, k, v = (qkv[:, :, 0], qkv[:, :, 1], qkv[:, :, 2])
        q = _layernorm(q, ln_gamma, ln_beta)
        k = _layernorm(k, ln_gamma, ln_beta)
        attn = jnp.einsum('bqhd,bkhd->bhqk', q * SCALE, k)
        attn = jax.nn.softmax(attn, axis=-1)
        out = jnp.einsum('bhqk,bkhd->bqhd', attn, v).reshape(B * nw, WINDOW, C)
        out = out @ W_proj + b_proj
        return out.reshape(B, N, C)

    def _L0_ffn_ref(x, Win, bin_, W1, b1, W2, b2, Wout, bout):
        import jax, jax.numpy as jnp
        import numpy as np
        D_MODEL = 128
        M = 64
        INNER = 16
        s = jnp.einsum('btd,dm->btm', x, Win) + bin_
        h = jax.nn.relu(s[..., None] * W1 + b1)
        g = jnp.einsum('btmh,mh->btm', h, W2) + b2
        out = jnp.einsum('btm,md->btd', g, Wout) + bout
        return out

    def _L1_attn_ref(x, Wq, bq, Wk, bk, Wv, bv, Wo, bo):
        import jax, jax.numpy as jnp
        import numpy as np
        D_MODEL = 128
        N_HEADS = 16
        TOP_FACTOR = 5
        B, L, D = x.shape
        H = N_HEADS
        hd = D // H
        BH = B * H
        top_u = max(1, L // TOP_FACTOR)

        def proj(W, b):
            y = x @ W.T + b
            return y.reshape(B, L, H, hd).transpose(0, 2, 1, 3).reshape(BH, L, hd)
        Q = proj(Wq, bq)
        K = proj(Wk, bk)
        V = proj(Wv, bv)
        query_norms = jnp.linalg.norm(Q, axis=2)
        _, top_idx = jax.lax.top_k(query_norms, top_u)
        Q_sel = jnp.take_along_axis(Q, top_idx[:, :, None], axis=1)
        scale = 1.0 / hd ** 0.5
        scores = jnp.einsum('bud,bld->bul', Q_sel, K) * scale
        attn = jax.nn.softmax(scores, axis=-1)
        out_sel = jnp.einsum('bul,bld->bud', attn, V)
        out_full = jnp.zeros((BH, L, hd), dtype=x.dtype)
        out_full = out_full.at[jnp.arange(BH)[:, None], top_idx].set(out_sel)
        out = out_full.reshape(B, H, L, hd).transpose(0, 2, 1, 3).reshape(B, L, D)
        return out @ Wo.T + bo

    def _L1_ffn_ref(inputs, gamma, beta, w_q, keys, key_in, key_out):
        import jax, jax.numpy as jnp
        import numpy as np
        TOPK = 8
        BN_EPS = 1e-05
        b, n, d = inputs.shape
        h, nk, _, kd = keys.shape
        k = TOPK
        x = inputs.reshape(b * n, d)
        mu = jnp.mean(x, axis=0)
        var = jnp.mean(jnp.square(x - mu), axis=0)
        xn = (x - mu) * jax.lax.rsqrt(var + BN_EPS) * gamma + beta
        q = (xn @ w_q.T).reshape(b, n, 2, h, kd).transpose(2, 0, 1, 3, 4)
        sim = jnp.einsum('pbnhd,hkpd->pbnhk', q, keys)
        s, i = jax.lax.top_k(sim, k)
        sx, sy = (s[0], s[1])
        ix, iy = (i[0], i[1])
        all_scores = (sx[..., :, None] + sy[..., None, :]).reshape(b, n, h, k * k)
        all_idx = (ix[..., :, None] * nk + iy[..., None, :]).reshape(b, n, h, k * k)
        scores, pk = jax.lax.top_k(all_scores, k)
        idx = jnp.take_along_axis(all_idx, pk, axis=-1)
        w_down = key_in[idx]
        w_up = key_out[idx]
        o = jnp.einsum('bnd,bnhkd->bnhk', inputs, w_down)
        o = jax.nn.gelu(o, approximate=False) * jax.nn.softmax(scores, axis=-1)
        return jnp.einsum('bnhk,bnhkd->bnd', o, w_up)
    x = L0_attn_x
    x = x + 0.5 * _L0_ffn_ref(_layernorm(x, axis=-1), L0_ffn_Win, L0_ffn_bin_, L0_ffn_W1, L0_ffn_b1, L0_ffn_W2, L0_ffn_b2, L0_ffn_Wout, L0_ffn_bout)
    x = x + _L0_attn_ref(_layernorm(x, axis=-1), L0_attn_W_qkv, L0_attn_ln_gamma, L0_attn_ln_beta, L0_attn_W_proj, L0_attn_b_proj)
    x = x + 0.5 * _L0_ffn_ref(_layernorm(x, axis=-1), L0_ffn_Win, L0_ffn_bin_, L0_ffn_W1, L0_ffn_b1, L0_ffn_W2, L0_ffn_b2, L0_ffn_Wout, L0_ffn_bout)
    x = x + 0.5 * _L1_ffn_ref(_layernorm(x, axis=-1), L1_ffn_gamma, L1_ffn_beta, L1_ffn_w_q, L1_ffn_keys, L1_ffn_key_in, L1_ffn_key_out)
    x = x + _L1_attn_ref(_layernorm(x, axis=-1), L1_attn_Wq, L1_attn_bq, L1_attn_Wk, L1_attn_bk, L1_attn_Wv, L1_attn_bv, L1_attn_Wo, L1_attn_bo)
    x = x + 0.5 * _L1_ffn_ref(_layernorm(x, axis=-1), L1_ffn_gamma, L1_ffn_beta, L1_ffn_w_q, L1_ffn_keys, L1_ffn_key_in, L1_ffn_key_out)
    return x

_drawn_inputs = setup_inputs


def setup_inputs(seed=0):
    import zlib

    import numpy as np

    out = dict(_drawn_inputs(seed))
    spreads = {'L0_attn_ln_gamma': (1.0, 0.2),
     'L0_attn_ln_beta': (0.0, 0.1),
     'L1_attn_bq': (0.0, 0.8),
     'L1_attn_bk': (0.0, 0.8),
     'L1_attn_bv': (0.0, 0.8),
     'L1_attn_bo': (0.0, 0.1),
     'L1_ffn_gamma': (1.0, 0.6),
     'L1_ffn_beta': (0.0, 0.8)}
    factors = {'L0_attn_b_proj': 3.181,
     'L0_ffn_bin_': 8.0,
     'L1_attn_Wq': 6.629,
     'L1_attn_Wk': 8.0,
     'L1_attn_Wv': 8.0,
     'L1_attn_Wo': 5.731,
     'L1_ffn_w_q': 8.0,
     'L1_ffn_keys': 8.0,
     'L1_ffn_key_in': 8.0,
     'L1_ffn_key_out': 8.0}
    for name, (base, spread) in spreads.items():
        noise = np.random.default_rng([zlib.crc32(name.encode()), seed]).standard_normal(out[name].shape)
        drawn = base * np.exp(spread * noise) if base else spread * noise
        out[name] = jnp.asarray(drawn.astype(out[name].dtype))
    for name, factor in factors.items():
        out[name] = (out[name] * factor).astype(out[name].dtype)
    return out
```

```python
import concourse.bass as bass
from concourse import mybir
from contextlib import ExitStack

import numpy as np

P = 128
D = 128
BATCH, SEQ = 16, 256
T = BATCH * SEQ
NT = T // P
HEADS, HD = 16, 8
WIN = 64
GT = 4
NG = NT // GT
GW = GT * P
NP_ = NT // 2
M_FF, INNER = 64, 16
NJ = INNER // 2
TOP_U = SEQ // 5
PH, NK, KD, TOPK = 8, 32, 128, 8
NE = NK * NK
NCH = NE // P
LN_EPS = 1e-5
STAGES = 6
STOP = 6


def build(nc, A, out):
    fp32 = mybir.dt.float32
    ALU = mybir.AluOpType
    ACT = mybir.ActivationFunctionType
    X = mybir.AxisListType.X

    ctx = ExitStack()
    with ctx:
        def sb(name, shape):
            return ctx.enter_context(nc.sbuf_tensor(name, shape, fp32))

        def sem(name):
            return ctx.enter_context(nc.semaphore(name))

        def sems(stage, names):
            return {n: sem(f"{stage}_{n}") for n in names.split()}

        x_sb = sb("x_sb", [P, NT, D])
        xT = sb("xT", [P, T])
        ident = sb("ident", [P, P])
        hmask = sb("hmask", [P, 4])
        vmask = sb("vmask", [P, 2])
        headsel = sb("headsel", [P, 8, P])
        stats = sb("stats", [P, NT, 6])
        mdiff = sb("mdiff", [P, NT])
        negmean = sb("negmean", [P, NT])
        vareps = sb("vareps", [P, NT])
        stdev = sb("stdev", [P, NT])
        rstd = sb("rstd", [P, NT])
        xn = sb("xn", [P, 2, GT, D])
        win2 = sb("win2", [P, 2, M_FF])
        bin2 = sb("bin2", [P, 1])
        w1c = sb("w1c", [P, NJ])
        b1c = sb("b1c", [P, NJ])
        b1e = sb("b1e", [P, NJ])
        w2c = sb("w2c", [P, NJ])
        b2c = sb("b2c", [M_FF, 1])
        b2r = sb("b2r", [M_FF, P])
        wout2 = sb("wout2", [P, D])
        w2o = sb("w2o", [P, NJ, D])
        bout_bc = sb("bout_bc", [P, D])
        ffn_add = sb("ffn_add", [P, D])
        wqkv = sb("wqkv", [P, 3 * D])
        wproj = sb("wproj", [P, D])
        bproj_bc = sb("bproj_bc", [P, D])
        gcol = sb("gcol", [P, 1])
        bcol = sb("bcol", [P, 1])
        gk = sb("gk", [P, 4])
        bk4 = sb("bk4", [P, 4])
        w1nat = sb("w1nat", [P, 4, D])
        w1T = sb("w1T", [P, 4, D])
        bqc = sb("bqc", [P, 1])
        bkc = sb("bkc", [P, 1])
        bkm = sb("bkm", [P, 4])
        bv_bc = sb("bv_bc", [P, D])
        bo_bc = sb("bo_bc", [P, D])
        weff = sb("weff", [P, 2, PH, NK])
        kinT = sb("kinT", [P, NE])
        kout = sb("kout", [P, NCH, D])
        pg = sb("pg", [P, 1])
        pb_ = sb("pb_", [P, 1])
        work = sb("work", [P, 26000])

        def cut(at, *shape):
            n = int(np.prod(shape))
            v = work[:, at:at + n]
            if len(shape) == 2:
                v = v.rearrange("p (a b) -> p a b", b=shape[1])
            if len(shape) == 3:
                v = v.rearrange("p (a b c) -> p a b c", b=shape[1], c=shape[2])
            if len(shape) == 4:
                v = v.rearrange("p (a b c d) -> p a b c d", b=shape[1], c=shape[2], d=shape[3])
            return v, at + n

        bank = [ctx.enter_context(nc.psum_tensor(f"bank{i}", [P, 512], fp32)) for i in range(8)]

        s_x = sem("s_x")
        s_w = sem("s_w")
        s_out = sem("s_out")
        s_go = sem("s_go")
        s_set = sem("s_set")
        s_setp = sem("s_setp")
        s_ps = sem("s_ps")
        pr = sems("pr", "stat aggr nm ve sd rstd xn tr ev sq")
        ff = sems("ff", "s h o cb x")
        L0 = sems("l0", "xs qk v cent sq rsum var sd rs qn qt qT kT st mx sub ex pt pe pv vb rec on ot oe y cb x")
        L1 = sems("l1", "sq_used pq psq pn nc mr selT str sel xs qk v qT kT vb st mx ex pt pe pv rec on ot oe y cb x")
        pk = sems("pk", "bst bag bve bsd brs bsc zt sim m8 sub ex cand c8 z rz sc P A M acc cg o g ct ce y x ys")
        last_x = {0: (s_x, 16 * NG)}
        last_x[1] = (ff["x"], 2 + NG)
        last_x[2] = (L0["x"], NP_)
        last_x[3] = (ff["x"], 2 + 2 * NG)
        last_x[4] = (pk["x"], 1 + NT)
        last_x[5] = (L1["x"], NP_)
        last_x[6] = (pk["x"], 1 + 2 * NT)

        h_ff, _ = cut(0, 2, NJ, GW)
        xs0, o = cut(0, 2 * P)
        qc0, o = cut(o, 512)
        sq0, o = cut(o, 512)
        qn0, o = cut(o, 4, P)
        qT0, o = cut(o, 2, P)
        kT0, o = cut(o, 4, 2, P)
        E0, o = cut(o, 4, 512)
        PT0, o = cut(o, 16, P)
        Vb0, o = cut(o, 32, 2, 9)
        on0, o = cut(o, 2, P)
        oT0, o = cut(o, 2, P)
        sum0, o = cut(o, 64)
        var0, o = cut(o, 64)
        sd0, o = cut(o, 64)
        rs0, o = cut(o, 64)
        mx0, o = cut(o, 4, 8)
        rec0, o = cut(o, 2, 16)
        sq1, o = cut(0, 2, SEQ)
        n2, o = cut(o, 2, SEQ)
        n2w, o = cut(o, 2, SEQ)
        m8, o = cut(o, 2, 8)
        selT, o = cut(o, 2, SEQ)
        sel, o = cut(o, 2, 2, P)
        xs1, o = cut(o, SEQ)
        qT1, o = cut(o, SEQ)
        kT1, o = cut(o, 4, SEQ)
        Vs1, o = cut(o, 2, HEADS, HD + 1)
        E1, o = cut(o, 8, SEQ)
        PT1, o = cut(o, 16, P)
        on1, o = cut(o, 2, P)
        oT1, o = cut(o, 2, P)
        mx1, o = cut(o, 8)
        rec1, o = cut(o, 2, 16)
        NPS, NMS = 4, 4
        bnst, o = cut(0, 8, 6)
        bnmv, o = cut(o, 2)
        bnve, o = cut(o, 1)
        bnsd, o = cut(o, 1)
        bnrs, o = cut(o, 1)
        bna, o = cut(o, 1)
        bnb, o = cut(o, 1)
        zT, o = cut(o, 2, P)
        yT, o = cut(o, 2, P)
        E5, o = cut(o, 2, 640)
        exs, o = cut(o, 2, PH * NK)
        m8raw, o = cut(o, 16, 8)
        cand, o = cut(o, PH, 20)
        c8, o = cut(o, PH, 8)
        zsum, o = cut(o, PH)
        rz, o = cut(o, PH)
        thr, o = cut(o, 2, PH)
        Pm, o = cut(o, NPS, NE)
        Mm, o = cut(o, NMS, NE)
        G5, o = cut(o, 2, NE)
        cg, o = cut(o, NE)
        cgT, o = cut(o, NE)
        assert o <= 26000, o
        POOL_HEADS = [0, 1, 2, 3, 4, 6, 7]
        DVE_HEADS = [h for h in range(PH) if h not in POOL_HEADS]
        MERGED = [7]
        UNITS = [h for h in range(PH) if h + 1 not in MERGED]
        NU = len(UNITS)

        def grid(buf, slot):
            return buf[:, slot, :].rearrange("p (i j) -> p i j", j=NK)

        def ex_rows(par, h):
            return exs[:, par, h * NK:(h + 1) * NK].unsqueeze(2).to_broadcast([P, NK, NK])

        def ey_cols(par, h):
            at = (PH + h) * NK
            return E5[:, par, at:at + NK].unsqueeze(1).to_broadcast([P, NK, NK])

        keysn, o = cut(0, 4, P)
        keysT, o = cut(o, 512)
        wqn, o = cut(o, 16, P)
        kinn, o = cut(o, NCH, P)

        block = ctx.enter_context(nc.Block())

        SET_FFN = 16
        NW = 1 + 12 + 1 + 4 + 3 + 2 + 2 + 4 + 4 + 4

        @block.sync
        def _(sp):
            xv = A["L0_attn_x"].rearrange("b (c p) d -> p (b c) d", p=P)
            nw = 0

            def load(dst, src):
                sp.dma_start(dst, src).then_inc(s_w, 16)

            load(ident[:, :], A["c_ident"])
            for g in range(NG):
                sp.dma_start(x_sb[:, g * GT:(g + 1) * GT, :], xv[:, g * GT:(g + 1) * GT, :]).then_inc(s_x, 16)
            for r in range(2):
                half = slice(r * M_FF, (r + 1) * M_FF)
                load(win2[:, r, :], A["L0_ffn_Win"])
                load(bin2[half, :], A["L0_ffn_bin_"].rearrange("(m o) -> m o", o=1))
                load(w1c[half, :], A["L0_ffn_W1"].rearrange("m (r j) -> r m j", r=2)[r])
                load(b1c[half, :], A["L0_ffn_b1"].rearrange("m (r j) -> r m j", r=2)[r])
                load(w2c[half, :], A["L0_ffn_W2"].rearrange("m (r j) -> r m j", r=2)[r])
                load(wout2[half, :], A["L0_ffn_Wout"])
            load(b2c[:, :], A["L0_ffn_b2"].rearrange("(m o) -> m o", o=1))
            for dst, name in ((bout_bc, "L0_ffn_bout"), (bproj_bc, "L0_attn_b_proj"), (bv_bc, "L1_attn_bv"),
                              (bo_bc, "L1_attn_bo")):
                load(dst[:, :], A[name].rearrange("(o d) -> o d", o=1).to_broadcast([P, D]))
            load(hmask[:, :], A["c_hmask"])
            load(vmask[:, :], A["c_vmask"])
            load(headsel[:, :, :], A["c_headsel"])
            load(wqkv[:, :], A["L0_attn_W_qkv"])
            load(wproj[:, :], A["L0_attn_W_proj"])
            for dst, name in ((gcol, "L0_attn_ln_gamma"), (bcol, "L0_attn_ln_beta")):
                load(dst[:, :], A[name].rearrange("(o d e) -> o d e", o=1, e=1).to_broadcast([HEADS, HD, 1]))
            for i, name in enumerate(("Wq", "Wk", "Wv", "Wo")):
                load(w1nat[:, i, :], A[f"L1_attn_{name}"])
            load(bqc[:, :], A["L1_attn_bq"].rearrange("(m o) -> m o", o=1))
            load(bkc[:, :], A["L1_attn_bk"].rearrange("(m o) -> m o", o=1))
            load(pg[:, :], A["L1_ffn_gamma"].rearrange("(m o) -> m o", o=1))
            load(pb_[:, :], A["L1_ffn_beta"].rearrange("(m o) -> m o", o=1))
            load(keysn, A["L1_ffn_keys"].rearrange("h k p d -> (h k p) d").rearrange("(c q) d -> q c d", q=P))
            load(wqn, A["L1_ffn_w_q"].rearrange("(c q) d -> q c d", q=P))
            load(kinn, A["L1_ffn_key_in"].rearrange("(c q) d -> q c d", q=P))
            load(kout[:, :, :], A["L1_ffn_key_out"].rearrange("(c q) d -> q c d", q=P))
            ov = out.rearrange("b (c p) d -> p (b c) d", p=P)
            sp.wait_ge(*last_x[STOP])
            for g in range(4):
                sp.dma_start(ov[:, g * 8:(g + 1) * 8, :], x_sb[:, g * 8:(g + 1) * 8, :]).then_inc(s_out, 16)
            sp.wait_ge(s_out, 64)


        @block.gpsimd
        def _(pool):
            def add_row(row, rows, done):
                with pool.Fori(0, NG) as g:
                    xg = x_sb[:, bass.ds(g * GT, GT), :]
                    nc.gpsimd.tensor_tensor(xg, xg, row[:, :].unsqueeze(1).to_broadcast([P, GT, D]),
                                            ALU.add).then_inc(done, 1)

            def xslots(s, slot, used):
                nc.gpsimd.tensor_copy(slot, xT[:, 0:SEQ]).then_inc(s["xs"], 1)
                with pool.Fori(1, NP_) as u:
                    pool.wait_ge(used, u)
                    nc.gpsimd.tensor_copy(slot, xT[:, bass.ds(u * SEQ, SEQ)]).then_inc(s["xs"], 1)

            def product_keys(s, f):
                base = f * NT
                def tile(n, par, front=True):
                    pool.wait_ge(s["sc"], 2 * (base + n) + 2)
                    for at, h in enumerate(POOL_HEADS):
                        pool.wait_ge(s["M"], 8 * (base + n) + h + 5)
                        nc.gpsimd.tensor_tensor(grid(Pm, h % NPS), ex_rows(par, h), ey_cols(par, h),
                                                ALU.mult).then_inc(s["P"], 1)

                tile(0, 0)
                with pool.Fori(0, NT // 2 - 1) as i:
                    tile(2 * i + 1, 1)
                    tile(2 * i + 2, 0)
                tile(NT - 1, 1, front=False)

            for k in range(STAGES):
                if k >= STOP:
                    break
                s = pr
                pool.wait_ge(s["tr"], 2 + (k + 1) * NG)
                if k == 0 or k == 2:
                    if k == 0:
                        pool.wait_ge(s_set, SET_FFN)
                    add_row(ffn_add, None, ff["cb"])
                if k == 1:
                    pool.wait_ge(s_w, 16 * NW)
                    add_row(bproj_bc, None, L0["cb"])
                    pool.wait_ge(s["ev"], 2 + (k + 1) * NG)
                    xslots(L0, xs0, L0["x"])
                if k == 4:
                    add_row(bo_bc, None, L1["cb"])
                    pool.wait_ge(s["ev"], 2 + (k + 1) * NG)
                    xslots(L1, xs1, L1["x"])
                if k == 3 or k == 5:
                    product_keys(pk, (k - 3) // 2)


        @block.vector
        def _(dve):
            seq = [0]

            dve.sem_inc(pk["M"], 8)
            dve.sem_inc(pk["x"], 1)
            dve.sem_inc(pk["ys"], 1)
            dve.sem_inc(ff["x"], 2)
            dve.sem_inc(L1["pe"], 1)

            def setup():
                dve.wait_ge(s_w, 16 * NW)
                nc.vector.tensor_scalar(b1e[:, :], w1c[:, :], bin2[:, 0:1], None, ALU.mult).then_inc(s_set, 1)
                dve.wait_ge(s_set, 1)
                nc.vector.tensor_tensor(b1e[:, :], b1e[:, :], b1c[:, :], ALU.add).then_inc(s_set, 1)
                nc.vector.tensor_copy(b2r[:, :], b2c[:, 0:1].to_broadcast([M_FF, P])).then_inc(s_set, 1)
                for j in range(NJ):
                    nc.vector.tensor_scalar(w2o[:, j, :], wout2[:, :], w2c[:, j:j + 1], None,
                                            ALU.mult).then_inc(s_set, 1)
                nc.vector.tensor_scalar(gk[:, :], hmask[:, :], gcol[:, 0:1], None, ALU.mult).then_inc(s_set, 1)
                nc.vector.tensor_scalar(bk4[:, :], hmask[:, :], bcol[:, 0:1], None, ALU.mult).then_inc(s_set, 1)
                nc.vector.tensor_scalar(bkm[:, :], hmask[:, :], bkc[:, 0:1], None, ALU.mult).then_inc(s_set, 1)
                dve.wait_ge(s_ps, 1)
                nc.vector.tensor_tensor(ffn_add[:, :], bank[0][:, 0:D], bout_bc[:, :], ALU.add).then_inc(s_set, 1)
                dve.wait_ge(s_set, 15)
                nc.vector.tensor_scalar(ffn_add[:, :], ffn_add[:, :], 0.5, None, ALU.mult).then_inc(s_set, 1)
                dve.wait_ge(s_ps, 2)
                nc.vector.tensor_copy(w1T[:, :, :].rearrange("p a b -> p (a b)"), bank[1][:, :]).then_inc(s_set, 1)
                nc.vector.tensor_copy(keysT, bank[2][:, :]).then_inc(s_set, 1)
                nc.vector.tensor_copy(kinT[:, 0:512], bank[3][:, :]).then_inc(s_set, 1)
                nc.vector.tensor_copy(kinT[:, 512:1024], bank[4][:, :]).then_inc(s_set, 1)
                dve.wait_ge(s_ps, 3)
                nc.vector.tensor_copy(weff[:, :, :, :].rearrange("p a b c -> p (a b c)"),
                                      bank[5][:, :]).then_inc(s_set, 1)
                dve.wait_ge(s_set, 21)

            def prep(k):
                s, base = pr, k * NG
                dve.wait_ge(*last_x[k])
                with dve.Fori(0, NT) as n:
                    nc.vector.bn_stats(stats[:, bass.ds(n, 1), :], x_sb[:, bass.ds(n, 1), :]).then_inc(s["stat"], 1)
                dve.wait_ge(s["stat"], (k + 1) * NT)
                even, odd = stats[:, :, 1], stats[:, :, 4]
                nc.vector.tensor_tensor(negmean[:, :], even, odd, ALU.add).then_inc(s["aggr"], 1)
                nc.vector.tensor_tensor(mdiff[:, :], even, odd, ALU.subtract).then_inc(s["aggr"], 1)
                nc.vector.tensor_tensor(vareps[:, :], stats[:, :, 2], stats[:, :, 5], ALU.add).then_inc(s["aggr"], 1)
                dve.wait_ge(s["aggr"], 3 * (k + 1))
                nc.vector.tensor_scalar(negmean[:, :], negmean[:, :], -0.5, None, ALU.mult).then_inc(s["nm"], 1)
                nc.vector.scalar_tensor_tensor(mdiff[:, :], mdiff[:, :], 0.25, mdiff[:, :], ALU.mult,
                                               ALU.mult).then_inc(s["sq"], 1)
                nc.vector.tensor_scalar(vareps[:, :], vareps[:, :], 1.0 / D, LN_EPS, ALU.mult,
                                        ALU.add).then_inc(s["sq"], 1)
                dve.wait_ge(s["sq"], 2 * (k + 1))
                nc.vector.tensor_tensor(vareps[:, :], vareps[:, :], mdiff[:, :], ALU.add).then_inc(s["ve"], 1)
                dve.wait_ge(s["sd"], k + 1)
                nc.vector.reciprocal(rstd[:, :], stdev[:, :]).then_inc(s["rstd"], 1)
                dve.wait_ge(s["rstd"], k + 1)
                dve.wait_ge(s["nm"], k + 1)

                def normalise(n, par):
                    dve.wait_ge(s["tr"], base + n + 1)
                    for t in range(GT):
                        c = n * GT + t
                        last = nc.vector.tensor_scalar(xn[:, par, t, :], x_sb[:, bass.ds(c, 1), :],
                                                       negmean[:, bass.ds(c, 1)], rstd[:, bass.ds(c, 1)],
                                                       ALU.add, ALU.mult)
                    last.then_inc(s["xn"], 1)

                with dve.Fori(0, NG // 2) as i:
                    for par in range(2):
                        normalise(2 * i + par, par)

            def ffn(s, f):
                base = f * NG
                with dve.Fori(0, NG // 2) as i:
                    for par in range(2):
                        g = 2 * i + par
                        dve.wait_ge(s["o"], base + g + 3)
                        dve.wait_ge(s["cb"], base + g + 1)
                        xg = x_sb[:, bass.ds(g * GT, GT), :].rearrange("p a b -> p (a b)")
                        nc.vector.scalar_tensor_tensor(xg, bank[4 + par][:, :], 0.5, xg, ALU.mult,
                                                       ALU.add).then_inc(s["x"], 1)

            def l0(s):
                ones = Vb0[:, :, :, HD]
                nc.vector.tensor_copy(ones, vmask[:, :].unsqueeze(1).to_broadcast([P, 32, 2])).then_inc(s["vb"], 1)
                with dve.Fori(0, NP_) as u:
                    dve.wait_ge(s["qk"], u + 1)
                    qk = bank[4][:, :].rearrange("p (h d) -> p h d", d=HD)
                    qc = qc0.rearrange("p (h d) -> p h d", d=HD)
                    nc.vector.tensor_reduce(sum0, qk, X, ALU.add).then_inc(s["rsum"], 1)
                    dve.wait_ge(s["rsum"], 2 * u + 1)
                    nc.vector.scalar_tensor_tensor(qc, sum0.unsqueeze(2).to_broadcast([P, 64, HD]), -1.0 / HD, qk,
                                                   ALU.mult, ALU.add).then_inc(s["cent"], 1)
                    dve.wait_ge(s["sq"], u + 1)
                    nc.vector.tensor_reduce(var0, sq0.rearrange("p (h d) -> p h d", d=HD), X,
                                            ALU.add).then_inc(s["rsum"], 1)
                    dve.wait_ge(s["rsum"], 2 * u + 2)
                    nc.vector.tensor_scalar(var0, var0, 1.0 / HD, LN_EPS, ALU.mult, ALU.add).then_inc(s["var"], 1)
                    dve.wait_ge(s["sd"], u + 1)
                    nc.vector.reciprocal(rs0, sd0).then_inc(s["rs"], 1)
                    dve.wait_ge(s["rs"], u + 1)
                    nc.vector.tensor_tensor(qn0.rearrange("p a (h d) -> p (a h) d", d=HD), qc,
                                            rs0.unsqueeze(2).to_broadcast([P, 64, HD]), ALU.mult).then_inc(s["qn"], 1)
                    dve.wait_ge(s["v"], u + 1)
                    vps = bank[5][:, :].rearrange("p (w r d) -> p w r d", r=2, d=HD)
                    for r in range(2):
                        last = nc.vector.tensor_scalar(Vb0[:, :, r, 0:HD], vps[:, :, r, :], vmask[:, r:r + 1], None,
                                                       ALU.mult)
                    last.then_inc(s["vb"], 1)
                    dve.wait_ge(s["qt"], u + 1)
                    nc.vector.tensor_scalar(qT0, bank[6][:, 0:2 * P].rearrange("p (t q) -> p t q", q=P), gcol[:, 0:1],
                                            bcol[:, 0:1], ALU.mult, ALU.add).then_inc(s["qT"], 1)
                    for g in range(4):
                        dve.wait_ge(s["st"], 4 * u + g + 1)
                        sv = bank[g][:, :].rearrange("p (h k) -> p h k", k=WIN)
                        nc.vector.tensor_reduce(mx0[:, g, :], sv, X, ALU.max).then_inc(s["mx"], 1)
                        dve.wait_ge(s["mx"], 4 * u + g + 1)
                        nc.vector.tensor_tensor(E0[:, g, :].rearrange("p (h k) -> p h k", k=WIN), sv,
                                                mx0[:, g, :].unsqueeze(2).to_broadcast([P, 8, WIN]),
                                                ALU.subtract).then_inc(s["sub"], 1)
                    dve.wait_ge(s["pv"], u + 1)
                    ov = bank[7][:, 0:288].rearrange("p (t h e) -> p t h e", t=2, e=HD + 1)
                    nc.vector.reciprocal(rec0, ov[:, :, :, HD]).then_inc(s["rec"], 1)
                    dve.wait_ge(s["rec"], u + 1)
                    for t in range(2):
                        last = nc.vector.tensor_tensor(on0[:, t, :].rearrange("p (h d) -> p h d", d=HD),
                                                       ov[:, t, :, 0:HD],
                                                       rec0[:, t, :].unsqueeze(2).to_broadcast([P, HEADS, HD]),
                                                       ALU.mult)
                    last.then_inc(s["on"], 1)
                    dve.wait_ge(s["y"], u + 1)
                    xu = x_sb[:, bass.ds(2 * u, 2), :].rearrange("p a b -> p (a b)")
                    nc.vector.tensor_tensor(xu, bank[5][:, 0:2 * P], xu, ALU.add).then_inc(s["x"], 1)

            def l1(s):
                for half in range(2):
                    dve.wait_ge(s["pn"], half + 1)
                    nc.vector.tensor_copy(n2[:, half, :], bank[2 + half][:, 0:SEQ]).then_inc(s["nc"], 1)
                rounds = -(-TOP_U // 8)
                for r in range(rounds):
                    for half in range(2):
                        src = n2 if r == 0 else n2w
                        dve.wait_ge(s["nc"], half + 1)
                        if r:
                            dve.wait_ge(s["mr"], 4 * r - 2 + half + 1)
                        nc.vector.max(m8[:, half, :], src[:, half, :]).then_inc(s["mr"], 1)
                    if r < rounds - 1:
                        for half in range(2):
                            dve.wait_ge(s["mr"], 4 * r + half + 1)
                            nc.vector.match_replace(n2w[:, half, :], m8[:, half, :], (n2 if r == 0 else n2w)[:, half, :],
                                                    -1.0).then_inc(s["mr"], 1)
                dve.wait_ge(s["mr"], 4 * (rounds - 1) + 2)
                rank = (TOP_U - 1) % 8
                for half in range(2):
                    nc.vector.tensor_scalar(selT[:, half, :], n2[:, half, :], m8[:, half, rank:rank + 1], None,
                                            ALU.is_ge).then_inc(s["selT"], 1)
                dve.wait_ge(s["str"], 1)
                nc.vector.tensor_copy(sel.rearrange("p a b c -> p (a b c)"), bank[4][:, :]).then_inc(s["sel"], 1)
                nc.vector.memset(Vs1[:, :, :, HD], 1.0).then_inc(s["vb"], 1)
                dve.wait_ge(s["sel"], 1)
                with dve.Fori(0, NP_) as b:
                    dve.wait_ge(s["qk"], b + 1)
                    nc.vector.tensor_scalar(qT1, bank[4][:, 0:SEQ], bqc[:, 0:1], HD ** -0.5, ALU.add,
                                            ALU.mult).then_inc(s["qT"], 1)
                    dve.wait_ge(s["v"], b + 1)
                    for c in range(2):
                        last = nc.vector.tensor_tensor(Vs1[:, c, :, 0:HD],
                                                       bank[5][:, c * P:(c + 1) * P].rearrange("p (h d) -> p h d", d=HD),
                                                       bv_bc[:, :].rearrange("p (h d) -> p h d", d=HD), ALU.add)
                    last.then_inc(s["vb"], 1)
                    for step in range(4):
                        for g in range(4):
                            at = 4 * step + g
                            dve.wait_ge(s["st"], 16 * b + at + 1)
                            dve.wait_ge(s["ex"], 32 * b + 8 * step + 1)
                            nc.vector.tensor_reduce(mx1[:, 2 * g:2 * g + 2],
                                                    bank[g][:, :].rearrange("p (h k) -> p h k", k=SEQ), X, ALU.max,
                                                    negate=True).then_inc(s["mx"], 1)
                        for g in range(4):
                            at = 4 * step + g
                            dve.wait_ge(s["pt"], 16 * b + at + 1)
                            nc.vector.tensor_copy(PT1[:, 4 * g:4 * g + 4, :].rearrange("p a b -> p (a b)"),
                                                  bank[6 if g % 2 else 4][:, :]).then_inc(s["pe"], 1)
                    dve.wait_ge(s["pv"], 4 * b + 4)
                    ov = bank[7][:, 0:288].rearrange("p (t h e) -> p t h e", t=2, e=HD + 1)
                    nc.vector.reciprocal(rec1, ov[:, :, :, HD]).then_inc(s["rec"], 1)
                    dve.wait_ge(s["rec"], 2 * b + 1)
                    nc.vector.tensor_tensor(rec1, rec1, sel.rearrange("p a b c -> p a (b c)")[:, :, bass.ds(b * HEADS, HEADS)],
                                            ALU.mult).then_inc(s["rec"], 1)
                    dve.wait_ge(s["rec"], 2 * b + 2)
                    for t in range(2):
                        last = nc.vector.tensor_tensor(on1[:, t, :].rearrange("p (h d) -> p h d", d=HD),
                                                       ov[:, t, :, 0:HD],
                                                       rec1[:, t, :].unsqueeze(2).to_broadcast([P, HEADS, HD]),
                                                       ALU.mult)
                    last.then_inc(s["on"], 1)
                    dve.wait_ge(s["y"], b + 1)
                    xu = x_sb[:, bass.ds(2 * b, 2), :].rearrange("p a b -> p (a b)")
                    nc.vector.tensor_tensor(xu, bank[5][:, 0:2 * P], xu, ALU.add).then_inc(s["x"], 1)

            def product_keys(s, f):
                base = f * NT
                dve.wait_ge(pr["ev"], 2 + (2 * f + 4) * NG)
                for g in range(NG):
                    last = nc.vector.bn_stats(bnst[:, g, :], xT[:, g * GW:(g + 1) * GW])
                last.then_inc(s["bst"], 1)
                dve.wait_ge(s["bst"], f + 1)
                nc.vector.bn_aggr(bnmv, bnst.rearrange("p a b -> p (a b)")).then_inc(s["bag"], 1)
                dve.wait_ge(s["bag"], f + 1)
                nc.vector.tensor_scalar(bnve, bnmv[:, 1:2], LN_EPS, None, ALU.add).then_inc(s["bve"], 1)
                dve.wait_ge(s["bsd"], f + 1)
                nc.vector.reciprocal(bnrs, bnsd).then_inc(s["brs"], 1)
                dve.wait_ge(s["brs"], 2 * f + 1)
                nc.vector.tensor_tensor(bna, pg[:, :], bnrs, ALU.mult).then_inc(s["bsc"], 1)
                dve.wait_ge(s["bsc"], 2 * f + 1)
                nc.vector.tensor_tensor(bnrs, bnmv[:, 0:1], bna, ALU.mult).then_inc(s["brs"], 1)
                dve.wait_ge(s["brs"], 2 * f + 2)
                nc.vector.tensor_tensor(bnb, pb_[:, :], bnrs, ALU.subtract).then_inc(s["bsc"], 1)

                def top8(n, par):
                    dve.wait_ge(s["sim"], base + n + 3)
                    dve.sem_inc(s_go, 1)
                    for c in range(2 * PH):
                        last = nc.vector.max(m8raw[:, c, :], bank[0][:, c * NK:(c + 1) * NK])
                    last.then_inc(s["m8"], 1)
                    dve.wait_ge(s["m8"], base + n + 1)
                    first = m8raw[:, :, 0:1]
                    nc.vector.tensor_tensor(E5[:, par, 0:512].rearrange("p (c k) -> p c k", k=NK),
                                            bank[0][:, :].rearrange("p (c k) -> p c k", k=NK),
                                            first.to_broadcast([P, 2 * PH, NK]), ALU.subtract).then_inc(s["sub"], 1)
                    nc.vector.tensor_tensor(E5[:, par, 512:640].rearrange("p (c k) -> p c k", k=8), m8raw,
                                            first.to_broadcast([P, 2 * PH, 8]), ALU.subtract).then_inc(s["sub"], 1)

                def weights(n, par):
                    dve.wait_ge(s["ex"], base + n + 1)
                    e8 = E5[:, par, 512:640].rearrange("p (q h k) -> p q h k", q=2, k=8)
                    x8, y8 = e8[:, 0], e8[:, 1]

                    def rank_products(at, a, na, b, nb):
                        m = max(na, nb)
                        xa = x8[:, :, a:a + na].to_broadcast([P, PH, m]) if na < m else x8[:, :, a:a + na]
                        yb = y8[:, :, b:b + nb].to_broadcast([P, PH, m]) if nb < m else y8[:, :, b:b + nb]
                        return nc.vector.tensor_tensor(cand[:, :, at:at + m], xa, yb, ALU.mult)

                    rank_products(0, 0, 1, 0, 8)
                    rank_products(8, 1, 1, 0, 4)
                    rank_products(12, 2, 6, 0, 1)
                    rank_products(18, 2, 2, 1, 1).then_inc(s["cand"], 1)
                    dve.wait_ge(s["cand"], base + n + 1)
                    dve.sem_inc(s_go, 1)
                    for h in range(PH):
                        last = nc.vector.max(c8[:, h, :], cand[:, h, :])
                    last.then_inc(s["c8"], 1)
                    dve.wait_ge(s["c8"], base + n + 1)
                    nc.vector.tensor_reduce(zsum, c8, X, ALU.add).then_inc(s["z"], 1)
                    dve.wait_ge(s["z"], base + n + 1)
                    nc.vector.reciprocal(rz, zsum).then_inc(s["rz"], 1)
                    dve.wait_ge(s["rz"], base + n + 1)
                    nc.vector.tensor_tensor(exs[:, par, :].rearrange("p (h k) -> p h k", k=NK),
                                            E5[:, par, 0:256].rearrange("p (h k) -> p h k", k=NK),
                                            rz.unsqueeze(2).to_broadcast([P, PH, NK]), ALU.mult).then_inc(s["sc"], 1)
                    nc.vector.scalar_tensor_tensor(thr[:, par, :], c8[:, :, 7], 1.0 - 5e-7, rz, ALU.mult,
                                                   ALU.mult).then_inc(s["sc"], 1)

                def combine(m, par):
                    dve.wait_ge(s["acc"], NU * (base + m + 2))
                    dve.wait_ge(s["g"], 2 * (base + m + 1))
                    for half in range(2):
                        c = slice(half * 512, (half + 1) * 512)
                        nc.vector.tensor_tensor(cg[:, c], bank[2 + 2 * par + half][:, :], G5[:, par, c],
                                                ALU.mult).then_inc(s["cg"], 1)

                def update(m):
                    dve.wait_ge(s["y"], base + m + 1)
                    xm = x_sb[:, bass.ds(m, 1), :].rearrange("p a b -> p (a b)")
                    nc.vector.scalar_tensor_tensor(xm, bank[7][:, 0:D], 0.5, xm, ALU.mult, ALU.add).then_inc(s["x"], 1)

                def tile(n, par, front=True, finish=True):
                    dve.wait_ge(s["sc"], 2 * (base + n) + 2)
                    for h in range(PH):
                        if h in POOL_HEADS:
                            dve.wait_ge(s["P"], len(POOL_HEADS) * (base + n) + POOL_HEADS.index(h) + 1)
                        else:
                            dve.wait_ge(s["M"], 8 * (base + n) + h + 5)
                            nc.vector.tensor_tensor(grid(Pm, h % NPS), ex_rows(par, h), ey_cols(par, h),
                                                    ALU.mult).then_inc(s["A"], 1)
                            dve.wait_ge(s["A"], len(DVE_HEADS) * (base + n) + DVE_HEADS.index(h) + 1)
                        back = h - NMS
                        if back >= 0 and back in UNITS:
                            dve.wait_ge(s["acc"], NU * (base + n + 1) + UNITS.index(back) + 1)
                        if back < 0 and back + PH in UNITS:
                            dve.wait_ge(s["acc"], NU * (base + n) + UNITS.index(back + PH) + 1)
                        if back >= 0 and back + 1 in MERGED:
                            dve.wait_ge(s["ys"], len(MERGED) * (base + n) + MERGED.index(back + 1) + 2)
                        if back < 0 and back + PH + 1 in MERGED:
                            dve.wait_ge(s["ys"], len(MERGED) * (base + n - 1) + MERGED.index(back + PH + 1) + 2)
                        nc.vector.scalar_tensor_tensor(Mm[:, h % NMS, :], Pm[:, h % NPS, :], thr[:, par, h:h + 1],
                                                       Pm[:, h % NPS, :], ALU.is_ge, ALU.mult).then_inc(s["M"], 1)
                        if h in MERGED:
                            dve.wait_ge(s["M"], 8 * (base + n) + h + 9)
                            nc.vector.tensor_tensor(Mm[:, h % NMS, :], Mm[:, h % NMS, :], Mm[:, (h - 1) % NMS, :],
                                                    ALU.add).then_inc(s["ys"], 1)
                        if h == 1 and front:
                            top8(n + 1, 1 - par)
                        if h == 2 and finish:
                            combine(n - 1, 1 - par)
                        if h == 4 and front:
                            weights(n + 1, 1 - par)
                        if h == 6 and finish:
                            update(n - 1)

                top8(0, 0)
                weights(0, 0)
                tile(0, 0, finish=False)
                with dve.Fori(0, NT // 2 - 1) as i:
                    tile(2 * i + 1, 1)
                    tile(2 * i + 2, 0)
                tile(NT - 1, 1, front=False)
                combine(NT - 1, 1)
                update(NT - 1)

            if STOP > 0:
                setup()
                for k in range(min(STOP, STAGES)):
                    prep(k)
                    if k in (0, 2):
                        ffn(ff, k // 2)
                    if k == 1:
                        l0(L0)
                    if k == 4:
                        l1(L1)
                    if k in (3, 5):
                        product_keys(pk, (k - 3) // 2)

        @block.scalar
        def _(act):
            def prep(k):
                s, base = pr, k * NG
                act.wait_ge(s["ve"], k + 1)
                nc.scalar.activation(stdev[:, :], vareps[:, :], ACT.Sqrt).then_inc(s["sd"], 1)
                with act.Fori(0, NG // 2) as i:
                    for par in range(2):
                        n = 2 * i + par
                        act.wait_ge(s["tr"], base + n + 3)
                        nc.scalar.activation(xT[:, bass.ds(n * GW, GW)], bank[6 + par][:, :],
                                             ACT.Copy).then_inc(s["ev"], 1)

            def ffn(s, f):
                base = f * NG
                with act.Fori(0, NG // 2) as i:
                    for par in range(2):
                        g = 2 * i + par
                        act.wait_ge(s["s"], base + g + 1)
                        act.wait_ge(s["o"], base + g + 1)
                        for j in range(NJ):
                            nc.scalar.activation(h_ff[:, par, j, :], bank[2 + par][:, :], ACT.Relu,
                                                 bias=b1e[:, j:j + 1], scale=w1c[:, j:j + 1]).then_inc(s["h"], 1)

            def l0(s):
                act.wait_ge(s_set, 14)
                with act.Fori(0, NP_) as u:
                    act.wait_ge(s["cent"], u + 1)
                    nc.scalar.activation(sq0, qc0, ACT.Square).then_inc(s["sq"], 1)
                    act.wait_ge(s["var"], u + 1)
                    nc.scalar.activation(sd0, var0, ACT.Sqrt).then_inc(s["sd"], 1)
                    act.wait_ge(s["qt"], u + 1)
                    act.wait_ge(s["qT"], u + 1)
                    for q in range(4):
                        nc.scalar.activation(kT0[:, q], bank[6][:, 2 * P:4 * P].rearrange("p (t q) -> p t q", q=P),
                                             ACT.Identity, bias=bk4[:, q:q + 1], scale=gk[:, q:q + 1]).then_inc(s["kT"], 1)
                    for g in range(4):
                        act.wait_ge(s["sub"], 4 * u + g + 1)
                        nc.scalar.activation(E0[:, g, :], E0[:, g, :], ACT.Exp).then_inc(s["ex"], 1)
                    for g in range(4):
                        act.wait_ge(s["pt"], 4 * u + g + 1)
                        nc.scalar.activation(PT0[:, 4 * g:4 * g + 4, :].rearrange("p a b -> p (a b)"),
                                             bank[4 if g % 2 else 6][:, :], ACT.Copy).then_inc(s["pe"], 1)
                    act.wait_ge(s["ot"], u + 1)
                    nc.scalar.activation(oT0.rearrange("p a b -> p (a b)"), bank[6][:, 0:2 * P],
                                         ACT.Copy).then_inc(s["oe"], 1)

            def l1(s):
                with act.Fori(0, NP_ // 2) as i:
                    for par in range(2):
                        act.wait_ge(s["pq"], 2 * i + par + 1)
                        act.wait_ge(s["sq_used"], 2 * i + par + 1)
                        nc.scalar.activation(sq1[:, par, :], bank[par][:, 0:SEQ], ACT.Square,
                                             bias=bqc[:, 0:1]).then_inc(s["psq"], 1)
                act.wait_ge(s_set, 14)
                with act.Fori(0, NP_) as b:
                    act.wait_ge(s["qT"], b + 1)
                    for q in range(4):
                        nc.scalar.activation(kT1[:, q, :], bank[4][:, SEQ:2 * SEQ], ACT.Identity,
                                             bias=bkm[:, q:q + 1], scale=hmask[:, q:q + 1]).then_inc(s["kT"], 1)
                    for step in range(4):
                        for g in range(4):
                            act.wait_ge(s["mx"], 16 * b + 4 * step + g + 1)
                            for q in range(2):
                                nc.scalar.activation(E1[:, 2 * g + q, :], bank[g][:, q * SEQ:(q + 1) * SEQ], ACT.Exp,
                                                     bias=mx1[:, 2 * g + q:2 * g + q + 1]).then_inc(s["ex"], 1)
                    act.wait_ge(s["ot"], b + 1)
                    nc.scalar.activation(oT1.rearrange("p a b -> p (a b)"), bank[6][:, 0:2 * P],
                                         ACT.Copy).then_inc(s["oe"], 1)

            def product_keys(s, f):
                base = f * NT
                act.wait_ge(s["bve"], f + 1)
                nc.scalar.activation(bnsd, bnve, ACT.Sqrt).then_inc(s["bsd"], 1)

                def slots(m, par):
                    act.wait_ge(s["sim"], base + m + 1)
                    act.sem_inc(s_go, 1)
                    nc.scalar.activation(zT[:, par, :], xT[:, bass.ds(m * P, P)], ACT.Identity, bias=bnb[:, 0:1],
                                         scale=bna[:, 0:1]).then_inc(s["zt"], 1)
                    act.wait_ge(s["o"], 2 * (base + m) + 2)
                    act.sem_inc(s_go, 1)
                    nc.scalar.activation(yT[:, par, :], xT[:, bass.ds(m * P, P)], ACT.Copy).then_inc(s["zt"], 1)

                def exponentials(m, par):
                    act.wait_ge(s["sub"], 2 * (base + m + 1))
                    nc.scalar.activation(E5[:, par, :], E5[:, par, :], ACT.Exp).then_inc(s["ex"], 1)

                def evacuate(m):
                    for half in range(2):
                        act.wait_ge(s["ct"], 2 * (base + m) + half + 1)
                        nc.scalar.activation(cgT[:, half * 512:(half + 1) * 512], bank[6][:, :],
                                             ACT.Copy).then_inc(s["ce"], 1)

                def tile(n, par, front=True, finish=True, ahead=True):
                    if front:
                        exponentials(n + 1, 1 - par)
                    if finish:
                        evacuate(n - 1)
                    for half in range(2):
                        act.wait_ge(s["o"], 2 * (base + n) + half + 5)
                        nc.scalar.activation(G5[:, par, half * 512:(half + 1) * 512], bank[1][:, :],
                                             ACT.Gelu).then_inc(s["g"], 1)
                    if ahead:
                        slots(n + 2, par)

                act.wait_ge(s["bsc"], 2 * f + 2)
                slots(0, 0)
                slots(1, 1)
                exponentials(0, 0)
                tile(0, 0, finish=False)
                with act.Fori(0, NT // 2 - 2) as i:
                    tile(2 * i + 1, 1)
                    tile(2 * i + 2, 0)
                tile(NT - 3, 1)
                tile(NT - 2, 0, ahead=False)
                tile(NT - 1, 1, front=False, ahead=False)
                evacuate(NT - 1)

            act.sem_inc(pr["ev"], 2)
            act.sem_inc(pk["ce"], 2)
            act.sem_inc(L1["ex"], 1)
            for k in range(min(STOP, STAGES)):
                prep(k)
                if k == 0:
                    act.wait_ge(s_set, 2)
                if k in (0, 2):
                    ffn(ff, k // 2)
                if k == 1:
                    l0(L0)
                if k == 4:
                    l1(L1)
                if k in (3, 5):
                    product_keys(pk, (k - 3) // 2)

        @block.tensor
        def _(pe):
            def setup():
                pe.wait_ge(s_w, 16 * NW)
                pe.wait_ge(s_set, 3)
                nc.tensor.matmul(bank[0][:, 0:D], b2r[:, :], wout2[0:M_FF, :], start=True,
                                 stop=True).then_inc(s_ps, 1)
                for i in range(4):
                    c = slice(i * P, (i + 1) * P)
                    nc.tensor.transpose(bank[1][:, c], w1nat[:, i, :], ident[:, :])
                    nc.tensor.transpose(bank[2][:, c], keysn[:, i, :], ident[:, :])
                    nc.tensor.transpose(bank[3][:, c], kinn[:, i, :], ident[:, :])
                    last = nc.tensor.transpose(bank[4][:, c], kinn[:, 4 + i, :], ident[:, :])
                last.then_inc(s_ps, 1)
                pe.wait_ge(s_set, 18)
                kv = keysT.rearrange("p (h k q) -> p q h k", h=PH, q=2)
                for q in range(2):
                    for h in range(PH):
                        c = q * PH + h
                        last = nc.tensor.matmul(bank[5][:, c * NK:(c + 1) * NK], wqn[:, c, :], kv[:, q, h, :],
                                                start=True, stop=True)
                last.then_inc(s_ps, 1)

            def prep(k):
                s, base = pr, k * NG
                if k:
                    pe.wait_ge(*last_x[k])
                with pe.Fori(0, NG // 2) as i:
                    for par in range(2):
                        n = 2 * i + par
                        pe.wait_ge(s["xn"], base + n + 1)
                        pe.wait_ge(s["ev"], base + n + 1)
                        for t in range(GT):
                            last = nc.tensor.transpose(bank[6 + par][:, t * P:(t + 1) * P], xn[:, par, t, :],
                                                       ident[:, :])
                        last.then_inc(s["tr"], 1)
                pe.wait_ge(s["ev"], 2 + (k + 1) * NG)

            def ffn(s, f):
                base = f * NG

                def project_in(n, par):
                    nc.tensor.matmul(bank[2 + par][:, :], win2[:, :, :].rearrange("p a b -> p (a b)"),
                                     xT[:, bass.ds(n * GW, GW)], start=True, stop=True).then_inc(s["s"], 1)

                def project_out(n, par):
                    pe.wait_ge(s["h"], NJ * (base + n + 1))
                    pe.wait_ge(s["x"], base + n + 1)
                    for t in range(GT):
                        for j in range(NJ):
                            last = nc.tensor.matmul(bank[4 + par][:, t * P:(t + 1) * P],
                                                    h_ff[:, par, j, t * P:(t + 1) * P], w2o[:, j, :],
                                                    start=(j == 0), stop=(j == NJ - 1))
                    last.then_inc(s["o"], 1)

                project_in(0, 0)
                project_in(1, 1)
                project_out(0, 0)
                with pe.Fori(1, NG // 2) as i:
                    project_in(2 * i, 0)
                    project_out(2 * i - 1, 1)
                    project_in(2 * i + 1, 1)
                    project_out(2 * i, 0)
                project_out(NG - 1, 1)

            def l0(s):
                with pe.Fori(0, NP_) as u:
                    pe.wait_ge(s["xs"], u + 1)
                    for t in range(2):
                        last = nc.tensor.matmul(bank[4][:, t * 2 * D:(t + 1) * 2 * D], xs0[:, t * P:(t + 1) * P],
                                                wqkv[:, 0:2 * D], start=True, stop=True)
                    last.then_inc(s["qk"], 1)
                    for w in range(4):
                        for r in range(2):
                            last = nc.tensor.matmul(bank[5][r * WIN:(r + 1) * WIN, w * D:(w + 1) * D],
                                                    xs0[:, w * WIN:(w + 1) * WIN], wqkv[:, 2 * D:3 * D],
                                                    start=True, stop=True)
                    last.then_inc(s["v"], 1)
                    pe.wait_ge(s["qn"], u + 1)
                    for t in range(2):
                        for j in range(2):
                            last = nc.tensor.transpose(bank[6][:, (2 * j + t) * P:(2 * j + t + 1) * P],
                                                       qn0[:, 2 * t + j, :], ident[:, :])
                    last.then_inc(s["qt"], 1)
                    pe.wait_ge(s["qT"], u + 1)
                    pe.wait_ge(s["kT"], 4 * u + 4)
                    for g in range(4):
                        rows = slice(32 * g, 32 * g + 32)
                        for w in range(4):
                            t, half = w // 2, w % 2
                            keys = slice(half * WIN, (half + 1) * WIN)
                            last = nc.tensor.matmul(bank[g][half * WIN:(half + 1) * WIN, t * 256:(t + 1) * 256],
                                                    qT0[rows, t, keys], kT0[rows, :, t, keys], start=True, stop=True)
                        last.then_inc(s["st"], 1)
                    for g in range(4):
                        pe.wait_ge(s["ex"], 4 * u + g + 1)
                        if g >= 2:
                            pe.wait_ge(s["pe"], 4 * u + g - 1)
                        for j in range(4):
                            last = nc.tensor.transpose(bank[4 if g % 2 else 6][:, j * P:(j + 1) * P],
                                                       E0[:, g, j * P:(j + 1) * P], ident[:, :])
                        last.then_inc(s["pt"], 1)
                    pe.wait_ge(s["pe"], 4 * u + 4)
                    pe.wait_ge(s["vb"], 1 + u + 1)
                    vb = Vb0.rearrange("p (w c) r e -> p w c (r e)", w=4)
                    for w in range(4):
                        t, half = w // 2, w % 2
                        for g in range(4):
                            for sp in range(2):
                                c = 2 * g + sp
                                last = nc.tensor.matmul(bank[7][half * WIN:(half + 1) * WIN,
                                                                t * 144 + c * 18:t * 144 + (c + 1) * 18],
                                                        PT0[:, 4 * g + 2 * t + sp, half * WIN:(half + 1) * WIN],
                                                        vb[:, w, c, :], start=True, stop=True)
                    last.then_inc(s["pv"], 1)
                    pe.wait_ge(s["on"], u + 1)
                    for t in range(2):
                        last = nc.tensor.transpose(bank[6][:, t * P:(t + 1) * P], on0[:, t, :], ident[:, :])
                    last.then_inc(s["ot"], 1)
                    pe.wait_ge(s["oe"], u + 1)
                    for t in range(2):
                        last = nc.tensor.matmul(bank[5][:, t * D:(t + 1) * D], oT0[:, t, :], wproj[:, :],
                                                start=True, stop=True)
                    last.then_inc(s["y"], 1)

            def l1(s):
                pe.wait_ge(s_set, 17)
                for half in range(2):
                    for b in range(8):
                        n = half * 8 + b
                        par = n % 2
                        if n >= 2:
                            pe.wait_ge(s["psq"], n - 1)
                        nc.tensor.matmul(bank[par][:, 0:SEQ], w1T[:, 0, :], xT[:, n * SEQ:(n + 1) * SEQ],
                                         start=True, stop=True).then_inc(s["pq"], 1)
                        if b >= 1:
                            pe.wait_ge(s["psq"], n)
                            nc.tensor.matmul(bank[2 + half][:, 0:SEQ], headsel[:, b - 1, :], sq1[:, 1 - par, :],
                                             start=(b == 1), stop=False).then_inc(s["sq_used"], 1)
                    pe.wait_ge(s["psq"], half * 8 + 8)
                    nc.tensor.matmul(bank[2 + half][:, 0:SEQ], headsel[:, 7, :], sq1[:, 1, :], start=False,
                                     stop=True).then_inc(s["sq_used"], 1)
                    pe.wait_ge(s["sq_used"], 2 + half * 8 + 8)
                    pe.sem_inc(s["pn"], 1)
                pe.wait_ge(s["selT"], 2)
                for c in range(2):
                    for half in range(2):
                        last = nc.tensor.transpose(bank[4][:, (2 * c + half) * P:(2 * c + half + 1) * P],
                                                   selT[:, half, c * P:(c + 1) * P], ident[:, :])
                last.then_inc(s["str"], 1)
                pe.wait_ge(s["sel"], 1)
                with pe.Fori(0, NP_) as b:
                    pe.wait_ge(s["xs"], b + 1)
                    nc.tensor.matmul(bank[4][:, 0:SEQ], w1T[:, 0, :], xs1, start=True, stop=True)
                    nc.tensor.matmul(bank[4][:, SEQ:2 * SEQ], w1T[:, 1, :], xs1, start=True, stop=True).then_inc(s["qk"], 1)
                    for c in range(2):
                        last = nc.tensor.matmul(bank[5][:, c * D:(c + 1) * D], xs1[:, c * P:(c + 1) * P], w1T[:, 2, :],
                                                start=True, stop=True)
                    last.then_inc(s["v"], 1)
                    pe.wait_ge(s["qT"], b + 1)
                    pe.wait_ge(s["kT"], 4 * b + 4)
                    for step in range(4):
                        c, sp = step // 2, step % 2
                        for g in range(4):
                            rows = slice(32 * g, 32 * g + 32)
                            pe.wait_ge(s["ex"], 32 * b + 8 * step + 1)
                            nc.tensor.matmul(bank[g][:, :], qT1[rows, c * P:(c + 1) * P],
                                             kT1[rows, 2 * sp:2 * sp + 2, :], start=True, stop=True).then_inc(s["st"], 1)
                        for g in range(4):
                            pe.wait_ge(s["ex"], 32 * b + 8 * step + 2 * g + 3)
                            pe.wait_ge(s["pe"], 16 * b + 4 * step + max(0, g - 1) + 1)
                            for q in range(2):
                                for kc in range(2):
                                    last = nc.tensor.transpose(bank[6 if g % 2 else 4][:, (2 * q + kc) * P:(2 * q + kc + 1) * P],
                                                               E1[:, 2 * g + q, kc * P:(kc + 1) * P], ident[:, :])
                            last.then_inc(s["pt"], 1)
                        pe.wait_ge(s["vb"], 1 + b + 1)
                        for g in range(4):
                            pe.wait_ge(s["pe"], 16 * b + 4 * step + g + 2)
                            for q in range(2):
                                h = 4 * g + 2 * sp + q
                                for kc in range(2):
                                    last = nc.tensor.matmul(bank[7][:, c * 144 + h * 9:c * 144 + (h + 1) * 9],
                                                            PT1[:, 4 * g + 2 * q + kc, :], Vs1[:, kc, h, :],
                                                            start=(kc == 0), stop=(kc == 1))
                        last.then_inc(s["pv"], 1)
                    pe.wait_ge(s["on"], b + 1)
                    for t in range(2):
                        last = nc.tensor.transpose(bank[6][:, t * P:(t + 1) * P], on1[:, t, :], ident[:, :])
                    last.then_inc(s["ot"], 1)
                    pe.wait_ge(s["oe"], b + 1)
                    pe.wait_ge(s["cb"], NG)
                    for t in range(2):
                        last = nc.tensor.matmul(bank[5][:, t * D:(t + 1) * D], oT1[:, t, :], w1T[:, 3, :],
                                                start=True, stop=True)
                    last.then_inc(s["y"], 1)

            def product_keys(s, f):
                base = f * NT

                def similarities(m, par):
                    pe.wait_ge(s["zt"], 2 * (base + m) + 1)
                    pe.wait_ge(s["sub"], 2 * (base + m))
                    nc.tensor.matmul(bank[0][:, :], zT[:, par, :], weff[:, :, :, :].rearrange("p a b c -> p (a b c)"),
                                     start=True, stop=True).then_inc(s["sim"], 1)

                def experts(m, par, half):
                    pe.wait_ge(s["zt"], 2 * (base + m) + 2)
                    pe.wait_ge(s["g"], 2 * (base + m) + half)
                    nc.tensor.matmul(bank[1][:, :], yT[:, par, :], kinT[:, half * 512:(half + 1) * 512],
                                     start=True, stop=True).then_inc(s["o"], 1)

                def add_unit(n, par, at):
                    h = UNITS[at]
                    if h in MERGED:
                        pe.wait_ge(s["ys"], len(MERGED) * (base + n) + MERGED.index(h) + 2)
                    else:
                        pe.wait_ge(s["M"], 8 * (base + n) + h + 9)
                    for half in range(2):
                        last = nc.tensor.matmul(bank[2 + 2 * par + half][:, :], ident[:, :],
                                                Mm[:, h % NMS, half * 512:(half + 1) * 512], start=(at == 0),
                                                stop=(at == NU - 1))
                    last.then_inc(s["acc"], 1)

                def turn(m, half):
                    pe.wait_ge(s["cg"], 2 * (base + m) + half + 1)
                    pe.wait_ge(s["ce"], 2 * (base + m) + half + 2)
                    for j in range(4):
                        c = half * 512 + j * P
                        last = nc.tensor.transpose(bank[6][:, j * P:(j + 1) * P], cg[:, c:c + P], ident[:, :])
                    last.then_inc(s["ct"], 1)

                def outputs(m):
                    pe.wait_ge(s["ce"], 2 * (base + m) + 4)
                    pe.wait_ge(s["x"], base + m + 1)
                    for c in range(NCH):
                        last = nc.tensor.matmul(bank[7][:, 0:D], cgT[:, c * P:(c + 1) * P], kout[:, c, :],
                                                start=(c == 0), stop=(c == NCH - 1))
                    last.then_inc(s["y"], 1)

                def tile(n, par, front=True, finish=True):
                    if front:
                        similarities(n + 1, 1 - par)
                    add_unit(n, par, 0)
                    add_unit(n, par, 1)
                    add_unit(n, par, 2)
                    if finish:
                        turn(n - 1, 0)
                    add_unit(n, par, 3)
                    if finish:
                        turn(n - 1, 1)
                    add_unit(n, par, 4)
                    if finish:
                        outputs(n - 1)
                    experts(n, par, 0)
                    for at in range(5, NU):
                        add_unit(n, par, at)
                    experts(n, par, 1)

                similarities(0, 0)
                tile(0, 0, finish=False)
                with pe.Fori(0, NT // 2 - 1) as i:
                    tile(2 * i + 1, 1)
                    tile(2 * i + 2, 0)
                tile(NT - 1, 1, front=False)
                turn(NT - 1, 0)
                turn(NT - 1, 1)
                outputs(NT - 1)

            pe.sem_inc(pr["tr"], 2)
            pe.sem_inc(ff["o"], 2)
            pe.sem_inc(L1["sq_used"], 2)
            pe.sem_inc(pk["sim"], 2)
            pe.sem_inc(pk["o"], 4)
            pe.sem_inc(pk["acc"], NU)
            if STOP > 0:
                setup()
                for k in range(min(STOP, STAGES)):
                    prep(k)
                    if k in (0, 2):
                        if k == 0:
                            pe.wait_ge(s_set, 11)
                        ffn(ff, k // 2)
                    if k == 1:
                        l0(L0)
                    if k == 4:
                        l1(L1)
                    if k in (3, 5):
                        product_keys(pk, (k - 3) // 2)


_INS = ['L0_attn_x', 'L0_attn_W_qkv', 'L0_attn_ln_gamma', 'L0_attn_ln_beta', 'L0_attn_W_proj', 'L0_attn_b_proj',
        'L0_ffn_Win', 'L0_ffn_bin_', 'L0_ffn_W1', 'L0_ffn_b1', 'L0_ffn_W2', 'L0_ffn_b2', 'L0_ffn_Wout', 'L0_ffn_bout',
        'L1_attn_Wq', 'L1_attn_bq', 'L1_attn_Wk', 'L1_attn_bk', 'L1_attn_Wv', 'L1_attn_bv', 'L1_attn_Wo',
        'L1_attn_bo', 'L1_ffn_gamma', 'L1_ffn_beta', 'L1_ffn_w_q', 'L1_ffn_keys', 'L1_ffn_key_in', 'L1_ffn_key_out']


def constants():
    p = np.arange(P)
    head = p // HD
    c = {"c_ident": np.eye(P, dtype=np.float32)}
    c["c_hmask"] = (head[:, None] % 4 == np.arange(4)[None]).astype(np.float32)
    c["c_vmask"] = (p[:, None] // WIN == np.arange(2)[None]).astype(np.float32)
    c["c_headsel"] = (16 * np.arange(8)[None, :, None] + head[:, None, None] == p[None, None, :]).astype(np.float32)
    return c


def kernel(**inputs):
    import concourse.bacc as _bacc
    from concourse import mybir as _mybir
    from concourse.bass_utils import run_bass_kernel_spmd as _run

    nc = _bacc.Bacc("TRN2", target_bir_lowering=False, num_devices=1)
    arrays, args = {}, {}
    named = {name: np.ascontiguousarray(inputs[name]) for name in _INS}
    named.update(constants())
    for name, a in named.items():
        arrays[f"in_{name}_dram"] = a
        args[name] = nc.dram_tensor(f"in_{name}_dram", a.shape, _mybir.dt.from_np(a.dtype), kind="ExternalInput").ap()
    out = nc.dram_tensor("out_0_dram", (BATCH, SEQ, D), _mybir.dt.float32, kind="ExternalOutput").ap()
    build(nc, args, out)
    r = _run(nc, [arrays], core_ids=[0])
    return r.results[0]["out_0_dram"]
```

```python
import concourse.bass as bass
from concourse import mybir
from contextlib import ExitStack

import numpy as np

P = 128
D = 128
BATCH, SEQ = 16, 256
T = BATCH * SEQ
NT = T // P
HEADS, HD = 16, 8
WIN = 64
GT = 4
NG = NT // GT
GW = GT * P
NP_ = NT // 2
M_FF, INNER = 64, 16
NJ = INNER // 2
TOP_U = SEQ // 5
PH, NK, KD, TOPK = 8, 32, 128, 8
NE = NK * NK
NCH = NE // P
LN_EPS = 1e-5
STAGES = 6
JPE = 3
STOP = 6


def build(nc, A, out):
    fp32 = mybir.dt.float32
    ALU = mybir.AluOpType
    ACT = mybir.ActivationFunctionType
    X = mybir.AxisListType.X

    ctx = ExitStack()
    with ctx:
        def sb(name, shape):
            return ctx.enter_context(nc.sbuf_tensor(name, shape, fp32))

        def sem(name):
            return ctx.enter_context(nc.semaphore(name))

        def sems(stage, names):
            return {n: sem(f"{stage}_{n}") for n in names.split()}

        x_sb = sb("x_sb", [P, NT, D])
        xT = sb("xT", [P, T])
        ident = sb("ident", [P, P])
        hmask = sb("hmask", [P, HEADS])
        vmask = sb("vmask", [P, 2])
        headsel = sb("headsel", [P, 8, P])
        stats = sb("stats", [P, NT, 6])
        mdiff = sb("mdiff", [P, NT])
        negmean = sb("negmean", [P, NT])
        vareps = sb("vareps", [P, NT])
        stdev = sb("stdev", [P, NT])
        rstd = sb("rstd", [P, NT])
        xn = sb("xn", [P, 2, GT, D])
        win2 = sb("win2", [P, 2, M_FF])
        bin2 = sb("bin2", [P, 1])
        w1c = sb("w1c", [P, NJ])
        b1c = sb("b1c", [P, NJ])
        b1e = sb("b1e", [P, NJ])
        w2c = sb("w2c", [P, NJ])
        b2c = sb("b2c", [M_FF, 1])
        b2r = sb("b2r", [M_FF, P])
        wout2 = sb("wout2", [P, D])
        w2o = sb("w2o", [P, JPE, D])
        bout_bc = sb("bout_bc", [P, D])
        ffn_add = sb("ffn_add", [P, D])
        wqkv = sb("wqkv", [P, 3 * D])
        wproj = sb("wproj", [P, D])
        bproj_bc = sb("bproj_bc", [P, D])
        gcol = sb("gcol", [P, 1])
        bcol = sb("bcol", [P, 1])
        gk = sb("gk", [P, HEADS])
        bk16 = sb("bk16", [P, HEADS])
        w1nat = sb("w1nat", [P, 4, D])
        w1T = sb("w1T", [P, 4, D])
        bqc = sb("bqc", [P, 1])
        bkc = sb("bkc", [P, 1])
        bkm = sb("bkm", [P, HEADS])
        bv_bc = sb("bv_bc", [P, D])
        bo_bc = sb("bo_bc", [P, D])
        weff = sb("weff", [P, 2, PH, NK])
        kinT = sb("kinT", [P, NE])
        kout = sb("kout", [P, NCH, D])
        pg = sb("pg", [P, 1])
        pb_ = sb("pb_", [P, 1])
        work = sb("work", [P, 26000])

        def cut(at, *shape):
            n = int(np.prod(shape))
            v = work[:, at:at + n]
            if len(shape) == 2:
                v = v.rearrange("p (a b) -> p a b", b=shape[1])
            if len(shape) == 3:
                v = v.rearrange("p (a b c) -> p a b c", b=shape[1], c=shape[2])
            if len(shape) == 4:
                v = v.rearrange("p (a b c d) -> p a b c d", b=shape[1], c=shape[2], d=shape[3])
            return v, at + n

        bank = [ctx.enter_context(nc.psum_tensor(f"bank{i}", [P, 512], fp32)) for i in range(8)]

        s_x = sem("s_x")
        s_id = sem("s_id")
        s_wf = sem("s_wf")
        s_w = sem("s_w")
        s_out = sem("s_out")
        s_go = sem("s_go")
        s_set = sem("s_set")
        s_setp = sem("s_setp")
        s_ps = sem("s_ps")
        pr = sems("pr", "stat aggr nm ve sd rstd xn tr ev sq")
        ff = sems("ff", "s h hs o cb x")
        L0 = sems("l0", "kM xs qk v cent sq rsum var sd rs qn qt qT kT st mx sub ex pt pe pv vb rec on ot oe y cb x")
        L1 = sems("l1", "kM sq_used pq psq pn nc mr selT str sel xs qk v qT kT vb st mx ex pt pe pv rec on ot oe y cb x")
        pk = sems("pk", "bst bag bve bsd brs bsc zt sim m8 sub ex cand c8 z rz sc P A M acc cg o g y x ys")
        last_x = {0: (s_x, 16 * NG)}
        last_x[1] = (ff["x"], 2 + NG)
        last_x[2] = (L0["x"], NP_)
        last_x[3] = (ff["x"], 2 + 2 * NG)
        last_x[4] = (pk["x"], 1 + NT)
        last_x[5] = (L1["x"], NP_)
        last_x[6] = (pk["x"], 1 + 2 * NT)

        h_ff, o = cut(0, 2, NJ, GW)
        hsum, _ = cut(o, 2, GW)
        xs0, o = cut(0, 2, 2 * P)
        qc0, o = cut(o, 512)
        sq0, o = cut(o, 512)
        qn0, o = cut(o, 4, P)
        qT0, o = cut(o, 2, 2 * P)
        kR0, o = cut(o, 2 * P)
        kM0, o = cut(o, 2 * HEADS, 2 * P)
        E0, o = cut(o, 2, 2, 512)
        PT0, o = cut(o, 16, P)
        Vb0, o = cut(o, 2, 32, 2, 9)
        on0, o = cut(o, 2, P)
        oT0, o = cut(o, 2 * P)
        sum0, o = cut(o, 64)
        var0, o = cut(o, 64)
        sd0, o = cut(o, 64)
        rs0, o = cut(o, 64)
        mx0, o = cut(o, 4, 8)
        rec0, o = cut(o, 2, 16)
        assert o <= 20000, o
        sq1, o = cut(0, 2, SEQ)
        n2, o = cut(o, 2, SEQ)
        n2w, o = cut(o, 2, SEQ)
        m8, o = cut(o, 2, 8)
        selT, o = cut(o, 2, SEQ)
        sel, o = cut(o, 2, 2, P)
        xs1, o = cut(o, SEQ)
        qT1, o = cut(o, 2, SEQ)
        kR1, o = cut(o, SEQ)
        kM1, o = cut(o, 2 * HEADS, SEQ)
        Vs1, o = cut(o, 4, HEADS, HD + 1)
        E1, o = cut(o, 2, 4, SEQ)
        PT1, o = cut(o, 2, 8, P)
        on1, o = cut(o, 2, P)
        oT1, o = cut(o, 2, P)
        mx1, o = cut(o, 2, 4)
        rec1, o = cut(o, 2, 16)
        NPS, NMS = 4, 4
        bnst, o = cut(0, 8, 6)
        bnmv, o = cut(o, 2)
        bnve, o = cut(o, 1)
        bnsd, o = cut(o, 1)
        bnrs, o = cut(o, 1)
        bna, o = cut(o, 1)
        bnb, o = cut(o, 1)
        zT, o = cut(o, 2, P)
        E5, o = cut(o, 2, 640)
        exs, o = cut(o, 2, PH * NK)
        m8raw, o = cut(o, 16, 8)
        cand, o = cut(o, PH, 20)
        c8, o = cut(o, PH, 8)
        zsum, o = cut(o, PH)
        rz, o = cut(o, PH)
        thr, o = cut(o, 2, PH)
        Pm, o = cut(o, NPS, NE)
        Mm, o = cut(o, NMS, NE)
        G5, o = cut(o, 2, NE)
        cg, o = cut(o, NE)
        assert o <= 26000, o
        POOL_HEADS = list(range(8))
        DVE_HEADS = [h for h in range(PH) if h not in POOL_HEADS]
        MERGED = [7]
        UNITS = [h for h in range(PH) if h + 1 not in MERGED]
        NU = len(UNITS)
        OUT_AT = 3

        def grid(buf, slot):
            return buf[:, slot, :].rearrange("p (i j) -> p i j", j=NK)

        def ex_rows(par, h):
            return exs[:, par, h * NK:(h + 1) * NK].unsqueeze(2).to_broadcast([P, NK, NK])

        def ey_cols(par, h):
            at = (PH + h) * NK
            return E5[:, par, at:at + NK].unsqueeze(1).to_broadcast([P, NK, NK])

        keysn, o = cut(20000, 4, P)
        keysT, o = cut(o, 512)
        wqn, o = cut(o, 16, P)
        kinn, o = cut(o, NCH, P)

        block = ctx.enter_context(nc.Block())

        NWF, NW = 14, 22
        SET_W2O = 3 + JPE
        SET_FFN = SET_W2O + 2
        SET_W1T = SET_FFN + 4
        SET_KEYS = SET_W1T + 1
        SET_ALL = SET_KEYS + 3

        @block.sync
        def _(sp):
            xv = A["L0_attn_x"].rearrange("b (c p) d -> p (b c) d", p=P)

            def load_ffn(dst, src):
                sp.dma_start(dst, src).then_inc(s_wf, 16)

            def load(dst, src):
                sp.dma_start(dst, src).then_inc(s_w, 16)

            for g in range(NG):
                sp.dma_start(x_sb[:, g * GT:(g + 1) * GT, :], xv[:, g * GT:(g + 1) * GT, :]).then_inc(s_x, 16)
            sp.dma_start(ident[:, :], A["c_ident"]).then_inc(s_id, 16)
            for r in range(2):
                half = slice(r * M_FF, (r + 1) * M_FF)
                load_ffn(win2[:, r, :], A["L0_ffn_Win"])
                load_ffn(bin2[half, :], A["L0_ffn_bin_"].rearrange("(m o) -> m o", o=1))
                load_ffn(w1c[half, :], A["L0_ffn_W1"].rearrange("m (r j) -> r m j", r=2)[r])
                load_ffn(b1c[half, :], A["L0_ffn_b1"].rearrange("m (r j) -> r m j", r=2)[r])
                load_ffn(w2c[half, :], A["L0_ffn_W2"].rearrange("m (r j) -> r m j", r=2)[r])
                load_ffn(wout2[half, :], A["L0_ffn_Wout"])
            load_ffn(b2c[:, :], A["L0_ffn_b2"].rearrange("(m o) -> m o", o=1))
            load_ffn(bout_bc[:, :], A["L0_ffn_bout"].rearrange("(o d) -> o d", o=1).to_broadcast([P, D]))
            for dst, name in ((bproj_bc, "L0_attn_b_proj"), (bv_bc, "L1_attn_bv"), (bo_bc, "L1_attn_bo")):
                load(dst[:, :], A[name].rearrange("(o d) -> o d", o=1).to_broadcast([P, D]))
            load(hmask[:, :], A["c_hmask"])
            load(vmask[:, :], A["c_vmask"])
            load(headsel[:, :, :], A["c_headsel"])
            load(wqkv[:, :], A["L0_attn_W_qkv"])
            load(wproj[:, :], A["L0_attn_W_proj"])
            for dst, name in ((gcol, "L0_attn_ln_gamma"), (bcol, "L0_attn_ln_beta")):
                load(dst[:, :], A[name].rearrange("(o d e) -> o d e", o=1, e=1).to_broadcast([HEADS, HD, 1]))
            for i, name in enumerate(("Wq", "Wk", "Wv", "Wo")):
                load(w1nat[:, i, :], A[f"L1_attn_{name}"])
            load(bqc[:, :], A["L1_attn_bq"].rearrange("(m o) -> m o", o=1))
            load(bkc[:, :], A["L1_attn_bk"].rearrange("(m o) -> m o", o=1))
            load(pg[:, :], A["L1_ffn_gamma"].rearrange("(m o) -> m o", o=1))
            load(pb_[:, :], A["L1_ffn_beta"].rearrange("(m o) -> m o", o=1))
            load(keysn, A["L1_ffn_keys"].rearrange("h k p d -> (h k p) d").rearrange("(c q) d -> q c d", q=P))
            load(wqn, A["L1_ffn_w_q"].rearrange("(c q) d -> q c d", q=P))
            load(kinn, A["L1_ffn_key_in"].rearrange("(c q) d -> q c d", q=P))
            load(kout[:, :, :], A["L1_ffn_key_out"].rearrange("(c q) d -> q c d", q=P))
            ov = out.rearrange("b (c p) d -> p (b c) d", p=P)
            sp.wait_ge(*last_x[STOP])
            for g in range(4):
                sp.dma_start(ov[:, g * 8:(g + 1) * 8, :], x_sb[:, g * 8:(g + 1) * 8, :]).then_inc(s_out, 16)
            sp.wait_ge(s_out, 64)


        @block.gpsimd
        def _(pool):
            def add_row(row, done):
                with pool.Fori(0, NG) as g:
                    xg = x_sb[:, bass.ds(g * GT, GT), :]
                    nc.gpsimd.tensor_tensor(xg, xg, row[:, :].unsqueeze(1).to_broadcast([P, GT, D]),
                                            ALU.add).then_inc(done, 1)

            def head_keys_0(s):
                def pair(u, par):
                    pool.wait_ge(s["kT"], u + 1)
                    pool.sem_inc(s_go, 1)
                    for h in range(HEADS):
                        last = nc.gpsimd.tensor_scalar(kM0[:, HEADS * par + h, :], kR0, gk[:, h:h + 1],
                                                       bk16[:, h:h + 1], ALU.mult, ALU.add)
                    last.then_inc(s["kM"], 1)

                def slot(u, par):
                    if not (isinstance(u, int) and u < 2):
                        pool.wait_ge(s["v"], u - 1)
                    nc.gpsimd.tensor_copy(xs0[:, par, :], xT[:, bass.ds(u * SEQ, SEQ)]).then_inc(s["xs"], 1)

                slot(0, 0)
                slot(1, 1)
                pair(0, 0)
                slot(2, 0)
                with pool.Fori(0, NP_ // 2 - 2) as i:
                    pair(2 * i + 1, 1)
                    slot(2 * i + 3, 1)
                    pair(2 * i + 2, 0)
                    slot(2 * i + 4, 0)
                pair(NP_ - 3, 1)
                slot(NP_ - 1, 1)
                pair(NP_ - 2, 0)
                pair(NP_ - 1, 1)

            def head_keys(s):
                def sequence(b, par):
                    pool.wait_ge(s["kT"], b + 1)
                    pool.sem_inc(s_go, 1)
                    for h in range(HEADS):
                        last = nc.gpsimd.tensor_scalar(kM1[:, HEADS * par + h, :], kR1, hmask[:, h:h + 1],
                                                       bkm[:, h:h + 1], ALU.mult, ALU.add)
                    last.then_inc(s["kM"], 1)

                def values(b):
                    pool.wait_ge(s["v"], b)
                    nc.gpsimd.tensor_copy(xs1, xT[:, bass.ds(b * SEQ, SEQ)]).then_inc(s["xs"], 1)

                nc.gpsimd.tensor_copy(xs1, xT[:, 0:SEQ]).then_inc(s["xs"], 1)
                sequence(0, 0)
                values(1)
                with pool.Fori(0, NP_ // 2 - 1) as i:
                    sequence(2 * i + 1, 1)
                    values(2 * i + 2)
                    sequence(2 * i + 2, 0)
                    values(2 * i + 3)
                sequence(NP_ - 1, 1)

            def product_keys(s, f):
                base = f * NT

                def tile(n, par):
                    pool.wait_ge(s["sc"], 2 * (base + n) + 2)
                    for at, h in enumerate(POOL_HEADS):
                        pool.wait_ge(s["M"], 8 * (base + n) + h + 5)
                        nc.gpsimd.tensor_tensor(grid(Pm, h % NPS), ex_rows(par, h), ey_cols(par, h),
                                                ALU.mult).then_inc(s["P"], 1)

                tile(0, 0)
                with pool.Fori(0, NT // 2 - 1) as i:
                    tile(2 * i + 1, 1)
                    tile(2 * i + 2, 0)
                tile(NT - 1, 1)

            for k in range(STAGES):
                if k >= STOP:
                    break
                s = pr
                pool.wait_ge(s["tr"], 2 + (k + 1) * NG)
                if k == 0 or k == 2:
                    pool.wait_ge(s_set, SET_FFN)
                    add_row(ffn_add, ff["cb"])
                if k == 1:
                    pool.wait_ge(s_w, 16 * NW)
                    add_row(bproj_bc, L0["cb"])
                    pool.wait_ge(s["ev"], 2 + (k + 1) * NG)
                    head_keys_0(L0)
                if k == 4:
                    add_row(bo_bc, L1["cb"])
                    pool.wait_ge(s["ev"], 2 + (k + 1) * NG)
                    head_keys(L1)
                if k == 3 or k == 5:
                    product_keys(pk, (k - 3) // 2)


        @block.vector
        def _(dve):
            dve.sem_inc(pk["M"], 8)
            dve.sem_inc(pk["x"], 1)
            dve.sem_inc(pk["ys"], 1)
            dve.sem_inc(pk["cg"], 2)
            dve.sem_inc(ff["x"], 2)
            dve.sem_inc(L1["pe"], 2)
            dve.sem_inc(L0["sub"], 4)
            dve.sem_inc(L0["on"], 1)
            dve.sem_inc(L1["on"], 1)

            def setup_ffn():
                dve.wait_ge(s_wf, 16 * NWF)
                nc.vector.tensor_scalar(b1e[:, :], w1c[:, :], bin2[:, 0:1], None, ALU.mult).then_inc(s_set, 1)
                dve.wait_ge(s_set, 1)
                nc.vector.tensor_tensor(b1e[:, :], b1e[:, :], b1c[:, :], ALU.add).then_inc(s_set, 1)
                nc.vector.tensor_copy(b2r[:, :], b2c[:, 0:1].to_broadcast([M_FF, P])).then_inc(s_set, 1)
                for j in range(JPE):
                    nc.vector.tensor_scalar(w2o[:, j, :], wout2[:, :], w2c[:, j:j + 1], None,
                                            ALU.mult).then_inc(s_set, 1)
                dve.wait_ge(s_ps, 1)
                nc.vector.tensor_tensor(ffn_add[:, :], bank[0][:, 0:D], bout_bc[:, :], ALU.add).then_inc(s_set, 1)
                dve.wait_ge(s_set, SET_FFN - 1)
                nc.vector.tensor_scalar(ffn_add[:, :], ffn_add[:, :], 0.5, None, ALU.mult).then_inc(s_set, 1)

            def setup_rest():
                dve.wait_ge(s_w, 16 * NW)
                nc.vector.tensor_scalar(gk[:, :], hmask[:, :], gcol[:, 0:1], None, ALU.mult).then_inc(s_set, 1)
                nc.vector.tensor_scalar(bk16[:, :], hmask[:, :], bcol[:, 0:1], None, ALU.mult).then_inc(s_set, 1)
                nc.vector.tensor_scalar(bkm[:, :], hmask[:, :], bkc[:, 0:1], None, ALU.mult).then_inc(s_set, 1)
                dve.wait_ge(s_ps, 2)
                nc.vector.tensor_copy(w1T[:, :, :].rearrange("p a b -> p (a b)"), bank[1][:, :]).then_inc(s_set, 1)
                nc.vector.tensor_copy(keysT, bank[2][:, :]).then_inc(s_set, 1)
                nc.vector.tensor_copy(kinT[:, 0:512], bank[3][:, :]).then_inc(s_set, 1)
                nc.vector.tensor_copy(kinT[:, 512:1024], bank[4][:, :]).then_inc(s_set, 1)
                dve.wait_ge(s_ps, 3)
                nc.vector.tensor_copy(weff[:, :, :, :].rearrange("p a b c -> p (a b c)"),
                                      bank[5][:, :]).then_inc(s_set, 1)
                dve.wait_ge(s_set, SET_ALL)

            def prep(k):
                s, base = pr, k * NG
                dve.wait_ge(*last_x[k])
                with dve.Fori(0, NT) as n:
                    nc.vector.bn_stats(stats[:, bass.ds(n, 1), :], x_sb[:, bass.ds(n, 1), :]).then_inc(s["stat"], 1)
                dve.wait_ge(s["stat"], (k + 1) * NT)
                even, odd = stats[:, :, 1], stats[:, :, 4]
                nc.vector.tensor_tensor(negmean[:, :], even, odd, ALU.add).then_inc(s["aggr"], 1)
                nc.vector.tensor_tensor(mdiff[:, :], even, odd, ALU.subtract).then_inc(s["aggr"], 1)
                nc.vector.tensor_tensor(vareps[:, :], stats[:, :, 2], stats[:, :, 5], ALU.add).then_inc(s["aggr"], 1)
                dve.wait_ge(s["aggr"], 3 * (k + 1))
                nc.vector.tensor_scalar(negmean[:, :], negmean[:, :], -0.5, None, ALU.mult).then_inc(s["nm"], 1)
                nc.vector.scalar_tensor_tensor(mdiff[:, :], mdiff[:, :], 0.25, mdiff[:, :], ALU.mult,
                                               ALU.mult).then_inc(s["sq"], 1)
                nc.vector.tensor_scalar(vareps[:, :], vareps[:, :], 1.0 / D, LN_EPS, ALU.mult,
                                        ALU.add).then_inc(s["sq"], 1)
                dve.wait_ge(s["sq"], 2 * (k + 1))
                nc.vector.tensor_tensor(vareps[:, :], vareps[:, :], mdiff[:, :], ALU.add).then_inc(s["ve"], 1)
                dve.wait_ge(s["sd"], k + 1)
                nc.vector.reciprocal(rstd[:, :], stdev[:, :]).then_inc(s["rstd"], 1)
                dve.wait_ge(s["rstd"], k + 1)
                dve.wait_ge(s["nm"], k + 1)

                def normalise(n, par):
                    dve.wait_ge(s["tr"], base + n + 1)
                    for t in range(GT):
                        c = n * GT + t
                        last = nc.vector.tensor_scalar(xn[:, par, t, :], x_sb[:, bass.ds(c, 1), :],
                                                       negmean[:, bass.ds(c, 1)], rstd[:, bass.ds(c, 1)],
                                                       ALU.add, ALU.mult)
                    last.then_inc(s["xn"], 1)

                with dve.Fori(0, NG // 2) as i:
                    for par in range(2):
                        normalise(2 * i + par, par)

            def ffn(s, f):
                base = f * NG

                def sums(g, par):
                    if not (isinstance(g, int) and g < 2 and f == 0):
                        dve.wait_ge(s["o"], base + g + 1)
                    for i in range(NJ - JPE):
                        j = JPE + i
                        dve.wait_ge(s["h"], NJ * (base + g) + i + 1)
                        if i == 0:
                            nc.vector.tensor_scalar(hsum[:, par, :], h_ff[:, par, j, :], w2c[:, j:j + 1], None,
                                                    ALU.mult).then_inc(s["hs"], 1)
                        else:
                            dve.wait_ge(s["hs"], (NJ - JPE) * (base + g) + i)
                            nc.vector.scalar_tensor_tensor(hsum[:, par, :], h_ff[:, par, j, :], w2c[:, j:j + 1],
                                                           hsum[:, par, :], ALU.mult, ALU.add).then_inc(s["hs"], 1)

                def update(g, par):
                    dve.wait_ge(s["o"], base + g + 3)
                    dve.wait_ge(s["cb"], base + g + 1)
                    xg = x_sb[:, bass.ds(g * GT, GT), :].rearrange("p a b -> p (a b)")
                    nc.vector.scalar_tensor_tensor(xg, bank[4 + par][:, :], 0.5, xg, ALU.mult,
                                                   ALU.add).then_inc(s["x"], 1)

                sums(0, 0)
                with dve.Fori(0, NG // 2 - 1) as i:
                    sums(2 * i + 1, 1)
                    update(2 * i, 0)
                    sums(2 * i + 2, 0)
                    update(2 * i + 1, 1)
                sums(NG - 1, 1)
                update(NG - 2, 0)
                update(NG - 1, 1)

            def l0(s):
                for par in range(2):
                    last = nc.vector.tensor_copy(Vb0[:, par, :, :, HD],
                                                 vmask[:, :].unsqueeze(1).to_broadcast([P, 32, 2]))
                last.then_inc(s["vb"], 1)
                qc = qc0.rearrange("p (h d) -> p h d", d=HD)

                def centre(u):
                    dve.wait_ge(s["qk"], u + 1)
                    qk = bank[4][:, :].rearrange("p (h d) -> p h d", d=HD)
                    nc.vector.tensor_reduce(sum0, qk, X, ALU.add).then_inc(s["rsum"], 1)
                    dve.wait_ge(s["rsum"], 2 * u + 1)
                    nc.vector.scalar_tensor_tensor(qc, sum0.unsqueeze(2).to_broadcast([P, 64, HD]), -1.0 / HD, qk,
                                                   ALU.mult, ALU.add).then_inc(s["cent"], 1)

                def variance(u):
                    dve.wait_ge(s["sq"], u + 1)
                    nc.vector.tensor_reduce(var0, sq0.rearrange("p (h d) -> p h d", d=HD), X,
                                            ALU.add).then_inc(s["rsum"], 1)
                    dve.wait_ge(s["rsum"], 2 * u + 2)
                    nc.vector.tensor_scalar(var0, var0, 1.0 / HD, LN_EPS, ALU.mult, ALU.add).then_inc(s["var"], 1)

                def scale(u):
                    dve.wait_ge(s["sd"], u + 1)
                    nc.vector.reciprocal(rs0, sd0).then_inc(s["rs"], 1)
                    dve.wait_ge(s["rs"], u + 1)
                    nc.vector.tensor_tensor(qn0.rearrange("p a (h d) -> p (a h) d", d=HD), qc,
                                            rs0.unsqueeze(2).to_broadcast([P, 64, HD]), ALU.mult).then_inc(s["qn"], 1)

                def values(u, par):
                    dve.wait_ge(s["v"], u + 1)
                    vps = bank[4][:, :].rearrange("p (w r d) -> p w r d", r=2, d=HD)
                    for r in range(2):
                        last = nc.vector.tensor_scalar(Vb0[:, par, :, r, 0:HD], vps[:, :, r, :], vmask[:, r:r + 1],
                                                       None, ALU.mult)
                    last.then_inc(s["vb"], 1)

                def queries(u, par):
                    dve.wait_ge(s["qt"], u + 1)
                    nc.vector.tensor_scalar(qT0[:, par, :], bank[4][:, 0:2 * P], gcol[:, 0:1], bcol[:, 0:1], ALU.mult,
                                            ALU.add).then_inc(s["qT"], 1)

                def less_max(u, t):
                    for hh in range(2):
                        at = 4 * u + 2 * t + hh
                        dve.wait_ge(s["st"], at + 1)
                        sv = bank[2 * t + hh][:, :].rearrange("p (h k) -> p h k", k=WIN)
                        nc.vector.tensor_reduce(mx0[:, 2 * t + hh, :], sv, X, ALU.max).then_inc(s["mx"], 1)
                    for hh in range(2):
                        at = 4 * u + 2 * t + hh
                        sv = bank[2 * t + hh][:, :].rearrange("p (h k) -> p h k", k=WIN)
                        dve.wait_ge(s["mx"], at + 1)
                        if not (isinstance(u, int) and u == 0):
                            dve.wait_ge(s["pt"], at - 3)
                        nc.vector.tensor_tensor(E0[:, t, hh, :].rearrange("p (h k) -> p h k", k=WIN), sv,
                                                mx0[:, 2 * t + hh, :].unsqueeze(2).to_broadcast([P, 8, WIN]),
                                                ALU.subtract).then_inc(s["sub"], 1)

                def normalise(u):
                    dve.wait_ge(s["pv"], 2 * u + 4)
                    ov = bank[7][:, 0:288].rearrange("p (t h e) -> p t h e", t=2, e=HD + 1)
                    nc.vector.reciprocal(rec0, ov[:, :, :, HD]).then_inc(s["rec"], 1)
                    dve.wait_ge(s["rec"], u + 1)
                    for t in range(2):
                        last = nc.vector.tensor_tensor(on0[:, t, :].rearrange("p (h d) -> p h d", d=HD),
                                                       ov[:, t, :, 0:HD],
                                                       rec0[:, t, :].unsqueeze(2).to_broadcast([P, HEADS, HD]),
                                                       ALU.mult)
                    last.then_inc(s["on"], 1)

                def update(u):
                    dve.wait_ge(s["y"], u + 1)
                    xu = x_sb[:, bass.ds(2 * u, 2), :].rearrange("p a b -> p (a b)")
                    nc.vector.tensor_tensor(xu, bank[4][:, 256:512], xu, ALU.add).then_inc(s["x"], 1)

                def pair(u, par, back=True, one=True, two=True):
                    if back:
                        normalise(u - 1)
                    less_max(u, 1)
                    if back:
                        update(u - 1)
                    if two:
                        centre(u + 2)
                    if one:
                        less_max(u + 1, 0)
                    if two:
                        variance(u + 2)
                    if one:
                        values(u + 1, 1 - par)
                    if two:
                        scale(u + 2)
                        queries(u + 2, par)

                centre(0)
                variance(0)
                scale(0)
                values(0, 0)
                queries(0, 0)
                centre(1)
                variance(1)
                scale(1)
                queries(1, 1)
                less_max(0, 0)
                pair(0, 0, back=False)
                with dve.Fori(0, NP_ // 2 - 2) as i:
                    pair(2 * i + 1, 1)
                    pair(2 * i + 2, 0)
                pair(NP_ - 3, 1)
                pair(NP_ - 2, 0, two=False)
                pair(NP_ - 1, 1, one=False, two=False)
                normalise(NP_ - 1)
                update(NP_ - 1)

            def l1(s):
                for half in range(2):
                    dve.wait_ge(s["pn"], half + 1)
                    nc.vector.tensor_copy(n2[:, half, :], bank[2 + half][:, 0:SEQ]).then_inc(s["nc"], 1)
                rounds = -(-TOP_U // 8)
                for r in range(rounds):
                    for half in range(2):
                        src = n2 if r == 0 else n2w
                        dve.wait_ge(s["nc"], half + 1)
                        if r:
                            dve.wait_ge(s["mr"], 4 * r - 2 + half + 1)
                        nc.vector.max(m8[:, half, :], src[:, half, :]).then_inc(s["mr"], 1)
                    if r < rounds - 1:
                        for half in range(2):
                            dve.wait_ge(s["mr"], 4 * r + half + 1)
                            nc.vector.match_replace(n2w[:, half, :], m8[:, half, :], (n2 if r == 0 else n2w)[:, half, :],
                                                    -1.0).then_inc(s["mr"], 1)
                dve.wait_ge(s["mr"], 4 * (rounds - 1) + 2)
                rank = (TOP_U - 1) % 8
                for half in range(2):
                    nc.vector.tensor_scalar(selT[:, half, :], n2[:, half, :], m8[:, half, rank:rank + 1], None,
                                            ALU.is_ge).then_inc(s["selT"], 1)
                dve.wait_ge(s["str"], 1)
                nc.vector.tensor_copy(sel.rearrange("p a b c -> p (a b c)"), bank[4][:, :]).then_inc(s["sel"], 1)
                nc.vector.memset(Vs1[:, :, :, HD], 1.0).then_inc(s["vb"], 1)
                dve.wait_ge(s["sel"], 1)

                def project(b, par):
                    dve.wait_ge(s["qk"], b + 1)
                    nc.vector.tensor_scalar(qT1[:, par, :], bank[5][:, 0:SEQ], bqc[:, 0:1], HD ** -0.5, ALU.add,
                                            ALU.mult).then_inc(s["qT"], 1)

                def values(b, par):
                    dve.wait_ge(s["v"], b + 1)
                    for c in range(2):
                        last = nc.vector.tensor_tensor(Vs1[:, 2 * par + c, :, 0:HD],
                                                       bank[5][:, c * P:(c + 1) * P].rearrange("p (h d) -> p h d", d=HD),
                                                       bv_bc[:, :].rearrange("p (h d) -> p h d", d=HD), ALU.add)
                    last.then_inc(s["vb"], 1)

                def maxima(b, k):
                    G, slot = 8 * b + k, k % 2
                    for j in range(2):
                        dve.wait_ge(s["st"], 2 * G + j + 1)
                        dve.wait_ge(s["ex"], 4 * G + 4)
                        nc.vector.tensor_reduce(mx1[:, slot, 2 * j:2 * j + 2],
                                                bank[2 * slot + j][:, :].rearrange("p (h k) -> p h k", k=SEQ), X,
                                                ALU.max, negate=True).then_inc(s["mx"], 1)

                def evacuate(b, k):
                    G, slot = 8 * b + k, k % 2
                    for j in range(2):
                        dve.wait_ge(s["pt"], 2 * G + j + 5)
                        dve.wait_ge(s["pv"], G + 1)
                        nc.vector.tensor_copy(PT1[:, slot, 4 * j:4 * j + 4, :].rearrange("p a b -> p (a b)"),
                                              bank[6 if j else 4][:, :]).then_inc(s["pe"], 1)

                def normalise(b):
                    dve.wait_ge(s["pv"], 8 * b + 10)
                    ov = bank[7][:, 0:288].rearrange("p (t h e) -> p t h e", t=2, e=HD + 1)
                    nc.vector.reciprocal(rec1, ov[:, :, :, HD]).then_inc(s["rec"], 1)
                    dve.wait_ge(s["rec"], 2 * b + 1)
                    nc.vector.tensor_tensor(rec1, rec1,
                                            sel.rearrange("p a b c -> p a (b c)")[:, :, bass.ds(b * HEADS, HEADS)],
                                            ALU.mult).then_inc(s["rec"], 1)
                    dve.wait_ge(s["rec"], 2 * b + 2)
                    for t in range(2):
                        last = nc.vector.tensor_tensor(on1[:, t, :].rearrange("p (h d) -> p h d", d=HD),
                                                       ov[:, t, :, 0:HD],
                                                       rec1[:, t, :].unsqueeze(2).to_broadcast([P, HEADS, HD]),
                                                       ALU.mult)
                    last.then_inc(s["on"], 1)

                def update(b):
                    dve.wait_ge(s["y"], b + 1)
                    xu = x_sb[:, bass.ds(2 * b, 2), :].rearrange("p a b -> p (a b)")
                    nc.vector.tensor_tensor(xu, bank[5][:, 256:512], xu, ALU.add).then_inc(s["x"], 1)

                def sequence(b, par, first=False, last=False):
                    for k in range(8):
                        if k < 7:
                            maxima(b, k + 1)
                        elif not last:
                            maxima(b + 1, 0)
                        evacuate(b, k)
                        if k == 0 and not first:
                            normalise(b - 1)
                        if k == 3 and not first:
                            update(b - 1)
                        if k == 4 and not last:
                            project(b + 1, 1 - par)
                        if k == 6 and not last:
                            values(b + 1, 1 - par)

                project(0, 0)
                values(0, 0)
                maxima(0, 0)
                sequence(0, 0, first=True)
                with dve.Fori(0, NP_ // 2 - 1) as i:
                    sequence(2 * i + 1, 1)
                    sequence(2 * i + 2, 0)
                sequence(NP_ - 1, 1, last=True)
                normalise(NP_ - 1)
                update(NP_ - 1)

            def product_keys(s, f):
                base = f * NT
                dve.wait_ge(pr["ev"], 2 + (2 * f + 4) * NG)
                for g in range(NG):
                    last = nc.vector.bn_stats(bnst[:, g, :], xT[:, g * GW:(g + 1) * GW])
                last.then_inc(s["bst"], 1)
                dve.wait_ge(s["bst"], f + 1)
                nc.vector.bn_aggr(bnmv, bnst.rearrange("p a b -> p (a b)")).then_inc(s["bag"], 1)
                dve.wait_ge(s["bag"], f + 1)
                nc.vector.tensor_scalar(bnve, bnmv[:, 1:2], LN_EPS, None, ALU.add).then_inc(s["bve"], 1)
                dve.wait_ge(s["bsd"], f + 1)
                nc.vector.reciprocal(bnrs, bnsd).then_inc(s["brs"], 1)
                dve.wait_ge(s["brs"], 2 * f + 1)
                nc.vector.tensor_tensor(bna, pg[:, :], bnrs, ALU.mult).then_inc(s["bsc"], 1)
                dve.wait_ge(s["bsc"], 2 * f + 1)
                nc.vector.tensor_tensor(bnrs, bnmv[:, 0:1], bna, ALU.mult).then_inc(s["brs"], 1)
                dve.wait_ge(s["brs"], 2 * f + 2)
                nc.vector.tensor_tensor(bnb, pb_[:, :], bnrs, ALU.subtract).then_inc(s["bsc"], 1)

                def top8(n, par):
                    dve.wait_ge(s["sim"], base + n + 3)
                    dve.sem_inc(s_go, 1)
                    for c in range(2 * PH):
                        last = nc.vector.max(m8raw[:, c, :], bank[0][:, c * NK:(c + 1) * NK])
                    last.then_inc(s["m8"], 1)
                    dve.wait_ge(s["m8"], base + n + 1)
                    first = m8raw[:, :, 0:1]
                    nc.vector.tensor_tensor(E5[:, par, 0:512].rearrange("p (c k) -> p c k", k=NK),
                                            bank[0][:, :].rearrange("p (c k) -> p c k", k=NK),
                                            first.to_broadcast([P, 2 * PH, NK]), ALU.subtract).then_inc(s["sub"], 1)
                    nc.vector.tensor_tensor(E5[:, par, 512:640].rearrange("p (c k) -> p c k", k=8), m8raw,
                                            first.to_broadcast([P, 2 * PH, 8]), ALU.subtract).then_inc(s["sub"], 1)

                def weights(n, par):
                    dve.wait_ge(s["ex"], base + n + 1)
                    e8 = E5[:, par, 512:640].rearrange("p (q h k) -> p q h k", q=2, k=8)
                    x8, y8 = e8[:, 0], e8[:, 1]

                    def rank_products(at, a, na, b, nb):
                        m = max(na, nb)
                        xa = x8[:, :, a:a + na].to_broadcast([P, PH, m]) if na < m else x8[:, :, a:a + na]
                        yb = y8[:, :, b:b + nb].to_broadcast([P, PH, m]) if nb < m else y8[:, :, b:b + nb]
                        return nc.vector.tensor_tensor(cand[:, :, at:at + m], xa, yb, ALU.mult)

                    rank_products(0, 0, 1, 0, 8)
                    rank_products(8, 1, 1, 0, 4)
                    rank_products(12, 2, 6, 0, 1)
                    rank_products(18, 2, 2, 1, 1).then_inc(s["cand"], 1)
                    dve.wait_ge(s["cand"], base + n + 1)
                    dve.sem_inc(s_go, 1)
                    for h in range(PH):
                        last = nc.vector.max(c8[:, h, :], cand[:, h, :])
                    last.then_inc(s["c8"], 1)
                    dve.wait_ge(s["c8"], base + n + 1)
                    nc.vector.tensor_reduce(zsum, c8, X, ALU.add).then_inc(s["z"], 1)
                    dve.wait_ge(s["z"], base + n + 1)
                    nc.vector.reciprocal(rz, zsum).then_inc(s["rz"], 1)
                    dve.wait_ge(s["rz"], base + n + 1)
                    nc.vector.tensor_tensor(exs[:, par, :].rearrange("p (h k) -> p h k", k=NK),
                                            E5[:, par, 0:256].rearrange("p (h k) -> p h k", k=NK),
                                            rz.unsqueeze(2).to_broadcast([P, PH, NK]), ALU.mult).then_inc(s["sc"], 1)
                    nc.vector.scalar_tensor_tensor(thr[:, par, :], c8[:, :, 7], 1.0 - 5e-7, rz, ALU.mult,
                                                   ALU.mult).then_inc(s["sc"], 1)

                def combine(m, par):
                    dve.wait_ge(s["acc"], NU * (base + m + 2))
                    for half in range(2):
                        c = slice(half * 512, (half + 1) * 512)
                        dve.wait_ge(s["g"], 2 * (base + m) + half + 2)
                        nc.vector.tensor_tensor(cg[:, c], bank[2 + 2 * par + half][:, :], G5[:, par, c],
                                                ALU.mult).then_inc(s["cg"], 1)

                def update(m):
                    dve.wait_ge(s["y"], base + m + 1)
                    xm = x_sb[:, bass.ds(m, 1), :].rearrange("p a b -> p (a b)")
                    nc.vector.scalar_tensor_tensor(xm, bank[7][:, 0:D], 0.5, xm, ALU.mult, ALU.add).then_inc(s["x"], 1)

                def tile(n, par, front=True, finish=True):
                    dve.wait_ge(s["sc"], 2 * (base + n) + 2)
                    for h in range(PH):
                        if h in POOL_HEADS:
                            dve.wait_ge(s["P"], len(POOL_HEADS) * (base + n) + POOL_HEADS.index(h) + 1)
                        else:
                            dve.wait_ge(s["M"], 8 * (base + n) + h + 5)
                            nc.vector.tensor_tensor(grid(Pm, h % NPS), ex_rows(par, h), ey_cols(par, h),
                                                    ALU.mult).then_inc(s["A"], 1)
                            dve.wait_ge(s["A"], len(DVE_HEADS) * (base + n) + DVE_HEADS.index(h) + 1)
                        back = h - NMS
                        if back >= 0 and back in UNITS:
                            dve.wait_ge(s["acc"], NU * (base + n + 1) + UNITS.index(back) + 1)
                        if back < 0 and back + PH in UNITS:
                            dve.wait_ge(s["acc"], NU * (base + n) + UNITS.index(back + PH) + 1)
                        if back >= 0 and back + 1 in MERGED:
                            dve.wait_ge(s["ys"], len(MERGED) * (base + n) + MERGED.index(back + 1) + 2)
                        if back < 0 and back + PH + 1 in MERGED:
                            dve.wait_ge(s["ys"], len(MERGED) * (base + n - 1) + MERGED.index(back + PH + 1) + 2)
                        nc.vector.scalar_tensor_tensor(Mm[:, h % NMS, :], Pm[:, h % NPS, :], thr[:, par, h:h + 1],
                                                       Pm[:, h % NPS, :], ALU.is_ge, ALU.mult).then_inc(s["M"], 1)
                        if h in MERGED:
                            dve.wait_ge(s["M"], 8 * (base + n) + h + 9)
                            nc.vector.tensor_tensor(Mm[:, h % NMS, :], Mm[:, h % NMS, :], Mm[:, (h - 1) % NMS, :],
                                                    ALU.add).then_inc(s["ys"], 1)
                        if h == 1 and front:
                            top8(n + 1, 1 - par)
                        if h == 2 and finish:
                            combine(n - 1, 1 - par)
                        if h == 4 and front:
                            weights(n + 1, 1 - par)
                        if h == 6 and finish:
                            update(n - 1)

                top8(0, 0)
                weights(0, 0)
                tile(0, 0, finish=False)
                with dve.Fori(0, NT // 2 - 1) as i:
                    tile(2 * i + 1, 1)
                    tile(2 * i + 2, 0)
                tile(NT - 1, 1, front=False)
                combine(NT - 1, 1)
                update(NT - 1)

            if STOP > 0:
                for k in range(min(STOP, STAGES)):
                    prep(k)
                    if k == 0:
                        setup_ffn()
                    if k == 1:
                        setup_rest()
                    if k in (0, 2):
                        ffn(ff, k // 2)
                    if k == 1:
                        l0(L0)
                    if k == 4:
                        l1(L1)
                    if k in (3, 5):
                        product_keys(pk, (k - 3) // 2)

        @block.scalar
        def _(act):
            def prep(k):
                s, base = pr, k * NG
                act.wait_ge(s["ve"], k + 1)
                nc.scalar.activation(stdev[:, :], vareps[:, :], ACT.Sqrt).then_inc(s["sd"], 1)
                with act.Fori(0, NG // 2) as i:
                    for par in range(2):
                        n = 2 * i + par
                        act.wait_ge(s["tr"], base + n + 3)
                        nc.scalar.activation(xT[:, bass.ds(n * GW, GW)], bank[6 + par][:, :],
                                             ACT.Copy).then_inc(s["ev"], 1)

            def ffn(s, f):
                base = f * NG
                with act.Fori(0, NG // 2) as i:
                    for par in range(2):
                        g = 2 * i + par
                        act.wait_ge(s["s"], base + g + 1)
                        act.wait_ge(s["o"], base + g + 1)
                        for j in list(range(JPE, NJ)) + list(range(JPE)):
                            nc.scalar.activation(h_ff[:, par, j, :], bank[2 + par][:, :], ACT.Relu,
                                                 bias=b1e[:, j:j + 1], scale=w1c[:, j:j + 1]).then_inc(s["h"], 1)

            def l0(s):
                def squares(u):
                    act.wait_ge(s["cent"], u + 1)
                    nc.scalar.activation(sq0, qc0, ACT.Square).then_inc(s["sq"], 1)

                def roots(u):
                    act.wait_ge(s["var"], u + 1)
                    nc.scalar.activation(sd0, var0, ACT.Sqrt).then_inc(s["sd"], 1)

                def keys(u):
                    act.wait_ge(s["qT"], u + 1)
                    act.wait_ge(s["kM"], u)
                    nc.scalar.activation(kR0, bank[4][:, 2 * P:4 * P], ACT.Copy).then_inc(s["kT"], 1)

                def exponentials(u, t):
                    for hh in range(2):
                        act.wait_ge(s["sub"], 4 * u + 2 * t + hh + 5)
                        nc.scalar.activation(E0[:, t, hh, :], E0[:, t, hh, :], ACT.Exp).then_inc(s["ex"], 1)

                def evacuate(u, t):
                    for hh in range(2):
                        act.wait_ge(s["pt"], 4 * u + 2 * t + hh + 1)
                        act.wait_ge(s["pv"], 2 * u + t + 1)
                        at = 8 * t + 4 * hh
                        nc.scalar.activation(PT0[:, at:at + 4, :].rearrange("p a b -> p (a b)"),
                                             bank[5 + hh][:, :], ACT.Copy).then_inc(s["pe"], 1)

                def outputs(u):
                    act.wait_ge(s["ot"], u + 1)
                    nc.scalar.activation(oT0, bank[4][:, 0:2 * P], ACT.Copy).then_inc(s["oe"], 1)

                def pair(u, back=True, one=True, two=True):
                    if back:
                        outputs(u - 1)
                    evacuate(u, 0)
                    exponentials(u, 1)
                    if two:
                        squares(u + 2)
                    if one:
                        exponentials(u + 1, 0)
                    evacuate(u, 1)
                    if two:
                        roots(u + 2)
                        keys(u + 2)

                for u in range(2):
                    squares(u)
                    roots(u)
                    keys(u)
                exponentials(0, 0)
                pair(0, back=False)
                with act.Fori(0, NP_ // 2 - 2) as i:
                    pair(2 * i + 1)
                    pair(2 * i + 2)
                pair(NP_ - 3)
                pair(NP_ - 2, two=False)
                pair(NP_ - 1, one=False, two=False)
                outputs(NP_ - 1)

            def l1(s):
                with act.Fori(0, NP_ // 2) as i:
                    for par in range(2):
                        act.wait_ge(s["pq"], 2 * i + par + 1)
                        act.wait_ge(s["sq_used"], 2 * i + par + 1)
                        nc.scalar.activation(sq1[:, par, :], bank[par][:, 0:SEQ], ACT.Square,
                                             bias=bqc[:, 0:1]).then_inc(s["psq"], 1)
                def keys(b):
                    act.wait_ge(s["qT"], b + 1)
                    act.wait_ge(s["kM"], b + 1)
                    nc.scalar.activation(kR1, bank[5][:, SEQ:2 * SEQ], ACT.Copy).then_inc(s["kT"], 1)

                def exponentials(b, k):
                    G, slot = 8 * b + k, k % 2
                    for j in range(2):
                        act.wait_ge(s["mx"], 2 * G + j + 1)
                        act.wait_ge(s["pt"], 2 * G + j + 1)
                        for q in range(2):
                            nc.scalar.activation(E1[:, slot, 2 * j + q, :], bank[2 * slot + j][:, q * SEQ:(q + 1) * SEQ],
                                                 ACT.Exp, bias=mx1[:, slot, 2 * j + q:2 * j + q + 1]).then_inc(s["ex"], 1)

                def outputs(b):
                    act.wait_ge(s["ot"], b + 1)
                    nc.scalar.activation(oT1.rearrange("p a b -> p (a b)"), bank[5][:, 0:2 * P],
                                         ACT.Copy).then_inc(s["oe"], 1)

                def sequence(b, par, first=False, last=False):
                    for k in range(8):
                        if k < 7:
                            exponentials(b, k + 1)
                        elif not last:
                            exponentials(b + 1, 0)
                        if k == 2 and not first:
                            outputs(b - 1)
                        if k == 5 and not last:
                            keys(b + 1)

                keys(0)
                exponentials(0, 0)
                sequence(0, 0, first=True)
                with act.Fori(0, NP_ // 2 - 1) as i:
                    sequence(2 * i + 1, 1)
                    sequence(2 * i + 2, 0)
                sequence(NP_ - 1, 1, last=True)
                outputs(NP_ - 1)

            def product_keys(s, f):
                base = f * NT
                act.wait_ge(s["bve"], f + 1)
                nc.scalar.activation(bnsd, bnve, ACT.Sqrt).then_inc(s["bsd"], 1)

                def slots(m, par):
                    act.wait_ge(s["sim"], base + m + 1)
                    act.sem_inc(s_go, 1)
                    nc.scalar.activation(zT[:, par, :], xT[:, bass.ds(m * P, P)], ACT.Identity, bias=bnb[:, 0:1],
                                         scale=bna[:, 0:1]).then_inc(s["zt"], 1)

                def exponentials(m, par):
                    act.wait_ge(s["sub"], 2 * (base + m + 1))
                    nc.scalar.activation(E5[:, par, :], E5[:, par, :], ACT.Exp).then_inc(s["ex"], 1)

                def tile(n, par, front=True, ahead=True):
                    if front:
                        exponentials(n + 1, 1 - par)
                    if not (f == 0 and isinstance(n, int) and n == 0):
                        act.wait_ge(s["cg"], 2 * (base + n))
                    for half in range(2):
                        act.wait_ge(s["o"], 2 * (base + n) + half + 1)
                        nc.scalar.activation(G5[:, par, half * 512:(half + 1) * 512], bank[6 if half else 1][:, :],
                                             ACT.Gelu).then_inc(s["g"], 1)
                    if ahead:
                        slots(n + 2, par)

                act.wait_ge(s["bsc"], 2 * f + 2)
                slots(0, 0)
                slots(1, 1)
                exponentials(0, 0)
                tile(0, 0)
                with act.Fori(0, NT // 2 - 2) as i:
                    tile(2 * i + 1, 1)
                    tile(2 * i + 2, 0)
                tile(NT - 3, 1)
                tile(NT - 2, 0, ahead=False)
                tile(NT - 1, 1, front=False, ahead=False)

            act.sem_inc(L1["kM"], 1)
            act.sem_inc(L0["pe"], 2)
            act.sem_inc(pr["ev"], 2)
            act.sem_inc(pk["g"], 1)
            act.sem_inc(L1["ex"], 8)
            for k in range(min(STOP, STAGES)):
                prep(k)
                if k == 0:
                    act.wait_ge(s_set, 2)
                if k in (0, 2):
                    ffn(ff, k // 2)
                if k == 1:
                    l0(L0)
                if k == 4:
                    l1(L1)
                if k in (3, 5):
                    product_keys(pk, (k - 3) // 2)

        @block.tensor
        def _(pe):
            def setup_ffn():
                pe.wait_ge(s_wf, 16 * NWF)
                pe.wait_ge(s_set, 3)
                nc.tensor.matmul(bank[0][:, 0:D], b2r[:, :], wout2[0:M_FF, :], start=True,
                                 stop=True).then_inc(s_ps, 1)
                pe.wait_ge(s_set, SET_W2O)

            def turn_weights():
                pe.wait_ge(s_w, 16 * NW)
                for i in range(4):
                    c = slice(i * P, (i + 1) * P)
                    nc.tensor.transpose(bank[1][:, c], w1nat[:, i, :], ident[:, :])
                    nc.tensor.transpose(bank[2][:, c], keysn[:, i, :], ident[:, :])
                    nc.tensor.transpose(bank[3][:, c], kinn[:, i, :], ident[:, :])
                    last = nc.tensor.transpose(bank[4][:, c], kinn[:, 4 + i, :], ident[:, :])
                last.then_inc(s_ps, 1)

            def fold_keys():
                pe.wait_ge(s_set, SET_KEYS)
                kv = keysT.rearrange("p (h k q) -> p q h k", h=PH, q=2)
                for q in range(2):
                    for h in range(PH):
                        c = q * PH + h
                        last = nc.tensor.matmul(bank[5][:, c * NK:(c + 1) * NK], wqn[:, c, :], kv[:, q, h, :],
                                                start=True, stop=True)
                last.then_inc(s_ps, 1)
                pe.wait_ge(s_set, SET_ALL)

            def prep(k):
                s, base = pr, k * NG
                if k:
                    pe.wait_ge(*last_x[k])
                if k == 0:
                    pe.wait_ge(s_id, 16)
                if k == 1:
                    turn_weights()
                with pe.Fori(0, NG // 2) as i:
                    for par in range(2):
                        n = 2 * i + par
                        pe.wait_ge(s["xn"], base + n + 1)
                        pe.wait_ge(s["ev"], base + n + 1)
                        for t in range(GT):
                            last = nc.tensor.transpose(bank[6 + par][:, t * P:(t + 1) * P], xn[:, par, t, :],
                                                       ident[:, :])
                        last.then_inc(s["tr"], 1)
                pe.wait_ge(s["ev"], 2 + (k + 1) * NG)

            def ffn(s, f):
                base = f * NG

                def project_in(n, par):
                    nc.tensor.matmul(bank[2 + par][:, :], win2[:, :, :].rearrange("p a b -> p (a b)"),
                                     xT[:, bass.ds(n * GW, GW)], start=True, stop=True).then_inc(s["s"], 1)

                def project_out(n, par):
                    pe.wait_ge(s["h"], NJ * (base + n + 1))
                    pe.wait_ge(s["hs"], (NJ - JPE) * (base + n + 1))
                    pe.wait_ge(s["x"], base + n + 1)
                    for t in range(GT):
                        c = slice(t * P, (t + 1) * P)
                        for j in range(JPE):
                            nc.tensor.matmul(bank[4 + par][:, c], h_ff[:, par, j, c], w2o[:, j, :],
                                             start=(j == 0), stop=False)
                        last = nc.tensor.matmul(bank[4 + par][:, c], hsum[:, par, c], wout2[:, :], start=False,
                                                stop=True)
                    last.then_inc(s["o"], 1)

                project_in(0, 0)
                project_in(1, 1)
                project_out(0, 0)
                with pe.Fori(1, NG // 2) as i:
                    project_in(2 * i, 0)
                    project_out(2 * i - 1, 1)
                    project_in(2 * i + 1, 1)
                    project_out(2 * i, 0)
                project_out(NG - 1, 1)

            def l0(s):
                def project(u, par):
                    pe.wait_ge(s["xs"], u + 1)
                    if not (isinstance(u, int) and u < 3):
                        pe.wait_ge(s["x"], u - 2)
                    for t in range(2):
                        last = nc.tensor.matmul(bank[4][:, t * 2 * D:(t + 1) * 2 * D], xs0[:, par, t * P:(t + 1) * P],
                                                wqkv[:, 0:2 * D], start=True, stop=True)
                    last.then_inc(s["qk"], 1)

                def values(u, par, left):
                    pe.wait_ge(s["cent"], left)
                    for w in range(4):
                        for r in range(2):
                            last = nc.tensor.matmul(bank[4][r * WIN:(r + 1) * WIN, w * D:(w + 1) * D],
                                                    xs0[:, par, w * WIN:(w + 1) * WIN], wqkv[:, 2 * D:3 * D],
                                                    start=True, stop=True)
                    last.then_inc(s["v"], 1)

                def turn_qk(u, valued):
                    pe.wait_ge(s["qn"], u + 1)
                    pe.wait_ge(s["vb"], valued)
                    for j in range(2):
                        for t in range(2):
                            last = nc.tensor.transpose(bank[4][:, (2 * j + t) * P:(2 * j + t + 1) * P],
                                                       qn0[:, 2 * t + j, :], ident[:, :])
                    last.then_inc(s["qt"], 1)

                def scores(u, par, t):
                    pe.wait_ge(s["kM"], u + 1)
                    pe.wait_ge(s["qT"], u + 1)
                    pe.wait_ge(s["sub"], 4 * u + 2 * t + 2)
                    km = kM0.rearrange("p (a h) q -> p a h q", a=2)
                    for hh in range(2):
                        for half in range(2):
                            keys = slice(t * P + half * WIN, t * P + (half + 1) * WIN)
                            last = nc.tensor.matmul(bank[2 * t + hh][half * WIN:(half + 1) * WIN, :],
                                                    qT0[:, par, keys], km[:, par, 8 * hh:8 * hh + 8, keys],
                                                    start=True, stop=True)
                        last.then_inc(s["st"], 1)

                def turn(u, t):
                    for hh in range(2):
                        pe.wait_ge(s["ex"], 4 * u + 2 * t + hh + 1)
                        pe.wait_ge(s["pe"], 4 * u + 2 * t + hh + 1)
                        for j in range(4):
                            last = nc.tensor.transpose(bank[5 + hh][:, j * P:(j + 1) * P],
                                                       E0[:, t, hh, j * P:(j + 1) * P], ident[:, :])
                        last.then_inc(s["pt"], 1)

                def weigh(u, par, t):
                    pe.wait_ge(s["pe"], 4 * u + 2 * t + 4)
                    pe.wait_ge(s["vb"], u + 2)
                    pe.wait_ge(s["on"], u + 1)
                    vb = Vb0.rearrange("p a (w c) r e -> p a w c (r e)", w=4)
                    for c in range(8):
                        for half in range(2):
                            last = nc.tensor.matmul(bank[7][half * WIN:(half + 1) * WIN,
                                                            t * 144 + c * 18:t * 144 + (c + 1) * 18],
                                                    PT0[:, 8 * t + c, half * WIN:(half + 1) * WIN],
                                                    vb[:, par, 2 * t + half, c, :], start=True, stop=True)
                    last.then_inc(s["pv"], 1)

                def turn_outputs(u, turned):
                    pe.wait_ge(s["on"], u + 2)
                    pe.wait_ge(s["qT"], turned)
                    pe.wait_ge(s["kT"], turned)
                    for t in range(2):
                        last = nc.tensor.transpose(bank[4][:, t * P:(t + 1) * P], on0[:, t, :], ident[:, :])
                    last.then_inc(s["ot"], 1)

                def outputs(u):
                    pe.wait_ge(s["oe"], u + 1)
                    pe.wait_ge(s["cb"], NG)
                    for t in range(2):
                        last = nc.tensor.matmul(bank[4][:, 256 + t * D:256 + (t + 1) * D], oT0[:, t * P:(t + 1) * P],
                                                wproj[:, :], start=True, stop=True)
                    last.then_inc(s["y"], 1)

                def pair(u, par, back=True, one=True, two=True):
                    scores(u, par, 1)
                    if back:
                        turn_outputs(u - 1, u + 2 if one else u + 1)
                    turn(u, 0)
                    if back:
                        outputs(u - 1)
                    weigh(u, par, 0)
                    if two:
                        project(u + 2, par)
                    if one:
                        scores(u + 1, 1 - par, 0)
                    turn(u, 1)
                    if one:
                        if not two:
                            pe.wait_ge(s["x"], u)
                        values(u + 1, 1 - par, u + 3 if two else u + 2)
                    weigh(u, par, 1)
                    if two:
                        turn_qk(u + 2, u + 3)

                project(0, 0)
                values(0, 0, 1)
                turn_qk(0, 2)
                pe.wait_ge(s["qT"], 1)
                pe.wait_ge(s["kT"], 1)
                project(1, 1)
                turn_qk(1, 2)
                scores(0, 0, 0)
                pe.wait_ge(s["qT"], 2)
                pe.wait_ge(s["kT"], 2)
                pair(0, 0, back=False)
                with pe.Fori(0, NP_ // 2 - 2) as i:
                    pair(2 * i + 1, 1)
                    pair(2 * i + 2, 0)
                pair(NP_ - 3, 1)
                pair(NP_ - 2, 0, two=False)
                pair(NP_ - 1, 1, one=False, two=False)
                turn_outputs(NP_ - 1, NP_)
                outputs(NP_ - 1)

            def l1(s):
                pe.wait_ge(s_set, SET_W1T)
                for half in range(2):
                    for b in range(8):
                        n = half * 8 + b
                        par = n % 2
                        if n >= 2:
                            pe.wait_ge(s["psq"], n - 1)
                        nc.tensor.matmul(bank[par][:, 0:SEQ], w1T[:, 0, :], xT[:, n * SEQ:(n + 1) * SEQ],
                                         start=True, stop=True).then_inc(s["pq"], 1)
                        if b >= 1:
                            pe.wait_ge(s["psq"], n)
                            nc.tensor.matmul(bank[2 + half][:, 0:SEQ], headsel[:, b - 1, :], sq1[:, 1 - par, :],
                                             start=(b == 1), stop=False).then_inc(s["sq_used"], 1)
                    pe.wait_ge(s["psq"], half * 8 + 8)
                    nc.tensor.matmul(bank[2 + half][:, 0:SEQ], headsel[:, 7, :], sq1[:, 1, :], start=False,
                                     stop=True).then_inc(s["sq_used"], 1)
                    pe.wait_ge(s["sq_used"], 2 + half * 8 + 8)
                    pe.sem_inc(s["pn"], 1)
                pe.wait_ge(s["selT"], 2)
                for c in range(2):
                    for half in range(2):
                        last = nc.tensor.transpose(bank[4][:, (2 * c + half) * P:(2 * c + half + 1) * P],
                                                   selT[:, half, c * P:(c + 1) * P], ident[:, :])
                last.then_inc(s["str"], 1)
                pe.wait_ge(s["sel"], 1)

                def queries_keys(b):
                    if not (isinstance(b, int) and b < 2):
                        pe.wait_ge(s["x"], b - 1)
                    xb = xT[:, bass.ds(b * SEQ, SEQ)]
                    nc.tensor.matmul(bank[5][:, 0:SEQ], w1T[:, 0, :], xb, start=True, stop=True)
                    nc.tensor.matmul(bank[5][:, SEQ:2 * SEQ], w1T[:, 1, :], xb, start=True,
                                     stop=True).then_inc(s["qk"], 1)

                def values(b):
                    pe.wait_ge(s["xs"], b + 1)
                    pe.wait_ge(s["qT"], b + 1)
                    pe.wait_ge(s["kT"], b + 1)
                    for c in range(2):
                        last = nc.tensor.matmul(bank[5][:, c * D:(c + 1) * D], xs1[:, c * P:(c + 1) * P], w1T[:, 2, :],
                                                start=True, stop=True)
                    last.then_inc(s["v"], 1)

                def scores(b, par, k):
                    G, c = 8 * b + k, k // 4
                    pe.wait_ge(s["ex"], 4 * G + 4)
                    pe.wait_ge(s["kM"], b + 2)
                    pe.wait_ge(s["qT"], b + 1)
                    for j in range(2):
                        h = HEADS * par + 4 * (k % 4) + 2 * j
                        nc.tensor.matmul(bank[2 * (k % 2) + j][:, :], qT1[:, par, c * P:(c + 1) * P],
                                         kM1[:, h:h + 2, :], start=True, stop=True).then_inc(s["st"], 1)

                def turn(b, k):
                    G, slot = 8 * b + k, k % 2
                    for j in range(2):
                        pe.wait_ge(s["ex"], 4 * G + 2 * j + 10)
                        pe.wait_ge(s["pe"], 2 * G + j + 1)
                        for q in range(2):
                            for kc in range(2):
                                last = nc.tensor.transpose(bank[6 if j else 4][:, (2 * q + kc) * P:(2 * q + kc + 1) * P],
                                                           E1[:, slot, 2 * j + q, kc * P:(kc + 1) * P], ident[:, :])
                        last.then_inc(s["pt"], 1)

                def weigh(b, par, k):
                    G, c = 8 * b + k, k // 4
                    pe.wait_ge(s["pe"], 2 * G + 4)
                    pe.wait_ge(s["vb"], b + 2)
                    pe.wait_ge(s["on"], b + 1)
                    for j in range(2):
                        for q in range(2):
                            h = 4 * (k % 4) + 2 * j + q
                            for kc in range(2):
                                last = nc.tensor.matmul(bank[7][:, c * 144 + h * 9:c * 144 + (h + 1) * 9],
                                                        PT1[:, k % 2, 4 * j + 2 * q + kc, :], Vs1[:, 2 * par + kc, h, :],
                                                        start=(kc == 0), stop=(kc == 1))
                    last.then_inc(s["pv"], 1)

                def turn_outputs(b, last=False):
                    pe.wait_ge(s["on"], b + 2)
                    if not last:
                        pe.wait_ge(s["vb"], b + 3)
                    for t in range(2):
                        last = nc.tensor.transpose(bank[5][:, t * P:(t + 1) * P], on1[:, t, :], ident[:, :])
                    last.then_inc(s["ot"], 1)

                def outputs(b):
                    pe.wait_ge(s["oe"], b + 1)
                    pe.wait_ge(s["cb"], NG)
                    for t in range(2):
                        last = nc.tensor.matmul(bank[5][:, 256 + t * D:256 + (t + 1) * D], oT1[:, t, :], w1T[:, 3, :],
                                                start=True, stop=True)
                    last.then_inc(s["y"], 1)

                def sequence(b, par, first=False, last=False):
                    for k in range(8):
                        if k < 7:
                            scores(b, par, k + 1)
                        elif not last:
                            scores(b + 1, 1 - par, 0)
                        turn(b, k)
                        if k > 0:
                            weigh(b, par, k - 1)
                        elif not first:
                            weigh(b - 1, 1 - par, 7)
                        if k == 1 and not first:
                            turn_outputs(b - 1)
                        if k == 2 and not first:
                            outputs(b - 1)
                        if k == 3 and not last:
                            queries_keys(b + 1)
                        if k == 5 and not last:
                            values(b + 1)

                queries_keys(0)
                values(0)
                scores(0, 0, 0)
                sequence(0, 0, first=True)
                with pe.Fori(0, NP_ // 2 - 1) as i:
                    sequence(2 * i + 1, 1)
                    sequence(2 * i + 2, 0)
                sequence(NP_ - 1, 1, last=True)
                weigh(NP_ - 1, 1, 7)
                turn_outputs(NP_ - 1, last=True)
                outputs(NP_ - 1)

            def product_keys(s, f):
                base = f * NT

                def similarities(m, par):
                    pe.wait_ge(s["zt"], base + m + 1)
                    pe.wait_ge(s["sub"], 2 * (base + m))
                    nc.tensor.matmul(bank[0][:, :], zT[:, par, :], weff[:, :, :, :].rearrange("p a b c -> p (a b c)"),
                                     start=True, stop=True).then_inc(s["sim"], 1)

                def experts(m, half):
                    if not (f == 0 and isinstance(m, int) and m == 0):
                        pe.wait_ge(s["g"], 2 * (base + m) + half)
                    for j in range(4):
                        c = half * 512 + j * P
                        last = nc.tensor.matmul(bank[6 if half else 1][:, j * P:(j + 1) * P], kinT[:, c:c + P],
                                                xT[:, bass.ds(m * P, P)], start=True, stop=True)
                    last.then_inc(s["o"], 1)

                def add_unit(n, par, at):
                    h = UNITS[at]
                    if h in MERGED:
                        pe.wait_ge(s["ys"], len(MERGED) * (base + n) + MERGED.index(h) + 2)
                    else:
                        pe.wait_ge(s["M"], 8 * (base + n) + h + 9)
                    for c in range(NCH):
                        last = nc.tensor.matmul(bank[2 + 2 * par + c // 4][:, (c % 4) * P:(c % 4 + 1) * P],
                                                Mm[:, h % NMS, c * P:(c + 1) * P], ident[:, :],
                                                start=(at == 0 and c % 4 == 0), stop=(at == NU - 1 and c % 4 == 3))
                    last.then_inc(s["acc"], 1)

                def outputs(m):
                    pe.wait_ge(s["x"], base + m + 1)
                    for c in range(NCH):
                        if c % 4 == 0:
                            pe.wait_ge(s["cg"], 2 * (base + m) + c // 4 + 3)
                        last = nc.tensor.matmul(bank[7][:, 0:D], cg[:, c * P:(c + 1) * P], kout[:, c, :],
                                                start=(c == 0), stop=(c == NCH - 1))
                    last.then_inc(s["y"], 1)

                def tile(n, par, front=True, finish=True):
                    if front:
                        similarities(n + 1, 1 - par)
                    for at in range(NU):
                        add_unit(n, par, at)
                        if at == OUT_AT and finish:
                            outputs(n - 1)
                        if at == OUT_AT:
                            experts(n, 0)
                            experts(n, 1)

                similarities(0, 0)
                tile(0, 0, finish=False)
                with pe.Fori(0, NT // 2 - 1) as i:
                    tile(2 * i + 1, 1)
                    tile(2 * i + 2, 0)
                tile(NT - 1, 1, front=False)
                outputs(NT - 1)

            pe.sem_inc(pr["tr"], 2)
            pe.sem_inc(ff["o"], 2)
            pe.sem_inc(L1["sq_used"], 2)
            pe.sem_inc(L0["pv"], 2)
            pe.sem_inc(L1["pt"], 4)
            pe.sem_inc(L1["pv"], 2)
            pe.sem_inc(pk["sim"], 2)
            pe.sem_inc(pk["acc"], NU)
            if STOP > 0:
                for k in range(min(STOP, STAGES)):
                    prep(k)
                    if k == 0:
                        setup_ffn()
                    if k in (0, 2):
                        ffn(ff, k // 2)
                    if k == 1:
                        fold_keys()
                        l0(L0)
                    if k == 4:
                        l1(L1)
                    if k in (3, 5):
                        product_keys(pk, (k - 3) // 2)


_INS = ['L0_attn_x', 'L0_attn_W_qkv', 'L0_attn_ln_gamma', 'L0_attn_ln_beta', 'L0_attn_W_proj', 'L0_attn_b_proj',
        'L0_ffn_Win', 'L0_ffn_bin_', 'L0_ffn_W1', 'L0_ffn_b1', 'L0_ffn_W2', 'L0_ffn_b2', 'L0_ffn_Wout', 'L0_ffn_bout',
        'L1_attn_Wq', 'L1_attn_bq', 'L1_attn_Wk', 'L1_attn_bk', 'L1_attn_Wv', 'L1_attn_bv', 'L1_attn_Wo',
        'L1_attn_bo', 'L1_ffn_gamma', 'L1_ffn_beta', 'L1_ffn_w_q', 'L1_ffn_keys', 'L1_ffn_key_in', 'L1_ffn_key_out']


def constants():
    p = np.arange(P)
    head = p // HD
    c = {"c_ident": np.eye(P, dtype=np.float32)}
    c["c_hmask"] = (head[:, None] == np.arange(HEADS)[None]).astype(np.float32)
    c["c_vmask"] = (p[:, None] // WIN == np.arange(2)[None]).astype(np.float32)
    c["c_headsel"] = (16 * np.arange(8)[None, :, None] + head[:, None, None] == p[None, None, :]).astype(np.float32)
    return c


def kernel(**inputs):
    import concourse.bacc as _bacc
    from concourse import mybir as _mybir
    from concourse.bass_utils import run_bass_kernel_spmd as _run

    nc = _bacc.Bacc("TRN2", target_bir_lowering=False, num_devices=1)
    arrays, args = {}, {}
    named = {name: np.ascontiguousarray(inputs[name]) for name in _INS}
    named.update(constants())
    for name, a in named.items():
        arrays[f"in_{name}_dram"] = a
        args[name] = nc.dram_tensor(f"in_{name}_dram", a.shape, _mybir.dt.from_np(a.dtype), kind="ExternalInput").ap()
    out = nc.dram_tensor("out_0_dram", (BATCH, SEQ, D), _mybir.dt.float32, kind="ExternalOutput").ap()
    build(nc, args, out)
    r = _run(nc, [arrays], core_ids=[0])
    return r.results[0]["out_0_dram"]
```

```python
import concourse.bass as bass
from concourse import mybir
from contextlib import ExitStack

import numpy as np

P = 128
D = 128
BATCH, SEQ = 16, 256
T = BATCH * SEQ
NT = T // P
HEADS, HD = 16, 8
WIN = 64
GT = 4
NG = NT // GT
GW = GT * P
NP_ = NT // 2
M_FF, INNER = 64, 16
NJ = INNER // 2
TOP_U = SEQ // 5
PH, NK, KD, TOPK = 8, 32, 128, 8
NE = NK * NK
NCH = NE // P
LN_EPS = 1e-5
STAGES = 6
JPE = 3
SLOTS = 64
PAIRS = HEADS // 2


def build(nc, A, out):
    fp32 = mybir.dt.float32
    ALU = mybir.AluOpType
    ACT = mybir.ActivationFunctionType
    X = mybir.AxisListType.X

    ctx = ExitStack()
    with ctx:
        def sb(name, shape):
            return ctx.enter_context(nc.sbuf_tensor(name, shape, fp32))

        def sem(name):
            return ctx.enter_context(nc.semaphore(name))

        def sems(stage, names):
            return {n: sem(f"{stage}_{n}") for n in names.split()}

        x_sb = sb("x_sb", [P, NT, D])
        xT = sb("xT", [P, T])
        ident = sb("ident", [P, P])
        hmask = sb("hmask", [P, HEADS])
        vmask = sb("vmask", [P, 2])
        headsel = sb("headsel", [P, 8, P])
        stats = sb("stats", [P, NT, 6])
        mdiff = sb("mdiff", [P, NT])
        negmean = sb("negmean", [P, NT])
        vareps = sb("vareps", [P, NT])
        stdev = sb("stdev", [P, NT])
        rstd = sb("rstd", [P, NT])
        xn = sb("xn", [P, 2, GT, D])
        win2 = sb("win2", [P, 2, M_FF])
        bin2 = sb("bin2", [P, 1])
        w1c = sb("w1c", [P, NJ])
        b1c = sb("b1c", [P, NJ])
        b1e = sb("b1e", [P, NJ])
        w2c = sb("w2c", [P, NJ])
        b2c = sb("b2c", [M_FF, 1])
        b2r = sb("b2r", [M_FF, P])
        wout2 = sb("wout2", [P, D])
        w2o = sb("w2o", [P, JPE, D])
        bout_bc = sb("bout_bc", [P, D])
        ffn_add = sb("ffn_add", [P, D])
        wqkv = sb("wqkv", [P, 3 * D])
        wproj = sb("wproj", [P, D])
        bproj_bc = sb("bproj_bc", [P, D])
        gcol = sb("gcol", [P, 1])
        bcol = sb("bcol", [P, 1])
        gk = sb("gk", [P, HEADS])
        bk16 = sb("bk16", [P, HEADS])
        w1nat = sb("w1nat", [P, 4, D])
        w1T = sb("w1T", [P, 4, D])
        bqc = sb("bqc", [P, 1])
        bkc = sb("bkc", [P, 1])
        bq_bc = sb("bq_bc", [P, D])
        upper = sb("upper", [P, P])
        slots = sb("slots", [P, SLOTS])
        bv_bc = sb("bv_bc", [P, D])
        bo_bc = sb("bo_bc", [P, D])
        weff = sb("weff", [P, 2, PH, NK])
        kinT = sb("kinT", [P, NE])
        kout = sb("kout", [P, NCH, D])
        pg = sb("pg", [P, 1])
        pb_ = sb("pb_", [P, 1])
        work = sb("work", [P, 26000])

        def cut(at, *shape):
            n = int(np.prod(shape))
            v = work[:, at:at + n]
            if len(shape) == 2:
                v = v.rearrange("p (a b) -> p a b", b=shape[1])
            if len(shape) == 3:
                v = v.rearrange("p (a b c) -> p a b c", b=shape[1], c=shape[2])
            if len(shape) == 4:
                v = v.rearrange("p (a b c d) -> p a b c d", b=shape[1], c=shape[2], d=shape[3])
            return v, at + n

        bank = [ctx.enter_context(nc.psum_tensor(f"bank{i}", [P, 512], fp32)) for i in range(8)]

        s_x = sem("s_x")
        s_id = sem("s_id")
        s_wf = sem("s_wf")
        s_w = sem("s_w")
        s_out = sem("s_out")
        s_go = sem("s_go")
        s_set = sem("s_set")
        s_setp = sem("s_setp")
        s_ps = sem("s_ps")
        pr = sems("pr", "stat aggr nm ve sd rstd xn tr ev sq")
        ff = sems("ff", "s h hs o cb x")
        L0 = sems("l0", "kM xs qk v cent sq rsum var sd rs qn qt qT kT st mx sub ex pt pe pv vb rec on ot oe y cb x")
        L1 = sems("l1", "sq_used pq psq pn nc mr selT str sel rk rm xs S qv k Qn vb kT g QM sc mx ex sT sTe pt pe pv "
                        "rec on sca oe1 ot oe y cb x")
        pk = sems("pk", "bst bag bve bsd brs bsc zt sim m8 sub ex cand c8 z rz sc P M acc cg o g y x ys")
        last_x = {0: (s_x, 16 * NG)}
        last_x[1] = (ff["x"], 2 + NG)
        last_x[2] = (L0["x"], NP_)
        last_x[3] = (ff["x"], 2 + 2 * NG)
        last_x[4] = (pk["x"], 1 + NT)
        last_x[5] = (L1["x"], 1 + NP_)
        last_x[6] = (pk["x"], 1 + 2 * NT)

        h_ff, o = cut(0, 2, NJ, GW)
        hsum, _ = cut(o, 2, GW)
        xs0, o = cut(0, 2, 2 * P)
        qc0, o = cut(o, 512)
        sq0, o = cut(o, 512)
        qn0, o = cut(o, 4, P)
        qT0, o = cut(o, 2, 2 * P)
        kR0, o = cut(o, 2 * P)
        kM0, o = cut(o, 2 * HEADS, 2 * P)
        E0, o = cut(o, 2, 2, 512)
        PT0, o = cut(o, 16, P)
        Vb0, o = cut(o, 2, 32, 2, 9)
        on0, o = cut(o, 2, P)
        oT0, o = cut(o, 2 * P)
        sum0, o = cut(o, 64)
        var0, o = cut(o, 64)
        sd0, o = cut(o, 64)
        rs0, o = cut(o, 64)
        mx0, o = cut(o, 4, 8)
        rec0, o = cut(o, 2, 16)
        assert o <= 20000, o
        sq1, o = cut(0, 2, SEQ)
        n2, o = cut(o, 2, SEQ)
        n2w, o = cut(o, 2, SEQ)
        m8, o = cut(o, 2, 8)
        selT, o = cut(o, 2, SEQ)
        sel, o = cut(o, 2, 2, P)
        rk, o = cut(o, 2, BATCH * HEADS)
        ones, o = cut(o, P)
        xs1, o = cut(o, SEQ)
        S1, o = cut(o, 2, 2, HEADS * SLOTS)
        Qn, o = cut(o, 2, P)
        QM1, o = cut(o, HEADS * SLOTS)
        kT1, o = cut(o, SEQ)
        Vs1, o = cut(o, 4, HEADS, HD + 1)
        E1, o = cut(o, PAIRS, SEQ)
        PT1, o = cut(o, PAIRS, 2, P)
        ST1, o = cut(o, PAIRS, SEQ)
        O1, o = cut(o, PAIRS, 2, HD)
        on1, o = cut(o, 2, P)
        oT1, o = cut(o, 2, P)
        mx1, o = cut(o, PAIRS)
        rec1, o = cut(o, PAIRS, 2)
        assert o <= 26000, o
        NPS, NMS = 4, PH
        bnst, o = cut(0, 8, 6)
        bnmv, o = cut(o, 2)
        bnve, o = cut(o, 1)
        bnsd, o = cut(o, 1)
        bnrs, o = cut(o, 1)
        bna, o = cut(o, 1)
        bnb, o = cut(o, 1)
        zT, o = cut(o, 2, P)
        E5, o = cut(o, 2, 640)
        exs, o = cut(o, 2, PH * NK)
        m8raw, o = cut(o, 16, 8)
        cand, o = cut(o, PH, 20)
        c8, o = cut(o, PH, 8)
        zsum, o = cut(o, PH)
        rz, o = cut(o, PH)
        thr, o = cut(o, 2, PH)
        Pm, o = cut(o, NPS, NE)
        Mm, o = cut(o, NMS, NE)
        G5, o = cut(o, 2, NE)
        cg, o = cut(o, NE)
        assert o <= 26000, o
        MERGED = [7]
        UNITS = [h for h in range(PH) if h + 1 not in MERGED]
        NU = len(UNITS)
        AT_COMB, AT_CAND = 1, 2
        OUT_AT = 1

        def grid(buf, slot):
            return buf[:, slot, :].rearrange("p (i j) -> p i j", j=NK)

        def ex_rows(par, h):
            return exs[:, par, h * NK:(h + 1) * NK].unsqueeze(2).to_broadcast([P, NK, NK])

        def ey_cols(par, h):
            at = (PH + h) * NK
            return E5[:, par, at:at + NK].unsqueeze(1).to_broadcast([P, NK, NK])

        keysn, o = cut(20000, 4, P)
        keysT, o = cut(o, 512)
        wqn, o = cut(o, 16, P)
        kinn, o = cut(o, NCH, P)

        block = ctx.enter_context(nc.Block())

        NWF, NW = 14, 25
        SET_W2O = 3 + JPE
        SET_FFN = SET_W2O + 2
        SET_W1T = SET_FFN + 3
        SET_KEYS = SET_W1T + 1
        SET_ALL = SET_KEYS + 3

        @block.sync
        def _(sp):
            xv = A["L0_attn_x"].rearrange("b (c p) d -> p (b c) d", p=P)

            def load_ffn(dst, src):
                sp.dma_start(dst, src).then_inc(s_wf, 16)

            def load(dst, src):
                sp.dma_start(dst, src).then_inc(s_w, 16)

            for g in range(NG):
                sp.dma_start(x_sb[:, g * GT:(g + 1) * GT, :], xv[:, g * GT:(g + 1) * GT, :]).then_inc(s_x, 16)
            sp.dma_start(ident[:, :], A["c_ident"]).then_inc(s_id, 16)
            for r in range(2):
                half = slice(r * M_FF, (r + 1) * M_FF)
                load_ffn(win2[:, r, :], A["L0_ffn_Win"])
                load_ffn(bin2[half, :], A["L0_ffn_bin_"].rearrange("(m o) -> m o", o=1))
                load_ffn(w1c[half, :], A["L0_ffn_W1"].rearrange("m (r j) -> r m j", r=2)[r])
                load_ffn(b1c[half, :], A["L0_ffn_b1"].rearrange("m (r j) -> r m j", r=2)[r])
                load_ffn(w2c[half, :], A["L0_ffn_W2"].rearrange("m (r j) -> r m j", r=2)[r])
                load_ffn(wout2[half, :], A["L0_ffn_Wout"])
            load_ffn(b2c[:, :], A["L0_ffn_b2"].rearrange("(m o) -> m o", o=1))
            load_ffn(bout_bc[:, :], A["L0_ffn_bout"].rearrange("(o d) -> o d", o=1).to_broadcast([P, D]))
            for dst, name in ((bproj_bc, "L0_attn_b_proj"), (bq_bc, "L1_attn_bq"), (bv_bc, "L1_attn_bv"),
                              (bo_bc, "L1_attn_bo")):
                load(dst[:, :], A[name].rearrange("(o d) -> o d", o=1).to_broadcast([P, D]))
            load(hmask[:, :], A["c_hmask"])
            load(upper[:, :], A["c_upper"])
            load(slots[:, :], A["c_slots"].rearrange("(o d) -> o d", o=1).to_broadcast([P, SLOTS]))
            load(vmask[:, :], A["c_vmask"])
            load(headsel[:, :, :], A["c_headsel"])
            load(wqkv[:, :], A["L0_attn_W_qkv"])
            load(wproj[:, :], A["L0_attn_W_proj"])
            for dst, name in ((gcol, "L0_attn_ln_gamma"), (bcol, "L0_attn_ln_beta")):
                load(dst[:, :], A[name].rearrange("(o d e) -> o d e", o=1, e=1).to_broadcast([HEADS, HD, 1]))
            for i, name in enumerate(("Wq", "Wk", "Wv", "Wo")):
                load(w1nat[:, i, :], A[f"L1_attn_{name}"])
            load(bqc[:, :], A["L1_attn_bq"].rearrange("(m o) -> m o", o=1))
            load(bkc[:, :], A["L1_attn_bk"].rearrange("(m o) -> m o", o=1))
            load(pg[:, :], A["L1_ffn_gamma"].rearrange("(m o) -> m o", o=1))
            load(pb_[:, :], A["L1_ffn_beta"].rearrange("(m o) -> m o", o=1))
            load(keysn, A["L1_ffn_keys"].rearrange("h k p d -> (h k p) d").rearrange("(c q) d -> q c d", q=P))
            load(wqn, A["L1_ffn_w_q"].rearrange("(c q) d -> q c d", q=P))
            load(kinn, A["L1_ffn_key_in"].rearrange("(c q) d -> q c d", q=P))
            load(kout[:, :, :], A["L1_ffn_key_out"].rearrange("(c q) d -> q c d", q=P))
            ov = out.rearrange("b (c p) d -> p (b c) d", p=P)
            sp.wait_ge(*last_x[STAGES])
            for g in range(4):
                sp.dma_start(ov[:, g * 8:(g + 1) * 8, :], x_sb[:, g * 8:(g + 1) * 8, :]).then_inc(s_out, 16)
            sp.wait_ge(s_out, 64)


        @block.gpsimd
        def _(pool):
            def add_row(row, done):
                with pool.Fori(0, NG) as g:
                    xg = x_sb[:, bass.ds(g * GT, GT), :]
                    nc.gpsimd.tensor_tensor(xg, xg, row[:, :].unsqueeze(1).to_broadcast([P, GT, D]),
                                            ALU.add).then_inc(done, 1)

            def head_keys_0(s):
                def pair(u, par):
                    pool.wait_ge(s["kT"], u + 1)
                    pool.sem_inc(s_go, 1)
                    for h in range(HEADS):
                        last = nc.gpsimd.tensor_scalar(kM0[:, HEADS * par + h, :], kR0, gk[:, h:h + 1],
                                                       bk16[:, h:h + 1], ALU.mult, ALU.add)
                    last.then_inc(s["kM"], 1)

                def slot(u, par):
                    if not (isinstance(u, int) and u < 2):
                        pool.wait_ge(s["v"], u - 1)
                    nc.gpsimd.tensor_copy(xs0[:, par, :], xT[:, bass.ds(u * SEQ, SEQ)]).then_inc(s["xs"], 1)

                slot(0, 0)
                slot(1, 1)
                pair(0, 0)
                slot(2, 0)
                with pool.Fori(0, NP_ // 2 - 2) as i:
                    pair(2 * i + 1, 1)
                    slot(2 * i + 3, 1)
                    pair(2 * i + 2, 0)
                    slot(2 * i + 4, 0)
                pair(NP_ - 3, 1)
                slot(NP_ - 1, 1)
                pair(NP_ - 2, 0)
                pair(NP_ - 1, 1)

            def values(s):
                nc.gpsimd.tensor_copy(xs1, xT[:, 0:SEQ]).then_inc(s["xs"], 1)
                with pool.Fori(1, NP_) as b:
                    pool.wait_ge(s["qv"], b)
                    nc.gpsimd.tensor_copy(xs1, xT[:, bass.ds(b * SEQ, SEQ)]).then_inc(s["xs"], 1)

            def product_keys(s, f):
                base = f * NT

                def tile(n, par):
                    pool.wait_ge(s["sc"], 2 * (base + n) + 2)
                    for h in range(PH):
                        pool.wait_ge(s["M"], 8 * (base + n) + h + 9 - NPS)
                        nc.gpsimd.tensor_tensor(grid(Pm, h % NPS), ex_rows(par, h), ey_cols(par, h),
                                                ALU.mult).then_inc(s["P"], 1)

                tile(0, 0)
                with pool.Fori(0, NT // 2 - 1) as i:
                    tile(2 * i + 1, 1)
                    tile(2 * i + 2, 0)
                tile(NT - 1, 1)

            for k in range(STAGES):
                s = pr
                pool.wait_ge(s["tr"], 2 + (k + 1) * NG)
                if k == 0 or k == 2:
                    pool.wait_ge(s_set, SET_FFN)
                    add_row(ffn_add, ff["cb"])
                if k == 1:
                    pool.wait_ge(s_w, 16 * NW)
                    add_row(bproj_bc, L0["cb"])
                    pool.wait_ge(s["ev"], 2 + (k + 1) * NG)
                    head_keys_0(L0)
                if k == 4:
                    add_row(bo_bc, L1["cb"])
                    pool.wait_ge(s["ev"], 2 + (k + 1) * NG)
                    values(L1)
                if k == 3 or k == 5:
                    product_keys(pk, (k - 3) // 2)


        @block.vector
        def _(dve):
            dve.sem_inc(pk["M"], 8)
            dve.sem_inc(pk["x"], 1)
            dve.sem_inc(pk["ys"], len(MERGED))
            dve.sem_inc(pk["cg"], 2)
            dve.sem_inc(ff["x"], 2)
            dve.sem_inc(L0["sub"], 4)
            dve.sem_inc(L0["on"], 1)
            dve.sem_inc(L1["x"], 1)

            def setup_ffn():
                dve.wait_ge(s_wf, 16 * NWF)
                nc.vector.tensor_scalar(b1e[:, :], w1c[:, :], bin2[:, 0:1], None, ALU.mult).then_inc(s_set, 1)
                dve.wait_ge(s_set, 1)
                nc.vector.tensor_tensor(b1e[:, :], b1e[:, :], b1c[:, :], ALU.add).then_inc(s_set, 1)
                nc.vector.tensor_copy(b2r[:, :], b2c[:, 0:1].to_broadcast([M_FF, P])).then_inc(s_set, 1)
                for j in range(JPE):
                    nc.vector.tensor_scalar(w2o[:, j, :], wout2[:, :], w2c[:, j:j + 1], None,
                                            ALU.mult).then_inc(s_set, 1)
                dve.wait_ge(s_ps, 1)
                nc.vector.tensor_tensor(ffn_add[:, :], bank[0][:, 0:D], bout_bc[:, :], ALU.add).then_inc(s_set, 1)
                dve.wait_ge(s_set, SET_FFN - 1)
                nc.vector.tensor_scalar(ffn_add[:, :], ffn_add[:, :], 0.5, None, ALU.mult).then_inc(s_set, 1)

            def setup_rest():
                dve.wait_ge(s_w, 16 * NW)
                nc.vector.tensor_scalar(gk[:, :], hmask[:, :], gcol[:, 0:1], None, ALU.mult).then_inc(s_set, 1)
                nc.vector.tensor_scalar(bk16[:, :], hmask[:, :], bcol[:, 0:1], None, ALU.mult).then_inc(s_set, 1)
                dve.wait_ge(s_ps, 2)
                nc.vector.tensor_copy(w1T[:, :, :].rearrange("p a b -> p (a b)"), bank[1][:, :]).then_inc(s_set, 1)
                nc.vector.tensor_copy(keysT, bank[2][:, :]).then_inc(s_set, 1)
                nc.vector.tensor_copy(kinT[:, 0:512], bank[3][:, :]).then_inc(s_set, 1)
                nc.vector.tensor_copy(kinT[:, 512:1024], bank[4][:, :]).then_inc(s_set, 1)
                dve.wait_ge(s_ps, 3)
                nc.vector.tensor_copy(weff[:, :, :, :].rearrange("p a b c -> p (a b c)"),
                                      bank[5][:, :]).then_inc(s_set, 1)
                dve.wait_ge(s_set, SET_ALL)

            def statistics(first, count, s, updated):
                dve.wait_ge(s["x"], updated)
                dve.sem_inc(s_go, 1)
                for t in range(count):
                    nc.vector.bn_stats(stats[:, bass.ds(first + t, 1), :],
                                       x_sb[:, bass.ds(first + t, 1), :]).then_inc(pr["stat"], 1)

            def prep(k):
                s, base = pr, k * NG
                if k == 0:
                    dve.wait_ge(s_x, 16 * NG)
                    with dve.Fori(0, NT) as n:
                        nc.vector.bn_stats(stats[:, bass.ds(n, 1), :], x_sb[:, bass.ds(n, 1), :]).then_inc(s["stat"], 1)
                dve.wait_ge(s["stat"], (k + 1) * NT)
                even, odd = stats[:, :, 1], stats[:, :, 4]
                nc.vector.tensor_tensor(negmean[:, :], even, odd, ALU.add).then_inc(s["aggr"], 1)
                nc.vector.tensor_tensor(mdiff[:, :], even, odd, ALU.subtract).then_inc(s["aggr"], 1)
                nc.vector.tensor_tensor(vareps[:, :], stats[:, :, 2], stats[:, :, 5], ALU.add).then_inc(s["aggr"], 1)
                dve.wait_ge(s["aggr"], 3 * (k + 1))
                nc.vector.tensor_scalar(negmean[:, :], negmean[:, :], -0.5, None, ALU.mult).then_inc(s["nm"], 1)
                nc.vector.scalar_tensor_tensor(mdiff[:, :], mdiff[:, :], 0.25, mdiff[:, :], ALU.mult,
                                               ALU.mult).then_inc(s["sq"], 1)
                nc.vector.tensor_scalar(vareps[:, :], vareps[:, :], 1.0 / D, LN_EPS, ALU.mult,
                                        ALU.add).then_inc(s["sq"], 1)
                dve.wait_ge(s["sq"], 2 * (k + 1))
                nc.vector.tensor_tensor(vareps[:, :], vareps[:, :], mdiff[:, :], ALU.add).then_inc(s["ve"], 1)
                dve.wait_ge(s["sd"], k + 1)
                nc.vector.reciprocal(rstd[:, :], stdev[:, :]).then_inc(s["rstd"], 1)
                dve.wait_ge(s["rstd"], k + 1)
                dve.wait_ge(s["nm"], k + 1)

                def normalise(n, par):
                    dve.wait_ge(s["tr"], base + n + 1)
                    for t in range(GT):
                        c = n * GT + t
                        last = nc.vector.tensor_scalar(xn[:, par, t, :], x_sb[:, bass.ds(c, 1), :],
                                                       negmean[:, bass.ds(c, 1)], rstd[:, bass.ds(c, 1)],
                                                       ALU.add, ALU.mult)
                    last.then_inc(s["xn"], 1)

                with dve.Fori(0, NG // 2) as i:
                    for par in range(2):
                        normalise(2 * i + par, par)

            def ffn(s, f):
                base = f * NG

                def sums(g, par):
                    if not (isinstance(g, int) and g < 2 and f == 0):
                        dve.wait_ge(s["o"], base + g + 1)
                    for i in range(NJ - JPE):
                        j = JPE + i
                        dve.wait_ge(s["h"], NJ * (base + g) + i + 1)
                        if i == 0:
                            nc.vector.tensor_scalar(hsum[:, par, :], h_ff[:, par, j, :], w2c[:, j:j + 1], None,
                                                    ALU.mult).then_inc(s["hs"], 1)
                        else:
                            dve.wait_ge(s["hs"], (NJ - JPE) * (base + g) + i)
                            nc.vector.scalar_tensor_tensor(hsum[:, par, :], h_ff[:, par, j, :], w2c[:, j:j + 1],
                                                           hsum[:, par, :], ALU.mult, ALU.add).then_inc(s["hs"], 1)

                def update(g, par):
                    dve.wait_ge(s["o"], base + g + 3)
                    dve.wait_ge(s["cb"], base + g + 1)
                    xg = x_sb[:, bass.ds(g * GT, GT), :].rearrange("p a b -> p (a b)")
                    nc.vector.scalar_tensor_tensor(xg, bank[4 + par][:, :], 0.5, xg, ALU.mult,
                                                   ALU.add).then_inc(s["x"], 1)
                    statistics(g * GT, GT, s, base + g + 3)

                sums(0, 0)
                with dve.Fori(0, NG // 2 - 1) as i:
                    sums(2 * i + 1, 1)
                    update(2 * i, 0)
                    sums(2 * i + 2, 0)
                    update(2 * i + 1, 1)
                sums(NG - 1, 1)
                update(NG - 2, 0)
                update(NG - 1, 1)

            def l0(s):
                for par in range(2):
                    last = nc.vector.tensor_copy(Vb0[:, par, :, :, HD],
                                                 vmask[:, :].unsqueeze(1).to_broadcast([P, 32, 2]))
                last.then_inc(s["vb"], 1)
                qc = qc0.rearrange("p (h d) -> p h d", d=HD)

                def centre(u):
                    dve.wait_ge(s["qk"], u + 1)
                    qk = bank[4][:, :].rearrange("p (h d) -> p h d", d=HD)
                    nc.vector.tensor_reduce(sum0, qk, X, ALU.add).then_inc(s["rsum"], 1)
                    dve.wait_ge(s["rsum"], 2 * u + 1)
                    nc.vector.scalar_tensor_tensor(qc, sum0.unsqueeze(2).to_broadcast([P, 64, HD]), -1.0 / HD, qk,
                                                   ALU.mult, ALU.add).then_inc(s["cent"], 1)

                def variance(u):
                    dve.wait_ge(s["sq"], u + 1)
                    nc.vector.tensor_reduce(var0, sq0.rearrange("p (h d) -> p h d", d=HD), X,
                                            ALU.add).then_inc(s["rsum"], 1)
                    dve.wait_ge(s["rsum"], 2 * u + 2)
                    nc.vector.tensor_scalar(var0, var0, 1.0 / HD, LN_EPS, ALU.mult, ALU.add).then_inc(s["var"], 1)

                def scale(u):
                    dve.wait_ge(s["sd"], u + 1)
                    nc.vector.reciprocal(rs0, sd0).then_inc(s["rs"], 1)
                    dve.wait_ge(s["rs"], u + 1)
                    nc.vector.tensor_tensor(qn0.rearrange("p a (h d) -> p (a h) d", d=HD), qc,
                                            rs0.unsqueeze(2).to_broadcast([P, 64, HD]), ALU.mult).then_inc(s["qn"], 1)

                def values(u, par):
                    dve.wait_ge(s["v"], u + 1)
                    vps = bank[4][:, :].rearrange("p (w r d) -> p w r d", r=2, d=HD)
                    for r in range(2):
                        last = nc.vector.tensor_scalar(Vb0[:, par, :, r, 0:HD], vps[:, :, r, :], vmask[:, r:r + 1],
                                                       None, ALU.mult)
                    last.then_inc(s["vb"], 1)

                def queries(u, par):
                    dve.wait_ge(s["qt"], u + 1)
                    nc.vector.tensor_scalar(qT0[:, par, :], bank[4][:, 0:2 * P], gcol[:, 0:1], bcol[:, 0:1], ALU.mult,
                                            ALU.add).then_inc(s["qT"], 1)

                def less_max(u, t):
                    for hh in range(2):
                        at = 4 * u + 2 * t + hh
                        dve.wait_ge(s["st"], at + 1)
                        sv = bank[2 * t + hh][:, :].rearrange("p (h k) -> p h k", k=WIN)
                        nc.vector.tensor_reduce(mx0[:, 2 * t + hh, :], sv, X, ALU.max).then_inc(s["mx"], 1)
                    for hh in range(2):
                        at = 4 * u + 2 * t + hh
                        sv = bank[2 * t + hh][:, :].rearrange("p (h k) -> p h k", k=WIN)
                        dve.wait_ge(s["mx"], at + 1)
                        if not (isinstance(u, int) and u == 0):
                            dve.wait_ge(s["pt"], at - 3)
                        nc.vector.tensor_tensor(E0[:, t, hh, :].rearrange("p (h k) -> p h k", k=WIN), sv,
                                                mx0[:, 2 * t + hh, :].unsqueeze(2).to_broadcast([P, 8, WIN]),
                                                ALU.subtract).then_inc(s["sub"], 1)

                def normalise(u):
                    dve.wait_ge(s["pv"], 2 * u + 4)
                    ov = bank[7][:, 0:288].rearrange("p (t h e) -> p t h e", t=2, e=HD + 1)
                    nc.vector.reciprocal(rec0, ov[:, :, :, HD]).then_inc(s["rec"], 1)
                    dve.wait_ge(s["rec"], u + 1)
                    for t in range(2):
                        last = nc.vector.tensor_tensor(on0[:, t, :].rearrange("p (h d) -> p h d", d=HD),
                                                       ov[:, t, :, 0:HD],
                                                       rec0[:, t, :].unsqueeze(2).to_broadcast([P, HEADS, HD]),
                                                       ALU.mult)
                    last.then_inc(s["on"], 1)

                def update(u):
                    dve.wait_ge(s["y"], u + 1)
                    xu = x_sb[:, bass.ds(2 * u, 2), :].rearrange("p a b -> p (a b)")
                    nc.vector.tensor_tensor(xu, bank[6][:, 0:2 * P], xu, ALU.add).then_inc(s["x"], 1)
                    statistics(2 * u, 2, s, u + 1)

                def pair(u, par, back=True, one=True, two=True):
                    if back:
                        normalise(u - 1)
                    less_max(u, 1)
                    if two:
                        centre(u + 2)
                    if one:
                        values(u + 1, 1 - par)
                    if back:
                        update(u - 1)
                    if two:
                        variance(u + 2)
                    if two:
                        scale(u + 2)
                        queries(u + 2, par)
                    if one:
                        less_max(u + 1, 0)

                centre(0)
                variance(0)
                scale(0)
                values(0, 0)
                queries(0, 0)
                centre(1)
                variance(1)
                scale(1)
                queries(1, 1)
                less_max(0, 0)
                pair(0, 0, back=False)
                with dve.Fori(0, NP_ // 2 - 2) as i:
                    pair(2 * i + 1, 1)
                    pair(2 * i + 2, 0)
                pair(NP_ - 3, 1)
                pair(NP_ - 2, 0, two=False)
                pair(NP_ - 1, 1, one=False, two=False)
                normalise(NP_ - 1)
                update(NP_ - 1)

            def l1(s):
                for half in range(2):
                    dve.wait_ge(s["pn"], half + 1)
                    nc.vector.tensor_copy(n2[:, half, :], bank[2 + half][:, 0:SEQ]).then_inc(s["nc"], 1)
                rounds = -(-TOP_U // 8)
                for r in range(rounds):
                    for half in range(2):
                        src = n2 if r == 0 else n2w
                        dve.wait_ge(s["nc"], half + 1)
                        if r:
                            dve.wait_ge(s["mr"], 4 * r - 2 + half + 1)
                        nc.vector.max(m8[:, half, :], src[:, half, :]).then_inc(s["mr"], 1)
                    if r < rounds - 1:
                        for half in range(2):
                            dve.wait_ge(s["mr"], 4 * r + half + 1)
                            nc.vector.match_replace(n2w[:, half, :], m8[:, half, :], (n2 if r == 0 else n2w)[:, half, :],
                                                    -1.0).then_inc(s["mr"], 1)
                dve.wait_ge(s["mr"], 4 * (rounds - 1) + 2)
                rank = (TOP_U - 1) % 8
                for half in range(2):
                    nc.vector.tensor_scalar(selT[:, half, :], n2[:, half, :], m8[:, half, rank:rank + 1], None,
                                            ALU.is_ge).then_inc(s["selT"], 1)
                dve.wait_ge(s["str"], 1)
                nc.vector.tensor_copy(sel.rearrange("p a b c -> p (a b c)"), bank[4][:, :]).then_inc(s["sel"], 1)
                nc.vector.memset(ones, 1.0).then_inc(s["sel"], 1)
                nc.vector.memset(Vs1[:, :, :, HD], 1.0).then_inc(s["vb"], 1)
                dve.wait_ge(s["sel"], 2)
                dve.wait_ge(s["rm"], 1)
                for c in range(2):
                    nc.vector.tensor_tensor(rk[:, c, :], bank[c][:, 0:BATCH * HEADS],
                                            sel[:, c, :, :].rearrange("p a b -> p (a b)"), ALU.mult).then_inc(s["mr"], 1)
                dve.wait_ge(s["mr"], 4 * (rounds - 1) + 4)
                for c in range(2):
                    nc.vector.tensor_scalar(rk[:, c, :], rk[:, c, :], -1.0, None, ALU.add).then_inc(s["rk"], 1)

                def project(b, par):
                    dve.wait_ge(s["qv"], b + 1)
                    qv = bank[7][:, :].rearrange("p (c j d) -> p c j d", c=2, j=2)
                    nc.vector.tensor_tensor(Qn, qv[:, :, 0, :], bq_bc[:, :].unsqueeze(1).to_broadcast([P, 2, D]),
                                            ALU.add).then_inc(s["Qn"], 1)
                    for c in range(2):
                        last = nc.vector.tensor_tensor(Vs1[:, 2 * par + c, :, 0:HD],
                                                       qv[:, c, 1, :].rearrange("p (h d) -> p h d", d=HD),
                                                       bv_bc[:, :].rearrange("p (h d) -> p h d", d=HD), ALU.add)
                    last.then_inc(s["vb"], 1)

                def one_hot(b, par):
                    for c in range(2):
                        last = nc.vector.tensor_tensor(
                            S1[:, par, c, :].rearrange("p (h s) -> p h s", s=SLOTS),
                            slots[:, :].unsqueeze(1).to_broadcast([P, HEADS, SLOTS]),
                            rk[:, c, bass.ds(b * HEADS, HEADS)].unsqueeze(2).to_broadcast([P, HEADS, SLOTS]),
                            ALU.is_equal)
                    last.then_inc(s["S"], 1)

                def gathered(b):
                    for i in range(2):
                        dve.wait_ge(s["g"], 2 * b + i + 1)
                        nc.vector.scalar_tensor_tensor(
                            QM1[:, 512 * i:512 * (i + 1)].rearrange("p (h s) -> p h s", s=SLOTS),
                            bank[4 + i][:, :].rearrange("p (h s) -> p h s", s=SLOTS), HD ** -0.5,
                            hmask[:, 8 * i:8 * i + 8].unsqueeze(2).to_broadcast([P, 8, SLOTS]),
                            ALU.mult, ALU.mult).then_inc(s["QM"], 1)

                def maxima(b):
                    for i in range(4):
                        dve.wait_ge(s["sc"], 4 * b + i + 1)
                        nc.vector.tensor_reduce(mx1[:, 2 * i:2 * i + 2],
                                                bank[i][:, :].rearrange("p (g k) -> p g k", k=SEQ), X,
                                                ALU.max, negate=True).then_inc(s["mx"], 1)

                def evacuate_slots(b):
                    for i in range(4):
                        dve.wait_ge(s["sT"], 4 * b + i + 1)
                        nc.vector.tensor_copy(ST1[:, 2 * i:2 * i + 2, :].rearrange("p a b -> p (a b)"),
                                              bank[4 + i % 2][:, :]).then_inc(s["sTe"], 1)

                def normalise(b):
                    dve.wait_ge(s["pv"], b + 1)
                    ov = bank[6][:, 0:PAIRS * 18].rearrange("p (g r e) -> p g r e", g=PAIRS, e=HD + 1)
                    nc.vector.reciprocal(rec1, ov[:, :, :, HD]).then_inc(s["rec"], 1)
                    dve.wait_ge(s["rec"], 2 * b + 1)
                    nc.vector.tensor_tensor(rec1, rec1, vmask[:, :].unsqueeze(1).to_broadcast([P, PAIRS, 2]),
                                            ALU.mult).then_inc(s["rec"], 1)
                    dve.wait_ge(s["rec"], 2 * b + 2)
                    nc.vector.tensor_tensor(O1, ov[:, :, :, 0:HD], rec1.unsqueeze(3).to_broadcast([P, PAIRS, 2, HD]),
                                            ALU.mult).then_inc(s["on"], 1)

                def outputs(b):
                    dve.wait_ge(s["sca"], b + 1)
                    nc.vector.tensor_copy(on1.rearrange("p a b -> p (a b)"), bank[7][:, 0:2 * P]).then_inc(s["oe1"], 1)

                def update(b):
                    dve.wait_ge(s["y"], b + 1)
                    xu = x_sb[:, bass.ds(2 * b, 2), :].rearrange("p a b -> p (a b)")
                    nc.vector.tensor_tensor(xu, bank[7][:, 0:2 * P], xu, ALU.add).then_inc(s["x"], 1)
                    statistics(2 * b, 2, s, b + 2)

                def sequence(b, par, first=False, last=False, ahead=True):
                    maxima(b)
                    if not first:
                        outputs(b - 1)
                    evacuate_slots(b)
                    if not last:
                        project(b + 1, 1 - par)
                    if not first:
                        update(b - 1)
                    if not last:
                        gathered(b + 1)
                    normalise(b)
                    if ahead:
                        one_hot(b + 2, par)

                dve.wait_ge(s["rk"], 2)
                project(0, 0)
                one_hot(0, 0)
                one_hot(1, 1)
                gathered(0)
                sequence(0, 0, first=True)
                with dve.Fori(0, NP_ // 2 - 2) as i:
                    sequence(2 * i + 1, 1)
                    sequence(2 * i + 2, 0)
                sequence(NP_ - 3, 1)
                sequence(NP_ - 2, 0, ahead=False)
                sequence(NP_ - 1, 1, last=True, ahead=False)
                outputs(NP_ - 1)
                update(NP_ - 1)

            def product_keys(s, f):
                base = f * NT
                dve.wait_ge(pr["ev"], 2 + (2 * f + 4) * NG)
                for g in range(NG):
                    last = nc.vector.bn_stats(bnst[:, g, :], xT[:, g * GW:(g + 1) * GW])
                last.then_inc(s["bst"], 1)
                dve.wait_ge(s["bst"], f + 1)
                nc.vector.bn_aggr(bnmv, bnst.rearrange("p a b -> p (a b)")).then_inc(s["bag"], 1)
                dve.wait_ge(s["bag"], f + 1)
                nc.vector.tensor_scalar(bnve, bnmv[:, 1:2], LN_EPS, None, ALU.add).then_inc(s["bve"], 1)
                dve.wait_ge(s["bsd"], f + 1)
                nc.vector.reciprocal(bnrs, bnsd).then_inc(s["brs"], 1)
                dve.wait_ge(s["brs"], 2 * f + 1)
                nc.vector.tensor_tensor(bna, pg[:, :], bnrs, ALU.mult).then_inc(s["bsc"], 1)
                dve.wait_ge(s["bsc"], 2 * f + 1)
                nc.vector.tensor_tensor(bnrs, bnmv[:, 0:1], bna, ALU.mult).then_inc(s["brs"], 1)
                dve.wait_ge(s["brs"], 2 * f + 2)
                nc.vector.tensor_tensor(bnb, pb_[:, :], bnrs, ALU.subtract).then_inc(s["bsc"], 1)

                def best8(n):
                    dve.wait_ge(s["sim"], base + n + 3)
                    dve.sem_inc(s_go, 1)
                    for c in range(2 * PH):
                        last = nc.vector.max(m8raw[:, c, :], bank[0][:, c * NK:(c + 1) * NK])
                    last.then_inc(s["m8"], 1)

                def less_best(n, par):
                    dve.wait_ge(s["m8"], base + n + 1)
                    first = m8raw[:, :, 0:1]
                    nc.vector.tensor_tensor(E5[:, par, 0:512].rearrange("p (c k) -> p c k", k=NK),
                                            bank[0][:, :].rearrange("p (c k) -> p c k", k=NK),
                                            first.to_broadcast([P, 2 * PH, NK]), ALU.subtract).then_inc(s["sub"], 1)
                    nc.vector.tensor_tensor(E5[:, par, 512:640].rearrange("p (c k) -> p c k", k=8), m8raw,
                                            first.to_broadcast([P, 2 * PH, 8]), ALU.subtract).then_inc(s["sub"], 1)

                def candidates(n, par):
                    dve.wait_ge(s["ex"], base + n + 1)
                    e8 = E5[:, par, 512:640].rearrange("p (q h k) -> p q h k", q=2, k=8)
                    x8, y8 = e8[:, 0], e8[:, 1]

                    def rank_products(at, a, na, b, nb):
                        m = max(na, nb)
                        xa = x8[:, :, a:a + na].to_broadcast([P, PH, m]) if na < m else x8[:, :, a:a + na]
                        yb = y8[:, :, b:b + nb].to_broadcast([P, PH, m]) if nb < m else y8[:, :, b:b + nb]
                        return nc.vector.tensor_tensor(cand[:, :, at:at + m], xa, yb, ALU.mult)

                    rank_products(0, 0, 1, 0, 8)
                    rank_products(8, 1, 1, 0, 4)
                    rank_products(12, 2, 6, 0, 1)
                    rank_products(18, 2, 2, 1, 1).then_inc(s["cand"], 1)

                def picks(n):
                    dve.wait_ge(s["cand"], base + n + 1)
                    dve.sem_inc(s_go, 1)
                    for h in range(PH):
                        last = nc.vector.max(c8[:, h, :], cand[:, h, :])
                    last.then_inc(s["c8"], 1)

                def total(n):
                    dve.wait_ge(s["c8"], base + n + 1)
                    nc.vector.tensor_reduce(zsum, c8, X, ALU.add).then_inc(s["z"], 1)

                def inverse(n):
                    dve.wait_ge(s["z"], base + n + 1)
                    nc.vector.reciprocal(rz, zsum).then_inc(s["rz"], 1)

                def scale(n, par):
                    dve.wait_ge(s["rz"], base + n + 1)
                    nc.vector.tensor_tensor(exs[:, par, :].rearrange("p (h k) -> p h k", k=NK),
                                            E5[:, par, 0:256].rearrange("p (h k) -> p h k", k=NK),
                                            rz.unsqueeze(2).to_broadcast([P, PH, NK]), ALU.mult).then_inc(s["sc"], 1)
                    nc.vector.scalar_tensor_tensor(thr[:, par, :], c8[:, :, 7], 1.0 - 5e-7, rz, ALU.mult,
                                                   ALU.mult).then_inc(s["sc"], 1)

                def combine(m, par):
                    dve.wait_ge(s["acc"], NU * (base + m + 2))
                    for half in range(2):
                        c = slice(half * 512, (half + 1) * 512)
                        dve.wait_ge(s["g"], 2 * (base + m) + half + 2)
                        nc.vector.tensor_tensor(cg[:, c], bank[2 + 2 * par + half][:, :], G5[:, par, c],
                                                ALU.mult).then_inc(s["cg"], 1)

                def update(m):
                    dve.wait_ge(s["y"], base + m + 1)
                    xm = x_sb[:, bass.ds(m, 1), :].rearrange("p a b -> p (a b)")
                    nc.vector.scalar_tensor_tensor(xm, bank[7][:, 0:D], 0.5, xm, ALU.mult, ALU.add).then_inc(s["x"], 1)

                def tile(n, par, front=True, finish=True, ahead=True):
                    dve.wait_ge(s["sc"], 2 * (base + n) + 2)
                    for h in range(PH):
                        dve.wait_ge(s["P"], PH * (base + n) + h + 1)
                        if h in UNITS:
                            dve.wait_ge(s["acc"], NU * (base + n) + UNITS.index(h) + 1)
                        else:
                            dve.wait_ge(s["ys"], len(MERGED) * (base + n) + MERGED.index(h + 1) + 1)
                        nc.vector.scalar_tensor_tensor(Mm[:, h % NMS, :], Pm[:, h % NPS, :], thr[:, par, h:h + 1],
                                                       Pm[:, h % NPS, :], ALU.is_ge, ALU.mult).then_inc(s["M"], 1)
                        if h in MERGED:
                            dve.wait_ge(s["M"], 8 * (base + n) + h + 9)
                            nc.vector.tensor_tensor(Mm[:, h % NMS, :], Mm[:, h % NMS, :], Mm[:, (h - 1) % NMS, :],
                                                    ALU.add).then_inc(s["ys"], 1)
                        if front:
                            if h == 0:
                                less_best(n + 1, 1 - par)
                            if h == AT_CAND:
                                candidates(n + 1, 1 - par)
                            if h == AT_CAND + 1:
                                picks(n + 1)
                            if h == AT_CAND + 2:
                                total(n + 1)
                            if h == AT_CAND + 3:
                                inverse(n + 1)
                            if h == AT_CAND + 4:
                                scale(n + 1, 1 - par)
                        if finish:
                            if h == AT_COMB:
                                combine(n - 1, 1 - par)
                            if h == AT_CAND + 3:
                                update(n - 1)
                            if h == AT_CAND + 4 and f == 0:
                                statistics(n - 1, 1, s, n + 1)
                    if ahead:
                        best8(n + 2)

                best8(0)
                less_best(0, 0)
                candidates(0, 0)
                picks(0)
                total(0)
                inverse(0)
                scale(0, 0)
                best8(1)
                tile(0, 0, finish=False)
                with dve.Fori(0, NT // 2 - 2) as i:
                    tile(2 * i + 1, 1)
                    tile(2 * i + 2, 0)
                tile(NT - 3, 1)
                tile(NT - 2, 0, ahead=False)
                tile(NT - 1, 1, front=False, ahead=False)
                combine(NT - 1, 1)
                update(NT - 1)
                if f == 0:
                    statistics(NT - 1, 1, s, NT + 1)

            for k in range(STAGES):
                prep(k)
                if k == 0:
                    setup_ffn()
                if k == 1:
                    setup_rest()
                if k in (0, 2):
                    ffn(ff, k // 2)
                if k == 1:
                    l0(L0)
                if k == 4:
                    l1(L1)
                if k in (3, 5):
                    product_keys(pk, (k - 3) // 2)

        @block.scalar
        def _(act):
            def prep(k):
                s, base = pr, k * NG
                act.wait_ge(s["ve"], k + 1)
                nc.scalar.activation(stdev[:, :], vareps[:, :], ACT.Sqrt).then_inc(s["sd"], 1)
                with act.Fori(0, NG // 2) as i:
                    for par in range(2):
                        n = 2 * i + par
                        act.wait_ge(s["tr"], base + n + 3)
                        nc.scalar.activation(xT[:, bass.ds(n * GW, GW)], bank[6 + par][:, :],
                                             ACT.Copy).then_inc(s["ev"], 1)

            def ffn(s, f):
                base = f * NG
                with act.Fori(0, NG // 2) as i:
                    for par in range(2):
                        g = 2 * i + par
                        act.wait_ge(s["s"], base + g + 1)
                        act.wait_ge(s["o"], base + g + 1)
                        for j in list(range(JPE, NJ)) + list(range(JPE)):
                            nc.scalar.activation(h_ff[:, par, j, :], bank[2 + par][:, :], ACT.Relu,
                                                 bias=b1e[:, j:j + 1], scale=w1c[:, j:j + 1]).then_inc(s["h"], 1)

            def l0(s):
                def squares(u):
                    act.wait_ge(s["cent"], u + 1)
                    nc.scalar.activation(sq0, qc0, ACT.Square).then_inc(s["sq"], 1)

                def roots(u):
                    act.wait_ge(s["var"], u + 1)
                    nc.scalar.activation(sd0, var0, ACT.Sqrt).then_inc(s["sd"], 1)

                def keys(u):
                    act.wait_ge(s["qT"], u + 1)
                    act.wait_ge(s["kM"], u)
                    nc.scalar.activation(kR0, bank[4][:, 2 * P:4 * P], ACT.Copy).then_inc(s["kT"], 1)

                def exponentials(u, t):
                    for hh in range(2):
                        act.wait_ge(s["sub"], 4 * u + 2 * t + hh + 5)
                        nc.scalar.activation(E0[:, t, hh, :], E0[:, t, hh, :], ACT.Exp).then_inc(s["ex"], 1)

                def evacuate(u, t):
                    for hh in range(2):
                        act.wait_ge(s["pt"], 4 * u + 2 * t + hh + 1)
                        act.wait_ge(s["pv"], 2 * u + t + 1)
                        at = 8 * t + 4 * hh
                        nc.scalar.activation(PT0[:, at:at + 4, :].rearrange("p a b -> p (a b)"),
                                             bank[5 + hh][:, :], ACT.Copy).then_inc(s["pe"], 1)

                def outputs(u):
                    act.wait_ge(s["ot"], u + 1)
                    nc.scalar.activation(oT0, bank[5][:, 0:2 * P], ACT.Copy).then_inc(s["oe"], 1)

                def pair(u, back=True, one=True, two=True):
                    evacuate(u, 0)
                    if back:
                        outputs(u - 1)
                    exponentials(u, 1)
                    if two:
                        squares(u + 2)
                        roots(u + 2)
                    evacuate(u, 1)
                    if two:
                        keys(u + 2)
                    if one:
                        exponentials(u + 1, 0)

                for u in range(2):
                    squares(u)
                    roots(u)
                    keys(u)
                exponentials(0, 0)
                pair(0, back=False)
                with act.Fori(0, NP_ // 2 - 2) as i:
                    pair(2 * i + 1)
                    pair(2 * i + 2)
                pair(NP_ - 3)
                pair(NP_ - 2, two=False)
                pair(NP_ - 1, one=False, two=False)
                outputs(NP_ - 1)

            def l1(s):
                with act.Fori(0, NP_ // 2) as i:
                    for par in range(2):
                        act.wait_ge(s["pq"], 2 * i + par + 1)
                        act.wait_ge(s["sq_used"], 2 * i + par + 1)
                        nc.scalar.activation(sq1[:, par, :], bank[par][:, 0:SEQ], ACT.Square,
                                             bias=bqc[:, 0:1]).then_inc(s["psq"], 1)

                def keys(b):
                    act.wait_ge(s["k"], b + 1)
                    nc.scalar.activation(kT1, bank[6][:, SEQ:2 * SEQ], ACT.Identity,
                                         bias=bkc[:, 0:1]).then_inc(s["kT"], 1)

                def exponentials(b):
                    for i in range(4):
                        act.wait_ge(s["mx"], 4 * b + i + 1)
                        for g in range(2 * i, 2 * i + 2):
                            last = nc.scalar.activation(E1[:, g, :], bank[i][:, (g % 2) * SEQ:(g % 2 + 1) * SEQ],
                                                        ACT.Exp, bias=mx1[:, g:g + 1])
                        last.then_inc(s["ex"], 1)

                def evacuate(b):
                    for i in range(4):
                        act.wait_ge(s["pt"], 4 * b + i + 1)
                        nc.scalar.activation(PT1[:, 2 * i:2 * i + 2, :, :].rearrange("p a b c -> p (a b c)"),
                                             bank[4 + i % 2][:, :], ACT.Copy).then_inc(s["pe"], 1)

                def outputs(b):
                    act.wait_ge(s["ot"], b + 1)
                    nc.scalar.activation(oT1.rearrange("p a b -> p (a b)"), bank[6][:, 0:2 * P],
                                         ACT.Copy).then_inc(s["oe"], 1)

                def sequence(b, first=False, last=False):
                    exponentials(b)
                    if not first:
                        outputs(b - 1)
                    if not last:
                        keys(b + 1)
                    evacuate(b)

                keys(0)
                sequence(0, first=True)
                with act.Fori(1, NP_ - 1) as b:
                    sequence(b)
                sequence(NP_ - 1, last=True)
                outputs(NP_ - 1)

            def product_keys(s, f):
                base = f * NT
                act.wait_ge(s["bve"], f + 1)
                nc.scalar.activation(bnsd, bnve, ACT.Sqrt).then_inc(s["bsd"], 1)

                def slots(m, par):
                    act.wait_ge(s["sim"], base + m + 1)
                    act.sem_inc(s_go, 1)
                    nc.scalar.activation(zT[:, par, :], xT[:, bass.ds(m * P, P)], ACT.Identity, bias=bnb[:, 0:1],
                                         scale=bna[:, 0:1]).then_inc(s["zt"], 1)

                def exponentials(m, par):
                    act.wait_ge(s["sub"], 2 * (base + m + 1))
                    nc.scalar.activation(E5[:, par, :], E5[:, par, :], ACT.Exp).then_inc(s["ex"], 1)

                def tile(n, par, front=True, ahead=True):
                    if ahead:
                        slots(n + 2, par)
                    if front:
                        exponentials(n + 1, 1 - par)
                    if not (f == 0 and isinstance(n, int) and n == 0):
                        act.wait_ge(s["cg"], 2 * (base + n))
                    for half in range(2):
                        act.wait_ge(s["o"], 2 * (base + n) + half + 1)
                        nc.scalar.activation(G5[:, par, half * 512:(half + 1) * 512], bank[6 if half else 1][:, :],
                                             ACT.Gelu).then_inc(s["g"], 1)

                act.wait_ge(s["bsc"], 2 * f + 2)
                slots(0, 0)
                slots(1, 1)
                exponentials(0, 0)
                tile(0, 0)
                with act.Fori(0, NT // 2 - 2) as i:
                    tile(2 * i + 1, 1)
                    tile(2 * i + 2, 0)
                tile(NT - 3, 1)
                tile(NT - 2, 0, ahead=False)
                tile(NT - 1, 1, front=False, ahead=False)

            act.sem_inc(L0["pe"], 2)
            act.sem_inc(pr["ev"], 2)
            act.sem_inc(pk["g"], 1)
            for k in range(STAGES):
                prep(k)
                if k == 0:
                    act.wait_ge(s_set, 2)
                if k in (0, 2):
                    ffn(ff, k // 2)
                if k == 1:
                    l0(L0)
                if k == 4:
                    l1(L1)
                if k in (3, 5):
                    product_keys(pk, (k - 3) // 2)

        @block.tensor
        def _(pe):
            def setup_ffn():
                pe.wait_ge(s_wf, 16 * NWF)
                pe.wait_ge(s_set, 3)
                nc.tensor.matmul(bank[0][:, 0:D], b2r[:, :], wout2[0:M_FF, :], start=True,
                                 stop=True).then_inc(s_ps, 1)
                pe.wait_ge(s_set, SET_W2O)

            def turn_weights():
                pe.wait_ge(s_w, 16 * NW)
                for i in range(4):
                    c = slice(i * P, (i + 1) * P)
                    nc.tensor.transpose(bank[1][:, c], w1nat[:, i, :], ident[:, :])
                    nc.tensor.transpose(bank[2][:, c], keysn[:, i, :], ident[:, :])
                    nc.tensor.transpose(bank[3][:, c], kinn[:, i, :], ident[:, :])
                    last = nc.tensor.transpose(bank[4][:, c], kinn[:, 4 + i, :], ident[:, :])
                last.then_inc(s_ps, 1)

            def fold_keys():
                pe.wait_ge(s_set, SET_KEYS)
                kv = keysT.rearrange("p (h k q) -> p q h k", h=PH, q=2)
                for q in range(2):
                    for h in range(PH):
                        c = q * PH + h
                        last = nc.tensor.matmul(bank[5][:, c * NK:(c + 1) * NK], wqn[:, c, :], kv[:, q, h, :],
                                                start=True, stop=True)
                last.then_inc(s_ps, 1)
                pe.wait_ge(s_set, SET_ALL)

            def prep(k):
                s, base = pr, k * NG
                if k:
                    pe.wait_ge(*last_x[k])
                if k == 0:
                    pe.wait_ge(s_id, 16)
                if k == 1:
                    turn_weights()
                with pe.Fori(0, NG // 2) as i:
                    for par in range(2):
                        n = 2 * i + par
                        pe.wait_ge(s["xn"], base + n + 1)
                        pe.wait_ge(s["ev"], base + n + 1)
                        for t in range(GT):
                            last = nc.tensor.transpose(bank[6 + par][:, t * P:(t + 1) * P], xn[:, par, t, :],
                                                       ident[:, :])
                        last.then_inc(s["tr"], 1)
                pe.wait_ge(s["ev"], 2 + (k + 1) * NG)

            def ffn(s, f):
                base = f * NG

                def project_in(n, par):
                    nc.tensor.matmul(bank[2 + par][:, :], win2[:, :, :].rearrange("p a b -> p (a b)"),
                                     xT[:, bass.ds(n * GW, GW)], start=True, stop=True).then_inc(s["s"], 1)

                def project_out(n, par):
                    pe.wait_ge(s["h"], NJ * (base + n + 1))
                    pe.wait_ge(s["hs"], (NJ - JPE) * (base + n + 1))
                    pe.wait_ge(s["x"], base + n + 1)
                    for t in range(GT):
                        c = slice(t * P, (t + 1) * P)
                        for j in range(JPE):
                            nc.tensor.matmul(bank[4 + par][:, c], h_ff[:, par, j, c], w2o[:, j, :],
                                             start=(j == 0), stop=False)
                        last = nc.tensor.matmul(bank[4 + par][:, c], hsum[:, par, c], wout2[:, :], start=False,
                                                stop=True)
                    last.then_inc(s["o"], 1)

                project_in(0, 0)
                project_in(1, 1)
                project_out(0, 0)
                with pe.Fori(1, NG // 2) as i:
                    project_in(2 * i, 0)
                    project_out(2 * i - 1, 1)
                    project_in(2 * i + 1, 1)
                    project_out(2 * i, 0)
                project_out(NG - 1, 1)

            def l0(s):
                def project(u, par):
                    pe.wait_ge(s["xs"], u + 1)
                    if not (isinstance(u, int) and u == 0):
                        pe.wait_ge(s["qT"], u)
                        pe.wait_ge(s["kT"], u)
                    for t in range(2):
                        last = nc.tensor.matmul(bank[4][:, t * 2 * D:(t + 1) * 2 * D], xs0[:, par, t * P:(t + 1) * P],
                                                wqkv[:, 0:2 * D], start=True, stop=True)
                    last.then_inc(s["qk"], 1)

                def values(u, par, left):
                    pe.wait_ge(s["cent"], left)
                    for w in range(4):
                        for r in range(2):
                            last = nc.tensor.matmul(bank[4][r * WIN:(r + 1) * WIN, w * D:(w + 1) * D],
                                                    xs0[:, par, w * WIN:(w + 1) * WIN], wqkv[:, 2 * D:3 * D],
                                                    start=True, stop=True)
                    last.then_inc(s["v"], 1)

                def turn_qk(u, valued):
                    pe.wait_ge(s["qn"], u + 1)
                    pe.wait_ge(s["vb"], valued)
                    for j in range(2):
                        for t in range(2):
                            last = nc.tensor.transpose(bank[4][:, (2 * j + t) * P:(2 * j + t + 1) * P],
                                                       qn0[:, 2 * t + j, :], ident[:, :])
                    last.then_inc(s["qt"], 1)

                def scores(u, par, t):
                    pe.wait_ge(s["kM"], u + 1)
                    pe.wait_ge(s["qT"], u + 1)
                    pe.wait_ge(s["sub"], 4 * u + 2 * t + 2)
                    km = kM0.rearrange("p (a h) q -> p a h q", a=2)
                    for hh in range(2):
                        for half in range(2):
                            keys = slice(t * P + half * WIN, t * P + (half + 1) * WIN)
                            last = nc.tensor.matmul(bank[2 * t + hh][half * WIN:(half + 1) * WIN, :],
                                                    qT0[:, par, keys], km[:, par, 8 * hh:8 * hh + 8, keys],
                                                    start=True, stop=True)
                        last.then_inc(s["st"], 1)

                def turn(u, t):
                    for hh in range(2):
                        pe.wait_ge(s["ex"], 4 * u + 2 * t + hh + 1)
                        pe.wait_ge(s["pe"], 4 * u + 2 * t + hh + 1)
                        if t == 1 and hh == 1 and not (isinstance(u, int) and u == 0):
                            pe.wait_ge(s["x"], u)
                        for j in range(4):
                            last = nc.tensor.transpose(bank[5 + hh][:, j * P:(j + 1) * P],
                                                       E0[:, t, hh, j * P:(j + 1) * P], ident[:, :])
                        last.then_inc(s["pt"], 1)

                def weigh(u, par, t):
                    pe.wait_ge(s["pe"], 4 * u + 2 * t + 4)
                    pe.wait_ge(s["vb"], u + 2)
                    pe.wait_ge(s["on"], u + 1)
                    vb = Vb0.rearrange("p a (w c) r e -> p a w c (r e)", w=4)
                    for c in range(8):
                        for half in range(2):
                            last = nc.tensor.matmul(bank[7][half * WIN:(half + 1) * WIN,
                                                            t * 144 + c * 18:t * 144 + (c + 1) * 18],
                                                    PT0[:, 8 * t + c, half * WIN:(half + 1) * WIN],
                                                    vb[:, par, 2 * t + half, c, :], start=True, stop=True)
                    last.then_inc(s["pv"], 1)

                def turn_outputs(u, last=False):
                    pe.wait_ge(s["on"], u + 2)
                    pe.wait_ge(s["pe"], 4 * u + 6 if last else 4 * u + 7)
                    for t in range(2):
                        last = nc.tensor.transpose(bank[5][:, t * P:(t + 1) * P], on0[:, t, :], ident[:, :])
                    last.then_inc(s["ot"], 1)

                def outputs(u, last=False):
                    pe.wait_ge(s["oe"], u + 1)
                    pe.wait_ge(s["cb"], NG)
                    pe.wait_ge(s["pe"], 4 * u + 6 if last else 4 * u + 8)
                    for t in range(2):
                        last = nc.tensor.matmul(bank[6][:, t * D:(t + 1) * D], oT0[:, t * P:(t + 1) * P],
                                                wproj[:, :], start=True, stop=True)
                    last.then_inc(s["y"], 1)

                def pair(u, par, back=True, one=True, two=True):
                    scores(u, par, 1)
                    if two:
                        project(u + 2, par)
                    turn(u, 0)
                    if back:
                        turn_outputs(u - 1)
                    if one:
                        values(u + 1, 1 - par, u + 3 if two else u + 2)
                    weigh(u, par, 0)
                    if back:
                        outputs(u - 1)
                    turn(u, 1)
                    if two:
                        turn_qk(u + 2, u + 3)
                    if one:
                        scores(u + 1, 1 - par, 0)
                    weigh(u, par, 1)

                project(0, 0)
                values(0, 0, 1)
                turn_qk(0, 2)
                pe.wait_ge(s["qT"], 1)
                pe.wait_ge(s["kT"], 1)
                project(1, 1)
                turn_qk(1, 2)
                scores(0, 0, 0)
                pe.wait_ge(s["qT"], 2)
                pe.wait_ge(s["kT"], 2)
                pair(0, 0, back=False)
                with pe.Fori(0, NP_ // 2 - 2) as i:
                    pair(2 * i + 1, 1)
                    pair(2 * i + 2, 0)
                pair(NP_ - 3, 1)
                pair(NP_ - 2, 0, two=False)
                pair(NP_ - 1, 1, one=False, two=False)
                turn_outputs(NP_ - 1, last=True)
                outputs(NP_ - 1, last=True)

            def l1(s):
                pe.wait_ge(s_set, SET_W1T)
                for half in range(2):
                    for b in range(8):
                        n = half * 8 + b
                        par = n % 2
                        if n >= 2:
                            pe.wait_ge(s["psq"], n - 1)
                        nc.tensor.matmul(bank[par][:, 0:SEQ], w1T[:, 0, :], xT[:, n * SEQ:(n + 1) * SEQ],
                                         start=True, stop=True).then_inc(s["pq"], 1)
                        if b >= 1:
                            pe.wait_ge(s["psq"], n)
                            nc.tensor.matmul(bank[2 + half][:, 0:SEQ], headsel[:, b - 1, :], sq1[:, 1 - par, :],
                                             start=(b == 1), stop=False).then_inc(s["sq_used"], 1)
                    pe.wait_ge(s["psq"], half * 8 + 8)
                    nc.tensor.matmul(bank[2 + half][:, 0:SEQ], headsel[:, 7, :], sq1[:, 1, :], start=False,
                                     stop=True).then_inc(s["sq_used"], 1)
                    pe.wait_ge(s["sq_used"], 2 + half * 8 + 8)
                    pe.sem_inc(s["pn"], 1)
                pe.wait_ge(s["selT"], 2)
                for c in range(2):
                    for half in range(2):
                        last = nc.tensor.transpose(bank[4][:, (2 * c + half) * P:(2 * c + half + 1) * P],
                                                   selT[:, half, c * P:(c + 1) * P], ident[:, :])
                last.then_inc(s["str"], 1)
                pe.wait_ge(s["sel"], 2)
                picked = sel.rearrange("p c a b -> p c (a b)")
                nc.tensor.matmul(bank[0][:, 0:BATCH * HEADS], upper[:, :], picked[:, 0, :], start=True, stop=True)
                nc.tensor.matmul(bank[1][:, 0:BATCH * HEADS], upper[:, :], picked[:, 1, :], start=True, stop=False)
                nc.tensor.matmul(bank[1][:, 0:BATCH * HEADS], ones, picked[:, 0, :], start=False,
                                 stop=True).then_inc(s["rm"], 1)

                def project(b):
                    pe.wait_ge(s["xs"], b + 1)
                    for c in range(2):
                        last = nc.tensor.matmul(bank[7][:, 2 * D * c:2 * D * (c + 1)], xs1[:, c * P:(c + 1) * P],
                                                w1T[:, 0:3:2, :], start=True, stop=True)
                    last.then_inc(s["qv"], 1)
                    if not (isinstance(b, int) and b < 2):
                        pe.wait_ge(s["oe"], b - 1)
                    nc.tensor.matmul(bank[6][:, SEQ:2 * SEQ], w1T[:, 1, :], xT[:, bass.ds(b * SEQ, SEQ)], start=True,
                                     stop=True).then_inc(s["k"], 1)

                def gather(b, par, first=False):
                    pe.wait_ge(s["Qn"], b + 1)
                    pe.wait_ge(s["S"], b + 1)
                    for i in range(2):
                        if not first:
                            pe.wait_ge(s["pe"], 4 * b - 1 + i)
                        for c in range(2):
                            last = nc.tensor.matmul(bank[4 + i][:, :], Qn[:, c, :],
                                                    S1[:, par, c, 512 * i:512 * (i + 1)], start=(c == 0),
                                                    stop=(c == 1))
                        last.then_inc(s["g"], 1)

                def scores(b):
                    pe.wait_ge(s["kT"], b + 1)
                    for i in range(4):
                        if i % 2 == 0:
                            pe.wait_ge(s["QM"], 2 * b + i // 2 + 1)
                        for g in range(2 * i, 2 * i + 2):
                            last = nc.tensor.matmul(bank[i][:, (g % 2) * SEQ:(g % 2 + 1) * SEQ],
                                                    QM1[:, g * P:(g + 1) * P], kT1, start=True, stop=True)
                        last.then_inc(s["sc"], 1)

                def turn_slots(b, par):
                    for i in range(4):
                        if i >= 2:
                            pe.wait_ge(s["sTe"], 4 * b + i - 1)
                        for j in range(4):
                            g, c = 2 * i + j // 2, j % 2
                            last = nc.tensor.transpose(bank[4 + i % 2][:, j * P:(j + 1) * P],
                                                       S1[:, par, c, g * P:(g + 1) * P], ident[:, :])
                        last.then_inc(s["sT"], 1)

                def turn(b):
                    for i in range(4):
                        pe.wait_ge(s["ex"], 4 * b + i + 1)
                        if i < 2:
                            pe.wait_ge(s["sTe"], 4 * b + i + 3)
                        else:
                            pe.wait_ge(s["pe"], 4 * b + i - 1)
                        for j in range(4):
                            g, c = 2 * i + j // 2, j % 2
                            last = nc.tensor.transpose(bank[4 + i % 2][:, j * P:(j + 1) * P],
                                                       E1[:, g, c * P:(c + 1) * P], ident[:, :])
                        last.then_inc(s["pt"], 1)

                def weigh(b, par, last=False):
                    pe.wait_ge(s["pe"], 4 * b + 4)
                    pe.wait_ge(s["vb"], b + 2)
                    if last:
                        pe.wait_ge(s["oe"], b)
                    else:
                        pe.wait_ge(s["kT"], b + 2)
                    for g in range(PAIRS):
                        for c in range(2):
                            mm = nc.tensor.matmul(bank[6][:, g * 18:(g + 1) * 18], PT1[:, g, c, :],
                                                  Vs1[:, 2 * par + c, 2 * g:2 * g + 2, :], start=(c == 0),
                                                  stop=(c == 1))
                    mm.then_inc(s["pv"], 1)

                def scatter(b):
                    pe.wait_ge(s["on"], b + 1)
                    pe.wait_ge(s["sTe"], 4 * b + 4)
                    pe.wait_ge(s["x"], b + 1)
                    for c in range(2):
                        for g in range(PAIRS):
                            last = nc.tensor.matmul(bank[7][:, c * P + 16 * g:c * P + 16 * (g + 1)],
                                                    ST1[:, g, c * P:(c + 1) * P],
                                                    O1[:, g, :, :].rearrange("p a b -> p (a b)"), start=True, stop=True)
                    last.then_inc(s["sca"], 1)

                def turn_outputs(b):
                    pe.wait_ge(s["oe1"], b + 1)
                    for t in range(2):
                        last = nc.tensor.transpose(bank[6][:, t * P:(t + 1) * P], on1[:, t, :], ident[:, :])
                    last.then_inc(s["ot"], 1)

                def outputs(b, valued):
                    pe.wait_ge(s["oe"], b + 1)
                    pe.wait_ge(s["cb"], NG)
                    pe.wait_ge(s["vb"], valued)
                    for t in range(2):
                        last = nc.tensor.matmul(bank[7][:, t * D:(t + 1) * D], oT1[:, t, :], w1T[:, 3, :],
                                                start=True, stop=True)
                    last.then_inc(s["y"], 1)

                def sequence(b, par, first=False, last=False):
                    scores(b)
                    if not first:
                        scatter(b - 1)
                    turn_slots(b, par)
                    if not first:
                        turn_outputs(b - 1)
                    if not last:
                        project(b + 1)
                    turn(b)
                    if not first:
                        outputs(b - 1, b + 2 if last else b + 3)
                    if not last:
                        gather(b + 1, 1 - par)
                    weigh(b, par, last)

                project(0)
                gather(0, 0, first=True)
                sequence(0, 0, first=True)
                with pe.Fori(0, NP_ // 2 - 1) as i:
                    sequence(2 * i + 1, 1)
                    sequence(2 * i + 2, 0)
                sequence(NP_ - 1, 1, last=True)
                scatter(NP_ - 1)
                turn_outputs(NP_ - 1)
                outputs(NP_ - 1, NP_ + 1)

            def product_keys(s, f):
                base = f * NT

                def similarities(m, par):
                    pe.wait_ge(s["zt"], base + m + 1)
                    pe.wait_ge(s["sub"], 2 * (base + m))
                    nc.tensor.matmul(bank[0][:, :], zT[:, par, :], weff[:, :, :, :].rearrange("p a b c -> p (a b c)"),
                                     start=True, stop=True).then_inc(s["sim"], 1)

                def experts(m, half):
                    if not (f == 0 and isinstance(m, int) and m == 0):
                        pe.wait_ge(s["g"], 2 * (base + m) + half)
                    for j in range(4):
                        c = half * 512 + j * P
                        last = nc.tensor.matmul(bank[6 if half else 1][:, j * P:(j + 1) * P], kinT[:, c:c + P],
                                                xT[:, bass.ds(m * P, P)], start=True, stop=True)
                    last.then_inc(s["o"], 1)

                def add_unit(n, par, at):
                    h = UNITS[at]
                    if h in MERGED:
                        pe.wait_ge(s["ys"], len(MERGED) * (base + n + 1) + MERGED.index(h) + 1)
                    else:
                        pe.wait_ge(s["M"], 8 * (base + n) + h + 9)
                    for c in range(NCH):
                        last = nc.tensor.matmul(bank[2 + 2 * par + c // 4][:, (c % 4) * P:(c % 4 + 1) * P],
                                                Mm[:, h % NMS, c * P:(c + 1) * P], ident[:, :],
                                                start=(at == 0 and c % 4 == 0), stop=(at == NU - 1 and c % 4 == 3))
                    last.then_inc(s["acc"], 1)

                def outputs(m):
                    pe.wait_ge(s["x"], base + m + 1)
                    for c in range(NCH):
                        if c % 4 == 0:
                            pe.wait_ge(s["cg"], 2 * (base + m) + c // 4 + 3)
                        last = nc.tensor.matmul(bank[7][:, 0:D], cg[:, c * P:(c + 1) * P], kout[:, c, :],
                                                start=(c == 0), stop=(c == NCH - 1))
                    last.then_inc(s["y"], 1)

                def tile(n, par, finish=True, ahead=True):
                    for at in range(NU):
                        add_unit(n, par, at)
                        if at == 0 and ahead:
                            similarities(n + 2, par)
                        if at == OUT_AT and finish:
                            outputs(n - 1)
                        if at == OUT_AT:
                            experts(n, 0)
                            experts(n, 1)

                similarities(0, 0)
                similarities(1, 1)
                tile(0, 0, finish=False)
                with pe.Fori(0, NT // 2 - 2) as i:
                    tile(2 * i + 1, 1)
                    tile(2 * i + 2, 0)
                tile(NT - 3, 1)
                tile(NT - 2, 0, ahead=False)
                tile(NT - 1, 1, ahead=False)
                outputs(NT - 1)

            pe.sem_inc(pr["tr"], 2)
            pe.sem_inc(ff["o"], 2)
            pe.sem_inc(L1["sq_used"], 2)
            pe.sem_inc(L0["pv"], 2)
            pe.sem_inc(pk["sim"], 2)
            pe.sem_inc(pk["acc"], NU)
            for k in range(STAGES):
                prep(k)
                if k == 0:
                    setup_ffn()
                if k in (0, 2):
                    ffn(ff, k // 2)
                if k == 1:
                    fold_keys()
                    l0(L0)
                if k == 4:
                    l1(L1)
                if k in (3, 5):
                    product_keys(pk, (k - 3) // 2)


_INS = ['L0_attn_x', 'L0_attn_W_qkv', 'L0_attn_ln_gamma', 'L0_attn_ln_beta', 'L0_attn_W_proj', 'L0_attn_b_proj',
        'L0_ffn_Win', 'L0_ffn_bin_', 'L0_ffn_W1', 'L0_ffn_b1', 'L0_ffn_W2', 'L0_ffn_b2', 'L0_ffn_Wout', 'L0_ffn_bout',
        'L1_attn_Wq', 'L1_attn_bq', 'L1_attn_Wk', 'L1_attn_bk', 'L1_attn_Wv', 'L1_attn_bv', 'L1_attn_Wo',
        'L1_attn_bo', 'L1_ffn_gamma', 'L1_ffn_beta', 'L1_ffn_w_q', 'L1_ffn_keys', 'L1_ffn_key_in', 'L1_ffn_key_out']


def constants():
    p = np.arange(P)
    head = p // HD
    c = {"c_ident": np.eye(P, dtype=np.float32)}
    c["c_hmask"] = (head[:, None] == np.arange(HEADS)[None]).astype(np.float32)
    c["c_vmask"] = (p[:, None] // WIN == np.arange(2)[None]).astype(np.float32)
    c["c_upper"] = (p[:, None] <= p[None]).astype(np.float32)
    rank = np.arange(SLOTS)
    c["c_slots"] = np.where(rank < TOP_U, rank, -7).astype(np.float32)
    c["c_headsel"] = (16 * np.arange(8)[None, :, None] + head[:, None, None] == p[None, None, :]).astype(np.float32)
    return c


def kernel(**inputs):
    import concourse.bacc as _bacc
    from concourse import mybir as _mybir
    from concourse.bass_utils import run_bass_kernel_spmd as _run

    nc = _bacc.Bacc("TRN2", target_bir_lowering=False, num_devices=1)
    arrays, args = {}, {}
    named = {name: np.ascontiguousarray(inputs[name]) for name in _INS}
    named.update(constants())
    for name, a in named.items():
        arrays[f"in_{name}_dram"] = a
        args[name] = nc.dram_tensor(f"in_{name}_dram", a.shape, _mybir.dt.from_np(a.dtype), kind="ExternalInput").ap()
    out = nc.dram_tensor("out_0_dram", (BATCH, SEQ, D), _mybir.dt.float32, kind="ExternalOutput").ap()
    build(nc, args, out)
    r = _run(nc, [arrays], core_ids=[0])
    return r.results[0]["out_0_dram"]
```
